# Optimizing a Trainium2 kernel written in Bass

```python
import numpy as np
import jax
import jax.numpy as jnp

def _softmax(x, axis=-1):
    return jax.nn.softmax(x, axis=axis)

def _gelu(x):
    return jax.nn.gelu(x, approximate=True)

def _silu(x):
    return jax.nn.silu(x)

def _sigmoid(x):
    return jax.nn.sigmoid(x)

def _layernorm(x, axis=-1, eps=1e-05):
    m = jnp.mean(x, axis=axis, keepdims=True)
    v = jnp.var(x, axis=axis, keepdims=True)
    return (x - m) / jnp.sqrt(v + eps)

def _scatter_add(tgt, idx, src, axis=0):
    return tgt.at[idx].add(src)

def _segment_sum(src, seg, n):
    return jax.ops.segment_sum(src, seg, n)
kernel_name = 'mk_sandwich_d1_jaxref_r4_19b08c'

def setup_inputs(seed: int=0):
    np.random.seed(seed)
    _w = jnp.asarray

    def _L0_attn_setup():
        import jax, jax.numpy as jnp
        import numpy as np
        EPS = 1e-06
        CHUNK = 16

        def _ln(x, g, b):
            mu = jnp.mean(x, -1, keepdims=True)
            var = jnp.var(x, -1, keepdims=True)
            xhat = (x - mu) * jax.lax.rsqrt(var + EPS)
            return g * xhat + b

        def chunk_ttt_linear(q, k, v, w, b, eta, scale=1.0):
            B, T, H, D = q.shape
            NC = T // CHUNK
            q = q * scale
            qc = q.reshape(B, NC, CHUNK, H, D).swapaxes(0, 1)
            kc = k.reshape(B, NC, CHUNK, H, D).swapaxes(0, 1)
            vc = v.reshape(B, NC, CHUNK, H, D).swapaxes(0, 1)
            ec = eta.reshape(B, NC, CHUNK, H).swapaxes(0, 1)
            tri = jnp.tril(jnp.ones((CHUNK, CHUNK), bool))
            S0 = jnp.zeros((B, H, D, D), q.dtype)

            def step(S, inp):
                qi, ki, vi, ei = inp
                kh = jnp.einsum('bchd,bhde->bche', ki, S)
                target = vi - ki
                mu = jnp.mean(kh, -1, keepdims=True)
                rstd = jax.lax.rsqrt(jnp.var(kh, -1, keepdims=True) + EPS)
                kh_hat = (kh - mu) * rstd
                g = w * kh_hat + b - target
                gw = g * w
                v_new = (gw - jnp.mean(gw, -1, keepdims=True) - kh_hat * jnp.mean(gw * kh_hat, -1, keepdims=True)) * rstd
                A = jnp.einsum('bchd,bshd->bhcs', qi, ki)
                A = jnp.where(tri, A, 0.0) * jnp.transpose(ei, (0, 2, 1))[:, :, None, :]
                qh = jnp.einsum('bchd,bhde->bche', qi, S) - jnp.einsum('bhcs,bshe->bche', A, v_new)
                o = qi + _ln(qh, w, b)
                S = S - jnp.einsum('bchd,bche->bhde', ki * ei[..., None], v_new)
                return (S, o)
            S_fin, o = jax.lax.scan(step, S0, (qc, kc, vc, ec))
            o = o.swapaxes(0, 1).reshape(B, T, H, D)
            return (o, S_fin)
        key = jax.random.key(seed)
        ks = jax.random.split(key, 11)
        B, T, D, H = (2, 1024, 512, 16)
        Dh = D // H
        std = 0.02
        x = jax.random.normal(ks[0], (B, T, D), jnp.float32)
        Wq = jax.random.normal(ks[1], (D, D), jnp.float32) * std
        Wk = jax.random.normal(ks[2], (D, D), jnp.float32) * std
        Wv = jax.random.normal(ks[3], (D, D), jnp.float32) * std
        Wo = jax.random.normal(ks[4], (D, D), jnp.float32) * std
        Wbeta = jax.random.normal(ks[5], (D, H), jnp.float32) * std
        ln_w = 1.0 + jax.random.normal(ks[6], (H, Dh), jnp.float32) * std
        ln_b = jax.random.normal(ks[7], (H, Dh), jnp.float32) * std
        Wg1 = jax.random.normal(ks[8], (D, Dh), jnp.float32) * std
        Wg2 = jax.random.normal(ks[9], (Dh, D), jnp.float32) * std
        norm_w = 1.0 + jax.random.normal(ks[10], (D,), jnp.float32) * std
        return dict(x=x, Wq=Wq, Wk=Wk, Wv=Wv, Wo=Wo, Wbeta=Wbeta, ln_w=ln_w, ln_b=ln_b, Wg1=Wg1, Wg2=Wg2, norm_w=norm_w)
    _L0_attn_in = _L0_attn_setup()

    def _L0_ffn_setup():
        import jax, jax.numpy as jnp
        import numpy as np
        B, S, H, I = (1, 64, 512, 1536)

        def _quantized_matmul(x, w, scale):
            wq = w.astype(jnp.float8_e4m3fn).astype(x.dtype)
            y = jnp.einsum('bsi,io->bso', x, wq)
            return y * scale
        key = jax.random.key(seed)
        ks = jax.random.split(key, 7)
        return {'x': jax.random.normal(ks[0], (B, S, H), dtype=jnp.float32), 'gate_w': jax.random.normal(ks[1], (H, I), dtype=jnp.float32) * 0.02, 'up_w': jax.random.normal(ks[2], (H, I), dtype=jnp.float32) * 0.02, 'down_w': jax.random.normal(ks[3], (I, H), dtype=jnp.float32) * 0.02, 'gate_scale': jax.random.uniform(ks[4], (I,), dtype=jnp.float32, minval=0.5, maxval=1.5), 'up_scale': jax.random.uniform(ks[5], (I,), dtype=jnp.float32, minval=0.5, maxval=1.5), 'down_scale': jax.random.uniform(ks[6], (H,), dtype=jnp.float32, minval=0.5, maxval=1.5)}
    _L0_ffn_in = _L0_ffn_setup()
    _d = {'L0_attn_x': _L0_attn_in['x'], 'L0_attn_Wq': _L0_attn_in['Wq'], 'L0_attn_Wk': _L0_attn_in['Wk'], 'L0_attn_Wv': _L0_attn_in['Wv'], 'L0_attn_Wo': _L0_attn_in['Wo'], 'L0_attn_Wbeta': _L0_attn_in['Wbeta'], 'L0_attn_ln_w': _L0_attn_in['ln_w'], 'L0_attn_ln_b': _L0_attn_in['ln_b'], 'L0_attn_Wg1': _L0_attn_in['Wg1'], 'L0_attn_Wg2': _L0_attn_in['Wg2'], 'L0_attn_norm_w': _L0_attn_in['norm_w'], 'L0_ffn_gate_w': _L0_ffn_in['gate_w'], 'L0_ffn_up_w': _L0_ffn_in['up_w'], 'L0_ffn_down_w': _L0_ffn_in['down_w'], 'L0_ffn_gate_scale': _L0_ffn_in['gate_scale'], 'L0_ffn_up_scale': _L0_ffn_in['up_scale'], 'L0_ffn_down_scale': _L0_ffn_in['down_scale']}
    _x0 = _d['L0_attn_x']
    _d['L0_attn_x'] = jax.random.normal(jax.random.fold_in(jax.random.key(seed), 1), (1, 2048, 512), dtype=_x0.dtype)
    del _x0
    return _d

def reference(L0_attn_x, L0_attn_Wq, L0_attn_Wk, L0_attn_Wv, L0_attn_Wo, L0_attn_Wbeta, L0_attn_ln_w, L0_attn_ln_b, L0_attn_Wg1, L0_attn_Wg2, L0_attn_norm_w, L0_ffn_gate_w, L0_ffn_up_w, L0_ffn_down_w, L0_ffn_gate_scale, L0_ffn_up_scale, L0_ffn_down_scale):

    def _L0_attn_ref(x, Wq, Wk, Wv, Wo, Wbeta, ln_w, ln_b, Wg1, Wg2, norm_w):
        import jax, jax.numpy as jnp
        import numpy as np
        EPS = 1e-06
        CHUNK = 16

        def _ln(x, g, b):
            mu = jnp.mean(x, -1, keepdims=True)
            var = jnp.var(x, -1, keepdims=True)
            xhat = (x - mu) * jax.lax.rsqrt(var + EPS)
            return g * xhat + b

        def chunk_ttt_linear(q, k, v, w, b, eta, scale=1.0):
            B, T, H, D = q.shape
            NC = T // CHUNK
            q = q * scale
            qc = q.reshape(B, NC, CHUNK, H, D).swapaxes(0, 1)
            kc = k.reshape(B, NC, CHUNK, H, D).swapaxes(0, 1)
            vc = v.reshape(B, NC, CHUNK, H, D).swapaxes(0, 1)
            ec = eta.reshape(B, NC, CHUNK, H).swapaxes(0, 1)
            tri = jnp.tril(jnp.ones((CHUNK, CHUNK), bool))
            S0 = jnp.zeros((B, H, D, D), q.dtype)

            def step(S, inp):
                qi, ki, vi, ei = inp
                kh = jnp.einsum('bchd,bhde->bche', ki, S)
                target = vi - ki
                mu = jnp.mean(kh, -1, keepdims=True)
                rstd = jax.lax.rsqrt(jnp.var(kh, -1, keepdims=True) + EPS)
                kh_hat = (kh - mu) * rstd
                g = w * kh_hat + b - target
                gw = g * w
                v_new = (gw - jnp.mean(gw, -1, keepdims=True) - kh_hat * jnp.mean(gw * kh_hat, -1, keepdims=True)) * rstd
                A = jnp.einsum('bchd,bshd->bhcs', qi, ki)
                A = jnp.where(tri, A, 0.0) * jnp.transpose(ei, (0, 2, 1))[:, :, None, :]
                qh = jnp.einsum('bchd,bhde->bche', qi, S) - jnp.einsum('bhcs,bshe->bche', A, v_new)
                o = qi + _ln(qh, w, b)
                S = S - jnp.einsum('bchd,bche->bhde', ki * ei[..., None], v_new)
                return (S, o)
            S_fin, o = jax.lax.scan(step, S0, (qc, kc, vc, ec))
            o = o.swapaxes(0, 1).reshape(B, T, H, D)
            return (o, S_fin)
        B, T, D = x.shape
        H, Dh = ln_w.shape
        q = jax.nn.silu(x @ Wq).reshape(B, T, H, Dh)
        k = (x @ Wk).reshape(B, T, H, Dh)
        k = k * jax.lax.rsqrt(jnp.sum(k * k, -1, keepdims=True) + EPS)
        v = (x @ Wv).reshape(B, T, H, Dh)
        beta = jax.nn.sigmoid(x @ Wbeta) * 2.0
        o, _ = chunk_ttt_linear(q, k, v, ln_w, ln_b, beta, 1.0)
        gate = x @ Wg1 @ Wg2
        og = o * jax.nn.sigmoid(gate.reshape(B, T, H, Dh))
        og = og * jax.lax.rsqrt(jnp.mean(og * og, -1, keepdims=True) + EPS)
        o = og.reshape(B, T, D) * norm_w
        return o @ Wo

    def _L0_ffn_ref(x, gate_w, up_w, down_w, gate_scale, up_scale, down_scale):
        import jax, jax.numpy as jnp
        import numpy as np
        B, S, H, I = (1, 64, 512, 1536)

        def _quantized_matmul(x, w, scale):
            wq = w.astype(jnp.float8_e4m3fn).astype(x.dtype)
            y = jnp.einsum('bsi,io->bso', x, wq)
            return y * scale
        gate = jax.nn.silu(_quantized_matmul(x, gate_w, gate_scale))
        up = _quantized_matmul(x, up_w, up_scale)
        fuse = gate * up
        return _quantized_matmul(fuse, down_w, down_scale)
    x = L0_attn_x
    x = x + _layernorm(_L0_attn_ref(_layernorm(x, axis=-1), L0_attn_Wq, L0_attn_Wk, L0_attn_Wv, L0_attn_Wo, L0_attn_Wbeta, L0_attn_ln_w, L0_attn_ln_b, L0_attn_Wg1, L0_attn_Wg2, L0_attn_norm_w), axis=-1)
    x = x + _layernorm(_L0_ffn_ref(_layernorm(x, axis=-1), L0_ffn_gate_w, L0_ffn_up_w, L0_ffn_down_w, L0_ffn_gate_scale, L0_ffn_up_scale, L0_ffn_down_scale), axis=-1)
    return x

_drawn_inputs = setup_inputs


def setup_inputs(seed=0):
    import zlib

    import numpy as np

    out = dict(_drawn_inputs(seed))
    spreads = {}
    factors = {'L0_attn_Wg1': 2.835, 'L0_attn_Wg2': 2.83, 'L0_attn_norm_w': 3.288}
    for name, (base, spread) in spreads.items():
        noise = np.random.default_rng([zlib.crc32(name.encode()), seed]).standard_normal(out[name].shape)
        drawn = base * np.exp(spread * noise) if base else spread * noise
        out[name] = jnp.asarray(drawn.astype(out[name].dtype))
    for name, factor in factors.items():
        out[name] = (out[name] * factor).astype(out[name].dtype)
    return out
```

```python
from contextlib import ExitStack

import numpy as np

import concourse.bass as bass
from concourse import mybir

F32 = mybir.dt.float32
F32R = mybir.dt.float32r
I32 = mybir.dt.int32
ALU = mybir.AluOpType
ACT = mybir.ActivationFunctionType
AX_X = mybir.AxisListType.X

P = 128
T, D = 2048, 512
H, DH = 16, 32
CH = 16
DG = 32
I = 1536
NT = T // P
NC = P // CH
KD = D // P
MI = I // P
RM = 4
NR = MI // RM
KAPPA = float(DH) ** 0.5
EPS_LN = 1e-5
EPS = 1e-6

C_ID = 0
C_REP = C_ID + P
C_TRI = C_REP + P
C_CHM = C_TRI + P
C_ROW = C_CHM + 64
C_GPM = C_ROW + 8
C_HM = C_GPM + 2
C_NH = C_HM + 4
C_ONE = C_NH + 16
NCONST = C_ONE + 16


class Steps:

    def __init__(self, sem, names):
        self.sem, self.names, self.next = sem, names.split(), 0

    def one(self, name):
        assert self.names[self.next] == name, (name, self.names[self.next])
        self.next = (self.next + 1) % len(self.names)
        return self.sem, 1

    def wait(self, eng, name, n):
        if isinstance(n, int) and n < 0:
            return
        eng.wait_ge(self.sem, len(self.names) * n + self.names.index(name) + 1)


def build(nc, x, wq, wk, wv, wo, wbeta, wg1, wg2, norm_w, ln_w, ln_b, gate_w, up_w, down_w,
          gate_s, up_s, down_s, consts, out):
    ctx = ExitStack()
    with ctx:
        def sb(name, cols, dt=F32, rows=P):
            return ctx.enter_context(nc.sbuf_tensor(name, [rows, cols], dt))

        def sem(name):
            return ctx.enter_context(nc.semaphore(name))

        Wq, Wk, Wv, Wo = (sb(n, KD * D) for n in ("Wq", "Wk", "Wv", "Wo"))
        Wg1, Wb = sb("Wg1", KD * DG), sb("Wb", KD * H)
        Wg2 = sb("Wg2", D, rows=DG)
        GW, UW, DW = (sb(n, KD * I, F32R) for n in ("GW", "UW", "DW"))
        nw, gs, us = sb("nw", KD), sb("gs", MI), sb("us", MI)
        ds = sb("ds", D)
        wR, bR = sb("wR", 64), sb("bR", 64)
        wK, w2K = sb("wK", 64), sb("w2K", 64)
        cst = sb("cst", NCONST)
        ident = cst[:, C_ID:C_ID + P]
        xt, xnT = sb("xt", D), sb("xnT", D)
        xn = dv = sb("xn_dv", D)
        kn = thT = sb("kn_th", D)
        kT = sb("kT", D)
        g1T = sb("g1T", P, rows=DG)
        bt, bx = sb("bt", H), sb("bx", P)
        em, etaR, etaM = sb("em", P), sb("etaR", 2 * 16), sb("etaM", 2 * 32)
        qT, qR, rR, kR, thR = ([sb(f"{n}{s}", D) for s in range(2)] for n in ("qT", "qR", "rR", "kR", "thR"))
        BDk, BDq = sb("BDk", 2 * 2 * 4 * 2 * P), sb("BDq", 2 * 2 * 4 * 2 * P)
        BDkR, ATB = sb("BDkR", 2 * 2 * P), sb("ATB", 2 * 2 * P)
        S = sb("S", P)
        y, ysq = sb("y", 64), sb("ysq", 2 * 33)
        PR, sums, u = sb("PR", 3 * 64), sb("sums", 8), sb("u", 64)
        ss, rho, re, rec, h2 = sb("ss", 2), sb("rho", 2), sb("re", 4), sb("rec", 2), sb("h2", 2)
        x2, U, tv, VX, VE = sb("x2", 64), sb("U", 64), sb("tv", 64), sb("VX", P), sb("VE", 64)
        qhR = [sb(f"qhR{s}", D) for s in range(2)]
        x1, o1, o2 = sb("x1", D), sb("o1", D), sb("o2", D)
        ogT = o1
        xh, xl, f = sb("xh", D, F32R), sb("xl", D, F32R), sb("f", D)
        fh, fl = sb("fh", D, F32R), sb("fl", D, F32R)
        xn2 = yb = f
        st = {n: sb(f"st_{n}", 6) for n in "paf"}
        st["y"] = sb("st_y", 6)
        mv = {n: sb(f"mv_{n}", 2) for n in "pafy"}
        ve = {n: sb(f"ve_{n}", 1) for n in "pafy"}
        rs = {n: sb(f"rs_{n}", 1) for n in "pafy"}
        nb = {"a": sb("nb_a", 1)}
        kss, kse, rk = sb("kss", H), sb("kse", H), sb("rk", H)
        qss, qse, rq = sb("qss", H), sb("qse", H), sb("rq", H)
        oss, ose, ro = sb("oss", H), sb("ose", H), sb("ro", H)
        rm = sb("rm", H)
        pause = sb("pause", 1)
        wst = [x1, o1, o2]
        wmg = [f, qhR[0], qhR[1]]

        bank = [ctx.enter_context(nc.psum_tensor(f"bank{n}", [P, 512], F32)) for n in range(8)]
        KH, dS = bank[0][:, 0:64], bank[0][:, 128:256]
        QH, AT = bank[1], bank[2]
        PA, PC = bank[3:5], bank[5:8]

        s_const, s_small = sem("s_const"), sem("s_small")
        s_wk, s_wv, s_wq, s_wo = sem("s_wk"), sem("s_wv"), sem("s_wq"), sem("s_wo")
        s_stage = [sem(f"s_stage{n}") for n in range(3)]
        s_magic, s_shift, s_quant = sem("s_magic"), sem("s_shift"), sem("s_quant")
        s_mask = sem("s_mask")
        s_zero = sem("s_zero")
        s_setup = sem("s_setup")
        s_x, s_xr, s_out = sem("s_x"), sem("s_xr"), sem("s_out")

        prep_v = Steps(sem("prep_v"), "stats mv veps xn kss kse kn d kR dR rb rw rm r qR thR bx em er eM")
        prep_a = Steps(sem("prep_a"), "xnT ksq kT q g1 beta th")
        prep_t = Steps(sem("prep_t"), "xnT k v kT dT q beta g1 gate brow")
        prep_g = Steps(sem("prep_g"), "rs rk b1 qb")
        diag_a = Steps(sem("diag_a"), "k0 q0 k1 q1")
        chunk_v = Steps(sem("chunk_v"), "at")
        chunk_t = Steps(sem("chunk_t"), "at")
        chunk_g = Steps(sem("chunk_g"), "kR")
        scan_t = Steps(sem("scan_t"), "kh qs upd qa")
        scan_v = Steps(sem("scan_v"), "y ysq p ss ry py sums u h x2 U t vx ve S")
        scan_g = Steps(sem("scan_g"), "rho re rec")
        scan_a = Steps(sem("scan_a"), "qh")
        post_v = Steps(sem("post_v"), "qss qse n og oss ose on ogT")
        tail_v = Steps(sem("tail_v"), "as aa ave nb x1 fs fa fve xf xl")
        post_a = Steps(sem("post_a"), "qsq osq")
        tail_a = Steps(sem("tail_a"), "xc xh")
        tail_t = Steps(sem("tail_t"), "wo xT")
        post_g = Steps(sem("post_g"), "rq nw o ro")
        tail_g = Steps(sem("tail_g"), "ra rf")
        ffn_t = Steps(sem("ffn_t"), "g u")
        down_t = Steps(sem("down_t"), "dn")
        ffn_a = Steps(sem("ffn_a"), "silu fh")
        ffn_v = Steps(sem("ffn_v"), "f fl")
        fin_v = Steps(sem("fin_v"), "y ys ya yve yn out")
        fin_g = Steps(sem("fin_g"), "ry")

        x_t = x.rearrange("(t p) d -> t p d", p=P)
        out_t = out.rearrange("(t p) d -> t p d", p=P)

        def rows(t):
            return t[:, :].rearrange("p (m e) -> p m e", e=DH)

        def heads(t):
            return t[:, :].rearrange("p (h e) -> p h e", e=DH)

        def wide(t, n=DH):
            return t.unsqueeze(2).broadcast_to([t.shape[0], t.shape[1], n])

        def feat(t):
            return t[:, :].rearrange("p (gp m c) -> p m gp c", gp=2, c=CH)

        def bd(t):
            return t[:, :].rearrange("p (f gh j gp r) -> p f gh j gp r", f=2, gh=2, j=4, gp=2)

        kTc = [t[:, :].rearrange("p (g j c) -> p g j c", g=4, c=CH) for t in (kT, qT[0], qT[1])]

        def chunk_cols(t, j):
            return t[:, :].rearrange("p (gh j e) -> p gh j e", gh=2, e=DH)[:, :, j, :]

        def pp(t, j):
            return t[:, (j % 2) * 256:(j % 2) * 256 + 256].rearrange("p (gh r) -> p gh r", gh=2)

        def timeline(scan_body, prologue, eng):
            prologue()
            for t in range(4):
                scan_body(t, t % 2)
            with eng.Fori(0, (NT - 6) // 2) as i:
                for s in range(2):
                    scan_body(2 * i + (4 + s), s)
            for t in (NT - 2, NT - 1, NT, NT + 1):
                scan_body(t, t % 2)

        def live(t):
            if not isinstance(t, int):
                return True, True, True, True, True
            return t + 2 < NT, t + 1 < NT, t < NT, 0 <= t - 1 < NT, 0 <= t - 2 < NT

        block = ctx.enter_context(nc.Block())

        @block.sync
        def _(sp):
            sp.dma_start(cst[:, :], consts).then_inc(s_const, 16)
            sp.dma_start(xt[:, :], x_t[0]).then_inc(s_x, 16)
            for dst, src, s in ((Wk, wk, s_wk), (Wv, wv, s_wv), (Wq, wq, s_wq)):
                sp.dma_start(dst[:, :].rearrange("p (k n) -> p k n", k=KD),
                             src.rearrange("(k p) n -> p k n", p=P)).then_inc(s, 16)
            for dst, src in ((Wg1, wg1), (Wb, wbeta)):
                sp.dma_start(dst[:, :].rearrange("p (k n) -> p k n", k=KD),
                             src.rearrange("(k p) n -> p k n", p=P)).then_inc(s_small, 16)
            for dst, src in ((Wg2, wg2), (nw, norm_w), (gs, gate_s), (us, up_s), (wR, ln_w), (bR, ln_b)):
                sp.dma_start(dst[:, :], src).then_inc(s_small, 16)
            prep_v.wait(sp, "xn", 0)
            sp.dma_start(xt[:, :], x_t[1]).then_inc(s_x, 16)
            sp.dma_start(ds[:, :], down_s.partition_broadcast(P)).then_inc(s_small, 16)
            sp.dma_start(Wo[:, :].rearrange("p (k n) -> p k n", k=KD),
                         wo.rearrange("(k p) n -> p k n", p=P)).then_inc(s_wo, 16)
            for n, src in enumerate((gate_w, up_w, down_w)):
                sp.dma_start(wst[n][:, :], src[:, 0:D]).then_inc(s_stage[n], 16)
            with sp.Fori(1, MI) as i:
                for n, src in enumerate((gate_w, up_w, down_w)):
                    sp.wait_ge(s_quant, 3 * i + (n - 2))
                    sp.dma_start(wst[n][:, :], src[:, bass.ds(i * D, D)]).then_inc(s_stage[n], 16)
            sp.wait_ge(s_quant, 3 * MI)

            def body(t, s):
                norm, prep, scan, post, tail = live(t)
                if norm:
                    prep_v.wait(sp, "xn", t + 1)
                    sp.dma_start(xt[:, :], x_t[t + 2]).then_inc(s_x, 16)
                if tail:
                    fin_v.wait(sp, "out", t - 3)
                    sp.dma_start(x1[:, :], x_t[t - 2]).then_inc(s_xr, 16)
                    fin_v.wait(sp, "out", t - 2)
                    sp.dma_start(out_t[t - 2], yb[:, :]).then_inc(s_out, 16)

            timeline(body, lambda: None, sp)
            sp.wait_ge(s_out, 16 * NT)

        @block.tensor
        def _(pe):
            mm = nc.tensor.matmul

            def proj(dst, W, n, one, first=True):
                for k in range(KD):
                    ins = mm(dst, xnT[:, k * P:(k + 1) * P], W[:, k * n:(k + 1) * n], start=(k == 0), stop=(k == KD - 1))
                ins.then_inc(*one)

            def turn(dst, src, one):
                for g in range(4):
                    ins = nc.tensor.transpose(dst[:, g * P:(g + 1) * P], src[:, g * P:(g + 1) * P], ident)
                ins.then_inc(*one)

            def prep_xnT(t):
                prep_v.wait(pe, "xn", t)
                prep_v.wait(pe, "em", t - 1)
                turn(PA[0], xn, prep_t.one("xnT"))

            def prep_k(t):
                prep_a.wait(pe, "xnT", t)
                prep_a.wait(pe, "th", t - 1)
                proj(PA[1][:, :], Wk, D, prep_t.one("k"))

            def prep_vv(t):
                proj(PA[0][:, :], Wv, D, prep_t.one("v"))

            def prep_kT(t):
                prep_v.wait(pe, "kn", t)
                turn(PA[1], kn, prep_t.one("kT"))

            def prep_dT(t):
                prep_v.wait(pe, "d", t)
                turn(PA[0], dv, prep_t.one("dT"))

            def prep_q(t):
                prep_a.wait(pe, "kT", t)
                for g in range(4):
                    for k in range(KD):
                        ins = mm(PA[1][:, g * P:(g + 1) * P], Wq[:, k * D + g * P:k * D + (g + 1) * P],
                                 xnT[:, k * P:(k + 1) * P], start=(k == 0), stop=(k == KD - 1))
                ins.then_inc(*prep_t.one("q"))

            def prep_beta(t):
                prep_v.wait(pe, "dR", t)
                proj(PA[0][:, P:P + H], Wb, H, prep_t.one("beta"))
                for k in range(KD):
                    ins = mm(PA[0][0:DG, 0:P], Wg1[:, k * DG:(k + 1) * DG], xnT[:, k * P:(k + 1) * P],
                             start=(k == 0), stop=(k == KD - 1))
                ins.then_inc(*prep_t.one("g1"))

            def prep_gate(t):
                prep_a.wait(pe, "g1", t)
                prep_a.wait(pe, "q", t)
                for g in range(4):
                    ins = mm(PA[1][:, g * P:(g + 1) * P], Wg2[:, g * P:(g + 1) * P], g1T[:, :], start=True, stop=True)
                ins.then_inc(*prep_t.one("gate"))

            def prep_brow(t):
                prep_v.wait(pe, "bx", t)
                prep_a.wait(pe, "beta", t)
                mm(PA[0][:, 2 * P:3 * P], cst[:, C_REP:C_REP + P], bx[:, :], start=True, stop=True).then_inc(*prep_t.one("brow"))

            def at(n, j, s):
                if j % 4 == 0:
                    diag_a.wait(pe, f"k{j // 4}", n)
                prep_a.wait(pe, "q", n)
                chunk_v.wait(pe, "at", NC * n + (j - 1))
                for gh in range(2):
                    for gp in range(2):
                        g = 2 * gp + gh
                        ins = mm(AT[:, gh * CH:(gh + 1) * CH], bd(BDk)[:, j // 4, gh, j % 4, gp, :],
                                 qT[s][:, g * P + j * CH:g * P + (j + 1) * CH],
                                 start=(gh == 0 and gp == 0), stop=(gp == 1), skip_group_check=True)
                ins.then_inc(*chunk_t.one("at"))

            def read_state(n, j):
                c = NC * n + j
                if j % 4 == 0:
                    diag_a.wait(pe, f"k{j // 4}", n)
                scan_v.wait(pe, "S", c - 1)
                for gh in range(2):
                    for gp in range(2):
                        ins = mm(KH[:, gh * DH:(gh + 1) * DH], bd(BDk)[:, j // 4, gh, j % 4, gp, :],
                                 S[:, (2 * gh + gp) * DH:(2 * gh + gp + 1) * DH],
                                 start=(gh == 0 and gp == 0), stop=(gp == 1), skip_group_check=True)
                ins.then_inc(*scan_t.one("kh"))
                if j % 4 == 0:
                    diag_a.wait(pe, f"q{j // 4}", n)
                scan_a.wait(pe, "qh", c - 1)
                for gh in range(2):
                    for gp in range(2):
                        ins = mm(QH[:, gh * DH:(gh + 1) * DH], bd(BDq)[:, j // 4, gh, j % 4, gp, :],
                                 S[:, (2 * gh + gp) * DH:(2 * gh + gp + 1) * DH],
                                 start=(gh == 0 and gp == 0), stop=False, skip_group_check=True)
                ins.then_inc(*scan_t.one("qs"))

            def write_state(n, j):
                c = NC * n + j
                chunk_g.wait(pe, "kR", c)
                scan_v.wait(pe, "vx", c)
                for gh in range(2):
                    ins = mm(dS[:, gh * 64:(gh + 1) * 64], pp(BDkR, j)[:, gh, :], VX[:, gh * 64:(gh + 1) * 64],
                             start=True, stop=True)
                ins.then_inc(*scan_t.one("upd"))
                chunk_v.wait(pe, "at", c)
                scan_v.wait(pe, "ve", c)
                for gh in range(2):
                    ins = mm(QH[:, gh * DH:(gh + 1) * DH], pp(ATB, j)[:, gh, :], VE[:, gh * DH:(gh + 1) * DH],
                             start=False, stop=True, skip_group_check=True)
                ins.then_inc(*scan_t.one("qa"))

            def post_wo(n):
                post_v.wait(pe, "ogT", n)
                fin_v.wait(pe, "y", n - 1)
                for g in range(4):
                    ins = mm(PC[2][:, :], ogT[:, g * P:(g + 1) * P], Wo[:, g * D:(g + 1) * D], start=(g == 0), stop=(g == 3))
                ins.then_inc(*tail_t.one("wo"))

            def post_xT(n):
                tail_v.wait(pe, "xf", n)
                turn(PC[2], xn2, tail_t.one("xT"))

            def ffn_gu(n, r):
                if r == 0:
                    tail_v.wait(pe, "xl", n)
                c = NR * n + r
                for W, b, name in ((GW, PC[0], "g"), (UW, PC[1], "u")):
                    if name == "g":
                        ffn_a.wait(pe, "silu", c - 1)
                    else:
                        ffn_v.wait(pe, "f", c - 1)
                    for q in range(RM):
                        m = RM * r + q
                        for part in (xh, xl):
                            for k in range(KD):
                                ins = mm(b[:, q * P:(q + 1) * P], W[:, k * I + m * P:k * I + (m + 1) * P],
                                         part[:, k * P:(k + 1) * P], start=(part is xh and k == 0),
                                         stop=(part is xl and k == KD - 1))
                    ins.then_inc(*ffn_t.one(name))

            def ffn_down(n, r):
                c = NR * n + r
                ffn_v.wait(pe, "fl", c)
                for q in range(RM):
                    m = RM * r + q
                    for part in (fh, fl):
                        ins = mm(PC[2][:, :], part[:, q * P:(q + 1) * P], DW[:, m * D:(m + 1) * D],
                                 start=(m == 0 and part is fh), stop=(m == MI - 1 and part is fl))
                ins.then_inc(*down_t.one("dn"))

            def body(t, s):
                norm, prep, scan, post, tail = live(t)
                o = 1 - s
                for j in range(NC):
                    if scan:
                        read_state(t, j)
                    if j == 0:
                        if prep:
                            prep_xnT(t + 1)
                        if tail:
                            post_wo(t - 2)
                    if j == 1 and prep:
                        prep_k(t + 1)
                    if j == 2:
                        if tail:
                            post_xT(t - 2)
                        if prep:
                            prep_vv(t + 1)
                    if j == 3 and tail:
                        ffn_gu(t - 2, 0)
                    if j == 4:
                        if prep:
                            prep_kT(t + 1)
                            prep_dT(t + 1)
                        if tail:
                            ffn_gu(t - 2, 1)
                            ffn_down(t - 2, 0)
                    if j == 5:
                        if prep:
                            prep_q(t + 1)
                            prep_beta(t + 1)
                    if j == 6:
                        if tail:
                            ffn_down(t - 2, 1)
                        if prep:
                            prep_gate(t + 1)
                        if tail:
                            ffn_gu(t - 2, 2)
                    if j == 7:
                        if prep:
                            prep_brow(t + 1)
                        if tail:
                            ffn_down(t - 2, 2)
                    if scan and j + 1 < NC:
                        at(t, j + 1, s)
                    if prep and j + 1 == NC:
                        at(t + 1, 0, o)
                    if scan:
                        write_state(t, j)

            def prologue():
                pe.wait_ge(s_const, 16)
                prep_xnT(0)
                pe.wait_ge(s_wk, 16)
                prep_k(0)
                pe.wait_ge(s_wv, 16)
                prep_vv(0)
                prep_kT(0)
                pe.wait_ge(s_wq, 16)
                prep_dT(0)
                prep_q(0)
                pe.wait_ge(s_small, 16 * 9)
                prep_beta(0)
                prep_gate(0)
                prep_brow(0)
                pe.wait_ge(s_zero, 4)
                at(0, 0, 0)
                pe.wait_ge(s_setup, 3)
                pe.wait_ge(s_quant, 3 * MI)

            timeline(body, prologue, pe)

        @block.scalar
        def _(act):
            fn = nc.scalar.activation

            def copy(dst, src, one):
                fn(dst, src, ACT.Copy).then_inc(*one)

            def prep_xnT(t):
                prep_t.wait(act, "xnT", t)
                prep_t.wait(act, "gate", t - 1)
                copy(xnT[:, :], PA[0][:, :], prep_a.one("xnT"))

            def prep_ksq(t):
                prep_t.wait(act, "k", t)
                fn(dv[:, :], PA[1][:, :], ACT.Square).then_inc(*prep_a.one("ksq"))

            def prep_kT(t):
                prep_t.wait(act, "kT", t)
                prep_v.wait(act, "kR", t - 1)
                diag_a.wait(act, "k1", t - 1)
                copy(kT[:, :], PA[1][:, :], prep_a.one("kT"))

            def prep_q(t, s):
                prep_t.wait(act, "q", t)
                prep_v.wait(act, "qR", t - 2)
                chunk_t.wait(act, "at", NC * (t - 1) - 1)
                diag_a.wait(act, "q1", t - 2)
                fn(qT[s][:, :], PA[1][:, :], ACT.Silu).then_inc(*prep_a.one("q"))

            def prep_g1(t):
                prep_t.wait(act, "g1", t)
                prep_t.wait(act, "gate", t - 1)
                copy(g1T[:, :], PA[0][0:DG, 0:P], prep_a.one("g1"))
                prep_g.wait(act, "b1", t - 1)
                fn(bt[:, :], PA[0][:, P:P + H], ACT.Tanh, scale=0.5).then_inc(*prep_a.one("beta"))

            def prep_th(t):
                prep_t.wait(act, "gate", t)
                fn(thT[:, :], PA[1][:, :], ACT.Tanh, scale=0.5).then_inc(*prep_a.one("th"))

            def diag(n, which, half, s):
                src = kTc[0] if which == "k" else kTc[1 + s]
                dst = bd(BDk if which == "k" else BDq)
                prep_a.wait(act, {"k": "kT", "q": "q"}[which], n)
                if which == "k":
                    scan_t.wait(act, "kh", NC * (n - 1) + 4 * half + 3)
                    chunk_t.wait(act, "at", NC * (n - 1) + 4 * half + 3)
                else:
                    scan_t.wait(act, "qs", NC * (n - 1) + 4 * half + 3)
                for h in range(4):
                    for gh in range(2):
                        q = slice(32 * h, 32 * h + 32)
                        d = dst[q, half, gh, :, :, :]
                        for gp in range(2):
                            ins = fn(d[:, :, gp, 32 * h + CH * gp:32 * h + CH * (gp + 1)],
                                     src[q, 2 * gp + gh, 4 * half:4 * half + 4, :], ACT.Copy)
                ins.then_inc(*diag_a.one(f"{which}{half}"))

            def take_qh(n, j, s):
                scan_t.wait(act, "qa", NC * n + j)
                if j == 0:
                    post_a.wait(act, "qsq", n - 2)
                    post_v.wait(act, "n", n - 2)
                fn(chunk_cols(qhR[s], j), QH[:, 0:64].rearrange("p (gh e) -> p gh e", gh=2), ACT.Copy)\
                    .then_inc(*scan_a.one("qh"))

            def post_qsq(n, s):
                scan_a.wait(act, "qh", NC * n + NC - 1)
                tail_t.wait(act, "wo", n - 1)
                fn(o1[:, :], qhR[s][:, :], ACT.Square).then_inc(*post_a.one("qsq"))

            def post_osq(n):
                post_v.wait(act, "og", n)
                post_v.wait(act, "qss", n)
                fn(o1[:, :], o2[:, :], ACT.Square).then_inc(*post_a.one("osq"))

            def post_xc(n):
                act.wait_ge(s_xr, 16 * n + 16)
                tail_v.wait(act, "nb", n)
                fn(x1[:, :], x1[:, :], ACT.Identity, bias=nb["a"][:, 0:1]).then_inc(*tail_a.one("xc"))

            def post_xh(n):
                tail_t.wait(act, "xT", n)
                ffn_t.wait(act, "u", NR * (n - 1) + NR - 1)
                copy(xh[:, :], PC[2][:, :], tail_a.one("xh"))

            def ffn_silu(n, r):
                c = NR * n + r
                ffn_t.wait(act, "g", c)
                ffn_v.wait(act, "fl", c - 1)
                if r == 0:
                    tail_t.wait(act, "xT", n)
                for q in range(RM):
                    ins = fn(f[:, q * P:(q + 1) * P], PC[0][:, q * P:(q + 1) * P], ACT.Silu,
                             scale=gs[:, RM * r + q:RM * r + q + 1])
                ins.then_inc(*ffn_a.one("silu"))

            def ffn_fh(n, r):
                c = NR * n + r
                ffn_v.wait(act, "f", c)
                down_t.wait(act, "dn", c - 1)
                copy(fh[:, :], f[:, :], ffn_a.one("fh"))

            def body(t, s):
                norm, prep, scan, post, tail = live(t)
                o = 1 - s
                for j in range(NC):
                    if j == 0:
                        if prep:
                            prep_xnT(t + 1)
                        if scan:
                            diag(t, "k", 1, s)
                        if post:
                            post_qsq(t - 1, o)
                    if j == 1:
                        if prep:
                            prep_ksq(t + 1)
                        if scan:
                            diag(t, "q", 1, s)
                    if j == 2 and tail:
                        post_xh(t - 2)
                    if j == 3 and tail:
                        ffn_silu(t - 2, 0)
                    if j == 4:
                        if prep:
                            prep_kT(t + 1)
                        if tail:
                            ffn_silu(t - 2, 1)
                    if j == 5:
                        if prep:
                            prep_q(t + 1, o)
                            prep_g1(t + 1)
                        if post:
                            post_osq(t - 1)
                        if prep:
                            diag(t + 1, "k", 0, o)
                    if j == 6:
                        if prep:
                            prep_th(t + 1)
                        if tail:
                            ffn_silu(t - 2, 2)
                        if prep:
                            diag(t + 1, "q", 0, o)
                    if scan:
                        take_qh(t, j, s)
                    if tail:
                        if j == 1:
                            post_xc(t - 2)
                        if j == 3:
                            ffn_fh(t - 2, 0)
                        if j == 4:
                            ffn_fh(t - 2, 1)
                        if j == 6:
                            ffn_fh(t - 2, 2)

            def prologue():
                prep_xnT(0)
                prep_ksq(0)
                prep_kT(0)
                prep_q(0, 0)
                prep_g1(0)
                act.wait_ge(s_zero, 4)
                diag(0, "k", 0, 0)
                diag(0, "q", 0, 0)
                prep_th(0)

            timeline(body, prologue, act)

        @block.gpsimd
        def _(pool):
            tt = nc.gpsimd.tensor_tensor

            def power(dst, src, n, one):
                tt(dst, src, cst[:, C_NH:C_NH + n], ALU.pow).then_inc(*one)

            def prep_rs(t):
                prep_v.wait(pool, "veps", t)
                power(rs["p"][:, :], ve["p"][:, :], 1, prep_g.one("rs"))

            def prep_rk(t):
                prep_v.wait(pool, "kse", t)
                power(rk[:, :], kse[:, :], H, prep_g.one("rk"))

            def prep_qb(t, s):
                prep_v.wait(pool, "qR", t)
                for gh in range(2):
                    m = rows(qR[s])[:, gh * NC:(gh + 1) * NC, :]
                    ins = tt(m, m, bR[:, gh * DH:(gh + 1) * DH].unsqueeze(1).broadcast_to([P, NC, DH]), ALU.add)
                ins.then_inc(*prep_g.one("qb"))

            def prep_b1(t):
                prep_a.wait(pool, "beta", t)
                prep_t.wait(pool, "brow", t - 1)
                prep_v.wait(pool, "bx", t - 1)
                tt(bt[:, :], bt[:, :], cst[:, C_ONE:C_ONE + H], ALU.add).then_inc(*prep_g.one("b1"))

            def chunk_kR(n, j, s):
                c = NC * n + j
                if j == 0:
                    prep_v.wait(pool, "kR", n)
                scan_t.wait(pool, "upd", c - 2)
                for gh in range(2):
                    k = rows(kR[s])[:, gh * NC + j, :]
                    ins = tt(pp(BDkR, j)[:, gh, :].rearrange("p (h d) -> p h d", h=4),
                             k.unsqueeze(1).broadcast_to([P, 4, DH]),
                             wide(cst[:, C_HM:C_HM + 4]), ALU.mult)
                ins.then_inc(*chunk_g.one("kR"))

            def scan_rho(n, j, s):
                c = NC * n + j
                scan_v.wait(pool, "ss", c)
                scan_v.wait(pool, "U", c - 1)
                power(rho[:, :], ss[:, :], 2, scan_g.one("rho"))
                scan_g.wait(pool, "rho", c)
                scan_v.wait(pool, "ve", c - 1)
                m = etaM[:, s * 32:s * 32 + 32].rearrange("p (gh j gp) -> p gh j gp", gh=2, gp=2)[:, :, j, :]
                tt(re[:, :].rearrange("p (gh gp) -> p gh gp", gh=2), wide(rho[:, :], 2), m, ALU.mult).then_inc(*scan_g.one("re"))
                m = etaR[:, s * 16:s * 16 + 16].rearrange("p (gh j) -> p gh j", gh=2)[:, :, j]
                tt(rec[:, :], rho[:, :], m, ALU.mult).then_inc(*scan_g.one("rec"))

            def post_rq(n):
                post_v.wait(pool, "qse", n)
                power(rq[:, :], qse[:, :], H, post_g.one("rq"))

            def post_o(n, s):
                post_v.wait(pool, "n", n)
                for gh in range(2):
                    m = rows(o2)[:, gh * NC:(gh + 1) * NC, :]
                    ins = tt(m, m, wK[:, gh * DH:(gh + 1) * DH].unsqueeze(1).broadcast_to([P, NC, DH]), ALU.mult)
                ins.then_inc(*post_g.one("nw"))
                post_g.wait(pool, "nw", n)
                tt(o2[:, :], o2[:, :], qR[s][:, :], ALU.add).then_inc(*post_g.one("o"))

            def post_ro(n):
                post_v.wait(pool, "ose", n)
                power(ro[:, :], ose[:, :], H, post_g.one("ro"))

            def tail_pow(n, k, before, name):
                tail_v.wait(pool, before, n)
                power(rs[k][:, :], ve[k][:, :], 1, tail_g.one(name))

            def fin_ry(n):
                fin_v.wait(pool, "yve", n)
                power(rs["y"][:, :], ve["y"][:, :], 1, fin_g.one("ry"))

            def body(t, s):
                norm, prep, scan, post, tail = live(t)
                o = 1 - s
                for j in range(NC):
                    if scan:
                        scan_rho(t, j, s)
                        if j + 1 < NC:
                            chunk_kR(t, j + 1, s)
                    if j == 0 and post:
                        post_rq(t - 1)
                    if j == 1 and tail:
                        tail_pow(t - 2, "a", "ave", "ra")
                        tail_pow(t - 2, "f", "fve", "rf")
                    if j == 2 and prep:
                        prep_rk(t + 1)
                    if j == 3 and post:
                        post_o(t - 1, o)
                    if j == 6:
                        if prep:
                            prep_b1(t + 1)
                        if post:
                            post_ro(t - 1)
                        if prep:
                            prep_qb(t + 1, o)
                    if j == 7:
                        if prep:
                            chunk_kR(t + 1, 0, o)
                        if norm:
                            prep_rs(t + 2)
                        if tail:
                            fin_ry(t - 2)

            def prologue():
                for b in (BDk, BDq):
                    for q in range(2):
                        nc.gpsimd.memset(b[:, q * 2048:(q + 1) * 2048], 0.0).then_inc(s_zero, 1)
                pool.wait_ge(s_const, 16)
                prep_rs(0)
                prep_rk(0)
                pool.wait_ge(s_small, 16 * 9)
                prep_b1(0)
                prep_qb(0, 0)
                prep_rs(1)
                chunk_kR(0, 0, 0)
                with pool.Fori(0, MI) as i:
                    for n in range(3):
                        pool.wait_ge(s_magic, 3 * i + (n + 1))
                        tt(wst[n][:, :], wst[n][:, :], wmg[n][:, :], ALU.add).then_inc(s_shift, 1)

            timeline(body, prologue, pool)

        @block.vector
        def _(dve):
            tt, ts, stt = nc.vector.tensor_tensor, nc.vector.tensor_scalar, nc.vector.scalar_tensor_tensor
            red = nc.vector.tensor_reduce

            def add_eps(dst, src, eps, one):
                ts(dst, src, eps, None, ALU.add).then_inc(*one)

            def prep_stats(t):
                dve.wait_ge(s_x, 16 * t + 16)
                nc.vector.bn_stats(st["p"][:, :], xt[:, :]).then_inc(*prep_v.one("stats"))
                prep_v.wait(dve, "stats", t)
                nc.vector.memset(pause[:, :], 0.0)
                nc.vector.bn_aggr(mv["p"][:, :], st["p"][:, :]).then_inc(*prep_v.one("mv"))
                prep_v.wait(dve, "mv", t)
                add_eps(ve["p"][:, :], mv["p"][:, 1:2], EPS_LN, prep_v.one("veps"))

            def prep_xn(t):
                prep_g.wait(dve, "rs", t)
                prep_t.wait(dve, "dT", t - 1)
                ts(xn[:, :], xt[:, :], mv["p"][:, 0:1], rs["p"][:, 0:1], ALU.subtract, ALU.mult)\
                    .then_inc(*prep_v.one("xn"))

            def prep_kss(t):
                prep_a.wait(dve, "ksq", t)
                red(kss[:, :], heads(dv), AX_X, ALU.add).then_inc(*prep_v.one("kss"))
                prep_v.wait(dve, "kss", t)
                add_eps(kse[:, :], kss[:, :], EPS, prep_v.one("kse"))

            def prep_kn(t):
                prep_g.wait(dve, "rk", t)
                tt(heads(kn), heads(PA[1]), wide(rk[:, :]), ALU.mult).then_inc(*prep_v.one("kn"))

            def prep_d(t):
                prep_v.wait(dve, "kn", t)
                prep_t.wait(dve, "v", t)
                tt(dv[:, :], kn[:, :], PA[0][:, :], ALU.subtract).then_inc(*prep_v.one("d"))

            def turn(dst, src, one):
                nc.vector.transpose(rows(dst), feat(src)).then_inc(*one)

            def prep_kR(t, s):
                prep_a.wait(dve, "kT", t)
                chunk_g.wait(dve, "kR", NC * (t - 1) - 1)
                turn(kR[s], kT, prep_v.one("kR"))
                prep_t.wait(dve, "dT", t)
                scan_v.wait(dve, "U", NC * (t - 1) - 1)
                turn(rR[s], PA[0], prep_v.one("dR"))

            def prep_r(t, s):
                for name, b, op, before in (("rb", bR, ALU.add, "dR"), ("rw", wR, ALU.mult, "rb")):
                    prep_v.wait(dve, before, t)
                    for gh in range(2):
                        m = rows(rR[s])[:, gh * NC:(gh + 1) * NC, :]
                        ins = tt(m, m, b[:, gh * DH:(gh + 1) * DH].unsqueeze(1).broadcast_to([P, NC, DH]), op)
                    ins.then_inc(*prep_v.one(name))
                prep_v.wait(dve, "rw", t)
                red(rm[:, :], rows(rR[s]), AX_X, ALU.add).then_inc(*prep_v.one("rm"))
                prep_v.wait(dve, "rm", t)
                stt(out=rows(rR[s]), in0=wide(rm[:, :]), scalar=-1.0 / DH, in1=rows(rR[s]),
                    op0=ALU.mult, op1=ALU.add).then_inc(*prep_v.one("r"))

            def prep_qR(t, s):
                prep_a.wait(dve, "q", t)
                post_g.wait(dve, "o", t - 2)
                turn(qR[s], qT[s], prep_v.one("qR"))

            def prep_thR(t, s):
                prep_a.wait(dve, "th", t)
                post_v.wait(dve, "og", t - 2)
                turn(thR[s], thT, prep_v.one("thR"))

            def prep_bx(t):
                prep_g.wait(dve, "b1", t)
                prep_t.wait(dve, "brow", t - 1)
                for gh in range(2):
                    e = bt[:, :].rearrange("p (gp gh h) -> p gh gp h", gp=2, gh=2)[:, gh]
                    ins = tt(bx[:, gh * 64:(gh + 1) * 64].rearrange("p (j gp h) -> p j gp h", j=NC, gp=2),
                             e.unsqueeze(1).broadcast_to([P, NC, 2, 4]),
                             cst[:, C_CHM:C_CHM + 64].rearrange("p (j gp h) -> p j gp h", j=NC, gp=2), ALU.mult)
                ins.then_inc(*prep_v.one("bx"))

            def prep_eta(t, s):
                prep_t.wait(dve, "brow", t)
                tt(em[:, :].rearrange("p (m h) -> p m h", h=8), PA[0][:, 2 * P:3 * P].rearrange("p (m h) -> p m h", h=8),
                   cst[:, C_ROW:C_ROW + 8].unsqueeze(1).broadcast_to([P, 16, 8]), ALU.mult).then_inc(*prep_v.one("em"))
                prep_v.wait(dve, "em", t)
                scan_g.wait(dve, "rec", NC * (t - 1) - 1)
                red(etaR[:, s * 16:(s + 1) * 16], em[:, :].rearrange("p (m h) -> p m h", h=8), AX_X, ALU.add)\
                    .then_inc(*prep_v.one("er"))
                prep_v.wait(dve, "er", t)
                tt(etaM[:, s * 32:(s + 1) * 32].rearrange("p (m gp) -> p m gp", gp=2),
                   wide(etaR[:, s * 16:(s + 1) * 16], 2),
                   cst[:, C_GPM:C_GPM + 2].unsqueeze(1).broadcast_to([P, 16, 2]), ALU.mult).then_inc(*prep_v.one("eM"))

            def chunk_at(n, j):
                c = NC * n + j
                chunk_t.wait(dve, "at", c)
                scan_t.wait(dve, "qa", c - 2)
                for gh in range(2):
                    ins = tt(pp(ATB, j)[:, gh, :].rearrange("p (h c) -> p h c", c=CH),
                             AT[:, gh * CH:(gh + 1) * CH].unsqueeze(1).broadcast_to([P, 8, CH]),
                             cst[:, C_TRI:C_TRI + P].rearrange("p (h c) -> p h c", c=CH), ALU.mult)
                ins.then_inc(*chunk_v.one("at"))

            def g2(t, w=DH):
                return t.rearrange("p (gh e) -> p gh e", e=w)

            def scan_front(n, j, s):
                c = NC * n + j
                scan_t.wait(dve, "kh", c)
                nc.vector.tensor_copy(y[:, :], KH).then_inc(*scan_v.one("y"))
                scan_v.wait(dve, "y", c)
                tt(g2(ysq[:, :], 33)[:, :, 0:DH], g2(y[:, :]), g2(y[:, :]), ALU.mult).then_inc(*scan_v.one("ysq"))
                tt(PR[:, 0:64], w2K[:, :], y[:, :], ALU.mult).then_inc(*scan_v.one("p"))
                scan_v.wait(dve, "ysq", c)
                red(ss[:, :], g2(ysq[:, :], 33), AX_X, ALU.add).then_inc(*scan_v.one("ss"))
                if j == 0:
                    prep_v.wait(dve, "r", n)
                tt(g2(PR[:, 128:192]), chunk_cols(rR[s], j), g2(y[:, :]), ALU.mult).then_inc(*scan_v.one("ry"))
                scan_v.wait(dve, "p", c)
                tt(PR[:, 64:128], PR[:, 0:64], y[:, :], ALU.mult).then_inc(*scan_v.one("py"))
                scan_v.wait(dve, "py", c)
                red(sums[:, 0:6], PR[:, :].rearrange("p (g e) -> p g e", e=DH), AX_X, ALU.add)\
                    .then_inc(*scan_v.one("sums"))
                scan_v.wait(dve, "sums", c)
                stt(out=g2(u[:, :]), in0=wide(sums[:, 0:2]), scalar=1.0 / DH, in1=g2(PR[:, 0:64]),
                    op0=ALU.mult, op1=ALU.subtract).then_inc(*scan_v.one("u"))

            def scan_back(n, j, s):
                c = NC * n + j
                scan_g.wait(dve, "rho", c)
                for gh in range(2):
                    ins = stt(out=h2[:, gh:gh + 1], in0=sums[:, 2 + gh:3 + gh], scalar=rho[:, gh:gh + 1],
                              in1=sums[:, 4 + gh:5 + gh], op0=ALU.mult, op1=ALU.add)
                ins.then_inc(*scan_v.one("h"))
                for gh in range(2):
                    e = slice(gh * DH, (gh + 1) * DH)
                    ins = ts(x2[:, e], y[:, e], rho[:, gh:gh + 1], rho[:, gh:gh + 1], ALU.mult, ALU.mult)
                ins.then_inc(*scan_v.one("x2"))
                scan_v.wait(dve, "u", c)
                for gh in range(2):
                    e = slice(gh * DH, (gh + 1) * DH)
                    ins = stt(out=U[:, e], in0=u[:, e], scalar=rho[:, gh:gh + 1], in1=chunk_cols(rR[s], j)[:, gh, :],
                              op0=ALU.mult, op1=ALU.subtract)
                ins.then_inc(*scan_v.one("U"))
                scan_v.wait(dve, "U", c)
                for gh in range(2):
                    e = slice(gh * DH, (gh + 1) * DH)
                    ins = stt(out=tv[:, e], in0=x2[:, e], scalar=h2[:, gh:gh + 1], in1=U[:, e],
                              op0=ALU.mult, op1=ALU.add)
                ins.then_inc(*scan_v.one("t"))
                scan_v.wait(dve, "t", c)
                scan_g.wait(dve, "rec", c)
                tt(VX[:, :].rearrange("p (gh gp e) -> p gh gp e", gh=2, gp=2),
                   g2(tv[:, :]).unsqueeze(2).broadcast_to([P, 2, 2, DH]),
                   g2(re[:, :], 2).unsqueeze(3).broadcast_to([P, 2, 2, DH]), ALU.mult).then_inc(*scan_v.one("vx"))
                scan_t.wait(dve, "qa", c - 1)
                tt(g2(VE[:, :]), g2(tv[:, :]), wide(rec[:, :]), ALU.mult).then_inc(*scan_v.one("ve"))

            def scan_state(n, j):
                c = NC * n + j
                scan_t.wait(dve, "upd", c)
                tt(S[:, :], S[:, :], dS, ALU.add).then_inc(*scan_v.one("S"))

            def post_qss(n):
                post_a.wait(dve, "qsq", n)
                red(qss[:, :], rows(o1), AX_X, ALU.add).then_inc(*post_v.one("qss"))
                post_v.wait(dve, "qss", n)
                add_eps(qse[:, :], qss[:, :], DH * EPS, post_v.one("qse"))

            def post_n(n, s):
                post_g.wait(dve, "rq", n)
                tt(rows(o2), rows(qhR[s]), wide(rq[:, :]), ALU.mult).then_inc(*post_v.one("n"))

            def post_og(n, s):
                post_g.wait(dve, "o", n)
                stt(out=o2[:, :], in0=thR[s][:, :], scalar=1.0, in1=o2[:, :], op0=ALU.add, op1=ALU.mult)\
                    .then_inc(*post_v.one("og"))

            def post_oss(n):
                post_a.wait(dve, "osq", n)
                red(oss[:, :], rows(o1), AX_X, ALU.add).then_inc(*post_v.one("oss"))
                post_v.wait(dve, "oss", n)
                add_eps(ose[:, :], oss[:, :], 4 * DH * EPS, post_v.one("ose"))

            def post_ogT(n):
                post_g.wait(dve, "ro", n)
                tt(rows(o2), rows(o2), wide(ro[:, :]), ALU.mult).then_inc(*post_v.one("on"))
                post_v.wait(dve, "on", n)
                nc.vector.transpose(feat(ogT), rows(o2)).then_inc(*post_v.one("ogT"))

            def norm_stats(src, k, steps, names, n):
                a, b, c = names
                nc.vector.bn_stats(st[k][:, :], src).then_inc(*steps.one(a))
                steps.wait(dve, a, n)
                nc.vector.memset(pause[:, :], 0.0)
                nc.vector.bn_aggr(mv[k][:, :], st[k][:, :]).then_inc(*steps.one(b))
                steps.wait(dve, b, n)
                add_eps(ve[k][:, :], mv[k][:, 1:2], EPS_LN, steps.one(c))

            def tail_stats(n):
                tail_t.wait(dve, "wo", n)
                norm_stats(PC[2][:, :], "a", tail_v, ("as", "aa", "ave"), n)

            def tail_x1(n):
                tail_g.wait(dve, "ra", n)
                stt(out=nb["a"][:, :], in0=mv["a"][:, 0:1], scalar=-1.0, in1=rs["a"][:, :], op0=ALU.mult, op1=ALU.mult)\
                    .then_inc(*tail_v.one("nb"))
                tail_a.wait(dve, "xc", n)
                stt(out=x1[:, :], in0=PC[2][:, :], scalar=rs["a"][:, 0:1], in1=x1[:, :], op0=ALU.mult, op1=ALU.add)\
                    .then_inc(*tail_v.one("x1"))
                tail_v.wait(dve, "x1", n)
                norm_stats(x1[:, :], "f", tail_v, ("fs", "fa", "fve"), n)
                tail_g.wait(dve, "rf", n)
                dve.wait_ge(s_out, 16 * n)
                ts(xn2[:, :], x1[:, :], mv["f"][:, 0:1], rs["f"][:, 0:1], ALU.subtract, ALU.mult)\
                    .then_inc(*tail_v.one("xf"))

            def post_xl(n):
                tail_a.wait(dve, "xh", n)
                tt(xl[:, :], PC[2][:, :], xh[:, :].bitcast(F32), ALU.subtract).then_inc(*tail_v.one("xl"))

            def ffn_f(n, r):
                c = NR * n + r
                ffn_a.wait(dve, "silu", c)
                ffn_t.wait(dve, "u", c)
                for q in range(RM):
                    e = slice(q * P, (q + 1) * P)
                    ins = stt(out=f[:, e], in0=PC[1][:, e], scalar=us[:, RM * r + q:RM * r + q + 1], in1=f[:, e],
                              op0=ALU.mult, op1=ALU.mult)
                ins.then_inc(*ffn_v.one("f"))
                ffn_a.wait(dve, "fh", c)
                tt(fl[:, :], f[:, :], fh[:, :].bitcast(F32), ALU.subtract).then_inc(*ffn_v.one("fl"))

            def fin_y(n):
                down_t.wait(dve, "dn", NR * n + NR - 1)
                tt(yb[:, :], PC[2][:, :], ds[:, :], ALU.mult).then_inc(*fin_v.one("y"))
                fin_v.wait(dve, "y", n)
                norm_stats(yb[:, :], "y", fin_v, ("ys", "ya", "yve"), n)
                fin_g.wait(dve, "ry", n)
                ts(yb[:, :], yb[:, :], mv["y"][:, 0:1], rs["y"][:, 0:1], ALU.subtract, ALU.mult)\
                    .then_inc(*fin_v.one("yn"))
                fin_v.wait(dve, "yn", n)
                tt(yb[:, :], yb[:, :], x1[:, :], ALU.add).then_inc(*fin_v.one("out"))

            def body(t, s):
                norm, prep, scan, post, tail = live(t)
                o = 1 - s
                for j in range(NC):
                    if scan:
                        scan_front(t, j, s)
                        scan_back(t, j, s)
                        scan_state(t, j)
                        if j + 1 < NC:
                            chunk_at(t, j + 1)
                    if j == 0:
                        if post:
                            post_qss(t - 1)
                        if tail:
                            tail_stats(t - 2)
                    if j == 1:
                        if prep:
                            prep_kss(t + 1)
                        if post:
                            post_n(t - 1, o)
                        if tail:
                            tail_x1(t - 2)
                    if j == 2 and tail:
                        post_xl(t - 2)
                    if j == 3:
                        if prep:
                            prep_kn(t + 1)
                            prep_d(t + 1)
                        if tail:
                            ffn_f(t - 2, 0)
                    if j == 4:
                        if prep:
                            prep_kR(t + 1, o)
                            prep_r(t + 1, o)
                        if post:
                            post_og(t - 1, o)
                        if tail:
                            ffn_f(t - 2, 1)
                    if j == 5:
                        if post:
                            post_oss(t - 1)
                        if prep:
                            prep_qR(t + 1, o)
                    if j == 6:
                        if prep:
                            prep_thR(t + 1, o)
                            prep_bx(t + 1)
                        if tail:
                            ffn_f(t - 2, 2)
                    if j == 7:
                        if prep:
                            prep_eta(t + 1, o)
                            chunk_at(t + 1, 0)
                        if norm:
                            prep_stats(t + 2)
                        if post:
                            post_ogT(t - 1)
                        if norm:
                            prep_xn(t + 2)
                        if tail:
                            fin_y(t - 2)

            def prologue():
                nc.vector.memset(S[:, :], 0.0).then_inc(s_mask, 1)
                nc.vector.memset(g2(ysq[:, :], 33)[:, :, DH:DH + 1], DH * EPS).then_inc(s_mask, 1)
                prep_stats(0)
                prep_xn(0)
                prep_kss(0)
                prep_kn(0)
                prep_d(0)
                prep_kR(0, 0)
                dve.wait_ge(s_small, 16 * 9)
                prep_r(0, 0)
                prep_qR(0, 0)
                prep_thR(0, 0)
                dve.wait_ge(s_const, 16)
                prep_bx(0)
                prep_eta(0, 0)
                prep_stats(1)
                prep_xn(1)
                chunk_at(0, 0)
                ts(wK[:, :], wR[:, :], KAPPA, None, ALU.mult).then_inc(s_setup, 1)
                stt(out=w2K[:, :], in0=wR[:, :], scalar=KAPPA, in1=wR[:, :], op0=ALU.mult, op1=ALU.mult)\
                    .then_inc(s_setup, 1)
                dve.wait_ge(s_wo, 16)
                for g in range(KD):
                    e = slice(g * D, (g + 1) * D)
                    ins = ts(Wo[:, e], Wo[:, e], nw[:, g:g + 1], KAPPA, ALU.mult, ALU.mult)
                ins.then_inc(s_setup, 1)
                dve.wait_ge(s_setup, 3)
                dve.wait_ge(s_mask, 2)

                with dve.Fori(0, MI) as i:
                    for n in range(3):
                        dve.wait_ge(s_stage[n], 16 * i + 16)
                        ts(wmg[n][:, :].bitcast(I32), wst[n][:, :].bitcast(I32), 0x7F800000, 0x00400000,
                           ALU.bitwise_and, ALU.bitwise_or).then_inc(s_mask, 1)
                        dve.wait_ge(s_mask, 3 * i + (n + 3))
                        ts(wmg[n][:, :], wmg[n][:, :], 1.5 * 2.0 ** -6, 2.0 ** 20, ALU.max, ALU.mult).then_inc(s_magic, 1)
                    for n, W in enumerate((GW, UW, DW)):
                        dve.wait_ge(s_shift, 3 * i + (n + 1))
                        tt(W[:, bass.ds(i * D, D)], wst[n][:, :], wmg[n][:, :], ALU.subtract).then_inc(s_quant, 1)

            timeline(body, prologue, dve)


def _consts():
    tok = np.arange(P)
    c, gp, h4 = tok % CH, tok // CH % 2, tok // 32
    table = np.zeros((P, NCONST), np.float32)
    table[:, C_ID:C_ID + P] = np.eye(P)
    table[:, C_REP:C_REP + P] = (tok[:, None] % CH) == c[None, :]
    same = (tok[:, None] // CH) == (tok[None, :] // CH)
    table[:, C_TRI:C_TRI + P] = same & (c[:, None] <= c[None, :])
    table[:, C_CHM:C_CHM + 64] = (tok[:, None] // CH) == (np.arange(64)[None, :] // 8)
    col = np.arange(8)
    table[:, C_ROW:C_ROW + 8] = (gp[:, None] == col[None, :] // 4) & (h4[:, None] == col[None, :] % 4)
    table[:, C_ROW:C_ROW + 8] *= KAPPA
    table[:, C_GPM:C_GPM + 2] = gp[:, None] == np.arange(2)[None, :]
    table[:, C_HM:C_HM + 4] = h4[:, None] == np.arange(4)[None, :]
    table[:, C_NH:C_NH + 16] = -0.5
    table[:, C_ONE:C_ONE + 16] = 1.0
    return table


def _by_row(a):
    a = a.reshape(2, 2, 4, DH).transpose(2, 0, 1, 3)[:, :, None]
    return np.broadcast_to(a, (4, 2, CH, 2, DH)).reshape(P, 2 * DH)


def kernel(L0_attn_x, L0_attn_Wq, L0_attn_Wk, L0_attn_Wv, L0_attn_Wo, L0_attn_Wbeta, L0_attn_ln_w, L0_attn_ln_b,
           L0_attn_Wg1, L0_attn_Wg2, L0_attn_norm_w, L0_ffn_gate_w, L0_ffn_up_w, L0_ffn_down_w,
           L0_ffn_gate_scale, L0_ffn_up_scale, L0_ffn_down_scale):
    import concourse.bacc as _bacc
    from concourse.bass_utils import run_bass_kernel_spmd as _run

    def blocks(a, n):
        return a.reshape(-1, P, n).transpose(1, 0, 2).reshape(P, -1)

    A = {k: np.asarray(v) for k, v in locals().items() if k.startswith("L0_")}
    ins = {
        "x": A["L0_attn_x"].reshape(T, D), "wq": A["L0_attn_Wq"], "wk": A["L0_attn_Wk"], "wv": A["L0_attn_Wv"],
        "wo": A["L0_attn_Wo"], "wbeta": A["L0_attn_Wbeta"], "wg1": A["L0_attn_Wg1"], "wg2": A["L0_attn_Wg2"],
        "norm_w": A["L0_attn_norm_w"].reshape(KD, P).T, "ln_w": _by_row(A["L0_attn_ln_w"]),
        "ln_b": _by_row(A["L0_attn_ln_b"]), "gate_w": blocks(A["L0_ffn_gate_w"], I),
        "up_w": blocks(A["L0_ffn_up_w"], I), "down_w": blocks(A["L0_ffn_down_w"], D),
        "gate_s": A["L0_ffn_gate_scale"].reshape(MI, P).T, "up_s": A["L0_ffn_up_scale"].reshape(MI, P).T,
        "down_s": A["L0_ffn_down_scale"], "consts": _consts(),
    }
    nc = _bacc.Bacc("TRN2", target_bir_lowering=False, num_devices=1)
    arrays, args = {}, {}
    for name, a in ins.items():
        a = np.ascontiguousarray(a)
        arrays[f"in_{name}"] = a
        args[name] = nc.dram_tensor(f"in_{name}", a.shape, mybir.dt.from_np(a.dtype), kind="ExternalInput").ap()
    args["out"] = nc.dram_tensor("out_0", (T, D), F32, kind="ExternalOutput").ap()
    build(nc, **args)
    r = _run(nc, [arrays], core_ids=[0])
    return r.results[0]["out_0"].reshape(1, T, D)
```

```python
from contextlib import ExitStack

import numpy as np

import concourse.bass as bass
from concourse import mybir

F32 = mybir.dt.float32
F32R = mybir.dt.float32r
I32 = mybir.dt.int32
ALU = mybir.AluOpType
ACT = mybir.ActivationFunctionType
AX_X = mybir.AxisListType.X

P = 128
T, D = 2048, 512
H, DH = 16, 32
CH = 16
DG = 32
I = 1536
NT = T // P
NC = P // CH
KD = D // P
MI = I // P
RM = 2
NR = MI // RM
PAIR = 2 * P
KAPPA = float(DH) ** 0.5
EPS_LN = 1e-5
EPS = 1e-6

C_ID = 0
C_REP = C_ID + P
C_TRI = C_REP + P
C_CHM = C_TRI + 64
C_ROW = C_CHM + 64
C_GPM = C_ROW + 8
C_HM = C_GPM + 2
C_NH = C_HM + 4
C_ONE = C_NH + 16
NCONST = C_ONE + 16


class Steps:

    def __init__(self, sem, names):
        self.sem, self.names, self.next = sem, names.split(), 0

    def one(self, name):
        assert self.names[self.next] == name, (name, self.names[self.next])
        self.next = (self.next + 1) % len(self.names)
        return self.sem, 1

    def at(self, name, n):
        return len(self.names) * n + self.names.index(name) + 1


def begun(n):
    return not isinstance(n, int) or n >= 0


def build(nc, x, wq, wk, wv, wo, wbeta, wg1, wg2, norm_w, ln_w, ln_b, gate_w, up_w, down_w,
          gate_s, up_s, down_s, ln_wf, ln_bf, consts, out):
    ctx = ExitStack()
    with ctx:
        def sb(name, cols, dt=F32, rows=P):
            return ctx.enter_context(nc.sbuf_tensor(name, [rows, cols], dt))

        def sem(name):
            return ctx.enter_context(nc.semaphore(name))

        Wq, Wk, Wv, Wo = (sb(n, KD * D) for n in ("Wq", "Wk", "Wv", "Wo"))
        Wg1, Wb = sb("Wg1", KD * DG), sb("Wb", KD * H)
        Wg2 = sb("Wg2", D, rows=DG)
        GW, UW, DW = (sb(n, KD * I, F32R) for n in ("GW", "UW", "DW"))
        nw, gs, us = sb("nw", KD), sb("gs", MI), sb("us", MI)
        ds = sb("ds", D)
        bR = sb("bR", 64)
        wF, bF, wbF = sb("wF", 4), sb("bF", 4), sb("wbF", 4)
        wK, w2K = sb("wK", 64), sb("w2K", 64)
        cst = sb("cst", NCONST)
        ident = cst[:, C_ID:C_ID + P]
        xt, xnT = sb("xt", D), sb("xnT", D)
        xn = dv = rT = sb("xn_dv_rT", D)
        qtok = kn = thT = sb("q_kn_th", D)
        g1T = sb("g1T", P, rows=DG)
        bt, bx = sb("bt", H), sb("bx", P)
        etaR, etaM = sb("etaR", 2 * 16), sb("etaM", 2 * 32)
        qT, qR, rR, kR, thR = ([sb(f"{n}{s}", D) for s in range(2)] for n in ("qT", "qR", "rR", "kR", "thR"))
        BDk = [sb(f"BDk{s}", 2 * NC * 2 * 64) for s in range(2)]
        BDq = sb("BDq", 2 * NC * 2 * 64)
        BDkR, ATB = sb("BDkR", 2 * P), sb("ATB", 2 * P)
        SQ = sb("SQ", 4 * 48)
        SQv = SQ[:, :].rearrange("p (g e) -> p g e", g=4)
        S = SQv[:, :, 0:DH]
        y, ysq = sb("y", 64), sb("ysq", 2 * 33)
        PR, sums, u = sb("PR", 3 * 64), sb("sums", 8), sb("u", 64)
        em = PR[:, 0:P]
        tv = sb("tv", 64)
        wR = tv
        ss, rho, re, rec, h2 = sb("ss", 2), sb("rho", 2), sb("re", 4), sb("rec", 2), sb("h2", 2)
        VX, VE = sb("VX", P), sb("VE", 64)
        x2, U = PR[:, 128:192], u
        qhR = [sb(f"qhR{s}", D) for s in range(2)]
        x1 = [sb(f"x1{s}", D) for s in range(2)]
        x1h = [sb(f"x1h{s}", D) for s in range(2)]
        o1, o2 = sb("o1", D), sb("o2", D)
        ogT = o1
        xh, xl = sb("xh", KD * PAIR, F32R), sb("xl", KD * PAIR, F32R)
        f = sb("f", D)
        fh, fl = sb("fh", D, F32R), sb("fl", D, F32R)
        yb = sb("yb", D)
        xn2 = [sb(f"xn2{s}", D) for s in range(2)]
        st = {n: sb(f"st_{n}", 6) for n in "paf"}
        st["y"] = sb("st_y", 6)
        mv = {n: sb(f"mv_{n}", 2) for n in "pafy"}
        ve = {n: sb(f"ve_{n}", 1) for n in "pafy"}
        rs = {n: sb(f"rs_{n}", 1) for n in "pafy"}
        nb = {"a": sb("nb_a", 1)}
        kss, kse, rk = sb("kss", H), sb("kse", H), sb("rk", H)
        qss, qse, rq = sb("qss", H), sb("qse", H), sb("rq", H)
        oss, ose, ro = sb("oss", H), sb("ose", H), sb("ro", H)
        rm = sb("rm", H)
        pause = sb("pause", 1)
        wst = [x1h[0], x1h[1], xn2[1]]
        wmg = [yb, f]

        bank = [ctx.enter_context(nc.psum_tensor(f"bank{n}", [P, 512], F32)) for n in range(8)]
        KA, dS = bank[0][:, 0:96], bank[0][:, 128:256]
        KAv = KA.rearrange("p (gh e) -> p gh e", gh=2)
        KH, AT = KAv[:, :, 0:DH], KAv[:, :, DH:48]
        QH = bank[1]
        PA, G, U4, Y = bank[2:4], bank[4], bank[5], bank[6:8]

        s_const, s_small = sem("s_const"), sem("s_small")
        s_wk, s_wv, s_wq, s_wo = sem("s_wk"), sem("s_wv"), sem("s_wq"), sem("s_wo")
        s_stage = [sem(f"s_stage{n}") for n in range(len(wst))]
        s_magic, s_shift, s_quant = sem("s_magic"), sem("s_shift"), sem("s_quant")
        s_mask = sem("s_mask")
        s_zero = sem("s_zero")
        s_setup = sem("s_setup")
        s_x, s_out = sem("s_x"), sem("s_out")
        s_xr = [sem(f"s_xr{s}") for s in range(2)]

        norm_v = Steps(sem("norm_v"), "stats mv veps xn")
        norm_g = Steps(sem("norm_g"), "rs")
        prep_v = Steps(sem("prep_v"), "kss kse bx qR kn d kR rR thR rm r em er eM")
        prep_a = Steps(sem("prep_a"), "xnT q g1 beta ksq qT BDk rT th")
        prep_t = Steps(sem("prep_t"), "xnT q g1 beta k qT1 qT2 v kT2 kT1 dT gate brow")
        prep_g = Steps(sem("prep_g"), "b1 rk qb")
        diag_a = Steps(sem("diag_a"), "q0 q1")
        chunk_v = Steps(sem("chunk_v"), "at")
        chunk_a = Steps(sem("chunk_a"), "q")
        chunk_g = Steps(sem("chunk_g"), "kR")
        scan_t = Steps(sem("scan_t"), "kh qs upd qa")
        scan_v = Steps(sem("scan_v"), "y ysq p ss ry py sums u h x2 U t ve vx S")
        scan_g = Steps(sem("scan_g"), "rho rec re")
        scan_a = Steps(sem("scan_a"), "qh")
        post_v = Steps(sem("post_v"), "qss qse n og oss ose on ogT")
        post_a = Steps(sem("post_a"), "qsq osq")
        post_g = Steps(sem("post_g"), "rq nw o ro")
        tail_t = Steps(sem("tail_t"), "wo")
        tail_v = Steps(sem("tail_v"), "as aa ave nb x1 fs fa fve xf")
        tail_a = Steps(sem("tail_a"), "xc")
        tail_g = Steps(sem("tail_g"), "ra rf")
        pair_t = Steps(sem("pair_t"), "xT0 xT1")
        pair_a = Steps(sem("pair_a"), "xh x1h")
        pair_v = Steps(sem("pair_v"), "xl")
        ffn_t = Steps(sem("ffn_t"), "g u")
        down_t = Steps(sem("down_t"), "dn")
        ffn_a = Steps(sem("ffn_a"), "silu fh")
        ffn_v = Steps(sem("ffn_v"), "f fl")
        fin_v = Steps(sem("fin_v"), "y ys ya yve yn out")
        fin_g = Steps(sem("fin_g"), "ry")

        x_t = x.rearrange("(t p) d -> t p d", p=P)
        out_t = out.rearrange("(t p) d -> t p d", p=P)

        def rows(t):
            return t[:, :].rearrange("p (m e) -> p m e", e=DH)

        def heads(t):
            return t[:, :].rearrange("p (h e) -> p h e", e=DH)

        def wide(t, n=DH):
            return t.unsqueeze(2).broadcast_to([t.shape[0], t.shape[1], n])

        def feat(t):
            return t[:, :].rearrange("p (lo m c) -> p m lo c", lo=2, c=CH)

        def bdk(s):
            return BDk[s][:, :].rearrange("p (m gp r) -> p m gp r", gp=2, r=64)

        bdq = BDq[:, :].rearrange("p (f g j r) -> p f g j r", f=2, g=4, j=4)

        def chunk_cols(t, j):
            return t[:, :].rearrange("p (gh j e) -> p gh j e", gh=2, e=DH)[:, :, j, :]

        bdkr = BDkR[:, :].rearrange("p (gh r) -> p gh r", gh=2)

        FILL, DRAIN = 4, 4

        def timeline(body, prologue, eng):
            prologue()
            for t in range(FILL):
                body(t, t % 2, t // 2)
            with eng.Fori(0, (NT - 2 - FILL) // 2) as i:
                for s in range(2):
                    body(2 * i + (FILL + s), s, i + FILL // 2)
            for t in range(NT - 2, NT + DRAIN):
                body(t, t % 2, t // 2)

        def live(t):
            if not isinstance(t, int):
                return True, True, True, True, True
            return t + 2 < NT, t + 1 < NT, t < NT, 0 <= t - 1 < NT, 0 <= t - 2 < NT

        def rounds(t, s, h):
            new, old = (h - 1, h - 2) if s else (None, h - 2)
            plan = [(0, old, 5, False), (1, old, 5, True), (3, new, 0, False), (4, new, 0, True),
                    (5, new, 1, False), (6, new, 1, True)] if s else \
                   [(0, old, 2, False), (2, old, 2, True), (3, old, 3, False), (4, old, 3, True),
                    (5, old, 4, False), (6, old, 4, True)]
            return [p for p in plan if is_pair(p[1])]

        def is_pair(p):
            return not isinstance(p, int) or 0 <= p < NT // 2

        def atb(j):
            return ATB[:, (j % 2) * P:(j % 2 + 1) * P].rearrange("p (gh r) -> p gh r", gh=2)

        UNITS = 3 * MI

        def units(t, j):
            c = NC * t + j if isinstance(t, int) else -1
            return [u for u in range(c * 3 // 2, (c + 1) * 3 // 2) if u < UNITS] if c >= 0 else []

        def last_units(t, j):
            return units(t, j - 1) if j else units(t - 1, NC - 1) if isinstance(t, int) and t else []

        block = ctx.enter_context(nc.Block())

        @block.sync
        def _(sp):
            def stage(u):
                src = (gate_w, up_w, down_w)[u % 3]
                sp.dma_start(wst[u % 3][:, :], src[:, u // 3 * D:(u // 3 + 1) * D]).then_inc(s_stage[u % 3], 16)

            sp.dma_start(xt[:, :], x_t[0]).then_inc(s_x, 16)
            sp.dma_start(cst[:, :], consts).then_inc(s_const, 16)
            sp.dma_start(Wq[:, :].rearrange("p (k n) -> p k n", k=KD),
                         wq.rearrange("(k p) n -> p k n", p=P)).then_inc(s_wq, 16)
            for dst, src in ((Wg1, wg1), (Wb, wbeta)):
                sp.dma_start(dst[:, :].rearrange("p (k n) -> p k n", k=KD),
                             src.rearrange("(k p) n -> p k n", p=P)).then_inc(s_small, 16)
            for dst, src, s in ((Wk, wk, s_wk), (Wv, wv, s_wv)):
                sp.dma_start(dst[:, :].rearrange("p (k n) -> p k n", k=KD),
                             src.rearrange("(k p) n -> p k n", p=P)).then_inc(s, 16)
            for dst, src in ((Wg2, wg2), (nw, norm_w), (gs, gate_s), (us, up_s), (wR, ln_w), (bR, ln_b),
                             (wF, ln_wf), (bF, ln_bf)):
                sp.dma_start(dst[:, :], src).then_inc(s_small, 16)
            sp.dma_start(ds[:, :], down_s.partition_broadcast(P)).then_inc(s_small, 16)
            sp.wait_ge(norm_v.sem, norm_v.at("xn", 0))
            sp.dma_start(xt[:, :], x_t[1]).then_inc(s_x, 16)
            sp.dma_start(Wo[:, :].rearrange("p (k n) -> p k n", k=KD),
                         wo.rearrange("(k p) n -> p k n", p=P)).then_inc(s_wo, 16)
            for u in range(3):
                stage(u)

            def body(t, s, h):
                norm, prep, scan, post, tail = live(t)
                if norm:
                    sp.wait_ge(norm_v.sem, norm_v.at("xn", t + 1))
                    sp.dma_start(xt[:, :], x_t[t + 2]).then_inc(s_x, 16)
                if tail:
                    if begun(h - 2):
                        sp.wait_ge(pair_a.sem, pair_a.at("x1h", h - 2))
                    sp.dma_start(x1[s][:, :], x_t[t - 2]).then_inc(s_xr[s], 16)
                for j in range(NC):
                    for u in last_units(t, j):
                        if u + 3 < UNITS:
                            sp.wait_ge(s_quant, u + 1)
                            stage(u + 3)
                if s and is_pair(h - 2):
                    for k in range(2):
                        sp.wait_ge(fin_v.sem, fin_v.at("out", 2 * (h - 2) + k))
                        sp.dma_start(out_t[t - 5 + k], x1h[k][:, :]).then_inc(s_out, 16)

            timeline(body, lambda: None, sp)
            sp.wait_ge(s_out, 16 * NT)

        @block.tensor
        def _(pe):
            mm = nc.tensor.matmul

            def proj(dst, W, n, one):
                for k in range(KD):
                    ins = mm(dst, xnT[:, k * P:(k + 1) * P], W[:, k * n:(k + 1) * n], start=(k == 0), stop=(k == KD - 1))
                ins.then_inc(*one)

            def turn(dst, src, one):
                for g in range(4):
                    ins = nc.tensor.transpose(dst[:, g * P:(g + 1) * P], src[:, g * P:(g + 1) * P], ident)
                ins.then_inc(*one)

            def turn_g(dst, src, one):
                for g in range(4):
                    for lo in range(2):
                        m = (2 * lo + g % 2) * P + g // 2 * 64
                        if lo == 0:
                            nc.tensor.transpose(dst[0:64, g * P:(g + 1) * P], src[:, m:m + 64], ident)
                        else:
                            ins = mm(dst[64:P, g * P:(g + 1) * P], src[:, m:m + 64], ident, start=True, stop=True)
                ins.then_inc(*one)

            def prep_xnT(t):
                pe.wait_ge(norm_v.sem, norm_v.at("xn", t))
                if begun(t - 1):
                    pe.wait_ge(prep_v.sem, prep_v.at("em", t - 1))
                turn(PA[0], xn, prep_t.one("xnT"))

            def prep_q(t):
                pe.wait_ge(prep_a.sem, prep_a.at("xnT", t))
                proj(PA[0][:, :], Wq, D, prep_t.one("q"))

            def prep_beta(t):
                pe.wait_ge(prep_a.sem, prep_a.at("q", t))
                for k in range(KD):
                    ins = mm(PA[0][0:DG, 0:P], Wg1[:, k * DG:(k + 1) * DG], xnT[:, k * P:(k + 1) * P],
                             start=(k == 0), stop=(k == KD - 1))
                ins.then_inc(*prep_t.one("g1"))
                proj(PA[0][:, P:P + H], Wb, H, prep_t.one("beta"))

            def prep_k(t):
                pe.wait_ge(prep_a.sem, prep_a.at("beta", t))
                if begun(t - 3):
                    pe.wait_ge(tail_v.sem, tail_v.at("x1", t - 3))
                proj(PA[0][:, :], Wk, D, prep_t.one("k"))

            def prep_qT1(t):
                turn_g(PA[1], qtok, prep_t.one("qT1"))

            def prep_qT2(t):
                pe.wait_ge(prep_a.sem, prep_a.at("qT", t))
                turn(PA[1], qtok, prep_t.one("qT2"))

            def prep_vv(t):
                pe.wait_ge(prep_v.sem, prep_v.at("qR", t))
                proj(PA[1][:, :], Wv, D, prep_t.one("v"))

            def prep_kT(t):
                pe.wait_ge(prep_v.sem, prep_v.at("d", t))
                turn(PA[1], kn, prep_t.one("kT2"))
                turn_g(PA[0], kn, prep_t.one("kT1"))

            def prep_dT(t):
                pe.wait_ge(prep_a.sem, prep_a.at("BDk", t))
                turn(PA[0], dv, prep_t.one("dT"))

            def prep_gate(t):
                pe.wait_ge(prep_v.sem, prep_v.at("kR", t))
                for m in range(4):
                    ins = mm(PA[1][:, m * P:(m + 1) * P], Wg2[:, m * P:(m + 1) * P], g1T[:, :], start=True, stop=True)
                ins.then_inc(*prep_t.one("gate"))

            def prep_brow(t):
                pe.wait_ge(prep_v.sem, prep_v.at("bx", t))
                pe.wait_ge(prep_a.sem, prep_a.at("rT", t))
                mm(PA[0][:, 0:P], cst[:, C_REP:C_REP + P], bx[:, :], start=True, stop=True).then_inc(*prep_t.one("brow"))

            def read_state(n, j, s):
                c = NC * n + j
                if j == 0:
                    pe.wait_ge(prep_a.sem, prep_a.at("BDk", n))
                pe.wait_ge(chunk_a.sem, chunk_a.at("q", c))
                if begun(c - 1):
                    pe.wait_ge(scan_v.sem, scan_v.at("S", c - 1))
                for gh in range(2):
                    for gp in range(2):
                        ins = mm(KAv[gp * 64:(gp + 1) * 64, gh, :], bdk(s)[:, gh * NC + j, gp, :],
                                 SQv[:, 2 * gh + gp, :], start=True, stop=True, skip_group_check=True)
                ins.then_inc(*scan_t.one("kh"))
                if j % 4 == 0:
                    pe.wait_ge(diag_a.sem, diag_a.at(f"q{j // 4}", n))
                if begun(c - 1):
                    pe.wait_ge(scan_a.sem, scan_a.at("qh", c - 1))
                for gh in range(2):
                    for gp in range(2):
                        ins = mm(QH[gp * 64:(gp + 1) * 64, gh * DH:(gh + 1) * DH], bdq[:, j // 4, 2 * gp + gh, j % 4, :],
                                 S[:, 2 * gh + gp, :], start=(gh == 0), stop=False, skip_group_check=True)
                ins.then_inc(*scan_t.one("qs"))

            def write_state(n, j):
                c = NC * n + j
                pe.wait_ge(chunk_g.sem, chunk_g.at("kR", c))
                pe.wait_ge(scan_v.sem, scan_v.at("vx", c))
                for gh in range(2):
                    ins = mm(dS[:, gh * 64:(gh + 1) * 64], bdkr[:, gh, :], VX[:, gh * 64:(gh + 1) * 64],
                             start=True, stop=True)
                ins.then_inc(*scan_t.one("upd"))
                for gh in range(2):
                    for gp in range(2):
                        p = slice(gp * 64, (gp + 1) * 64)
                        ins = mm(QH[p, gh * DH:(gh + 1) * DH], atb(j)[p, gh, :], VE[p, gh * DH:(gh + 1) * DH],
                                 start=False, stop=True, skip_group_check=True)
                ins.then_inc(*scan_t.one("qa"))

            def post_wo(n):
                pe.wait_ge(post_v.sem, post_v.at("ogT", n))
                if not isinstance(n, int) or n + 2 < NT:
                    pe.wait_ge(prep_a.sem, prep_a.at("th", n + 2))
                else:
                    if begun(n - 1):
                        pe.wait_ge(tail_v.sem, tail_v.at("x1", n - 1))
                for g in range(4):
                    ins = mm(PA[1][:, :], ogT[:, g * P:(g + 1) * P], Wo[:, g * D:(g + 1) * D], start=(g == 0), stop=(g == 3))
                ins.then_inc(*tail_t.one("wo"))

            def pair_xT(p):
                pe.wait_ge(tail_v.sem, tail_v.at("xf", 2 * p + 1))
                if begun(NR * p - 1):
                    pe.wait_ge(ffn_a.sem, ffn_a.at("silu", NR * p - 1))
                turn(G, xn2[0], pair_t.one("xT0"))
                if begun(NR * p - 1):
                    pe.wait_ge(ffn_v.sem, ffn_v.at("f", NR * p - 1))
                turn(U4, xn2[1], pair_t.one("xT1"))

            def ffn_gu(p, r):
                c = NR * p + r
                if r == 0:
                    if isinstance(p, int) and p == 0:
                        pe.wait_ge(s_quant, UNITS)
                    pe.wait_ge(pair_v.sem, pair_v.at("xl", p))
                for W, b, name in ((GW, G, "g"), (UW, U4, "u")):
                    if name == "g":
                        if begun(c - 1):
                            pe.wait_ge(ffn_a.sem, ffn_a.at("silu", c - 1))
                    else:
                        if begun(c - 1):
                            pe.wait_ge(ffn_v.sem, ffn_v.at("f", c - 1))
                    for q in range(RM):
                        m = RM * r + q
                        for part in (xh, xl):
                            for k in range(KD):
                                ins = mm(b[:, q * PAIR:(q + 1) * PAIR], W[:, k * I + m * P:k * I + (m + 1) * P],
                                         part[:, k * PAIR:(k + 1) * PAIR], start=(part is xh and k == 0),
                                         stop=(part is xl and k == KD - 1))
                    ins.then_inc(*ffn_t.one(name))

            def ffn_down(p, r):
                pe.wait_ge(ffn_v.sem, ffn_v.at("fl", NR * p + r))
                if r == 0:
                    if begun(2 * p - 1):
                        pe.wait_ge(fin_v.sem, fin_v.at("y", 2 * p - 1))
                for k in range(2):
                    for q in range(RM):
                        m = RM * r + q
                        for part in (fh, fl):
                            ins = mm(Y[k][:, :], part[:, q * PAIR + k * P:q * PAIR + (k + 1) * P], DW[:, m * D:(m + 1) * D],
                                     start=(m == 0 and part is fh), stop=(m == MI - 1 and part is fl))
                ins.then_inc(*down_t.one("dn"))

            def body(t, s, h):
                norm, prep, scan, post, tail = live(t)
                o = 1 - s
                ffn = {j: (p, r, down) for j, p, r, down in rounds(t, s, h)}

                def feed(j, down):
                    if j in ffn and ffn[j][2] == down:
                        p, r, _ = ffn[j]
                        (ffn_down if down else ffn_gu)(p, r)

                for j in range(NC):
                    if scan:
                        read_state(t, j, s)
                    if j == 0 and prep:
                        prep_xnT(t + 1)
                    if j == 1 and prep:
                        prep_q(t + 1)
                    if j == 2:
                        if s and is_pair(h - 1):
                            pair_xT(h - 1)
                        feed(j, True)
                        if prep:
                            prep_k(t + 1)
                    if j == 3 and prep:
                        prep_qT2(t + 1)
                    if j == 4 and prep:
                        prep_vv(t + 1)
                    if j == 5 and prep:
                        prep_kT(t + 1)
                    if j == 6:
                        if prep:
                            prep_dT(t + 1)
                        feed(j, True)
                    if j == 7 and post:
                        post_wo(t - 1)
                    feed(j, False)
                    if scan:
                        write_state(t, j)
                    if j in (1, 4):
                        feed(j, True)
                    if j == 1 and prep:
                        prep_beta(t + 1)
                    if j == 2 and prep:
                        prep_qT1(t + 1)
                    if j == 6 and prep:
                        prep_gate(t + 1)
                    if j == 7 and prep:
                        prep_brow(t + 1)

            def prologue():
                pe.wait_ge(s_const, 16)
                prep_xnT(0)
                pe.wait_ge(s_wq, 16)
                prep_q(0)
                pe.wait_ge(s_small, 16 * 11)
                prep_beta(0)
                pe.wait_ge(s_wk, 16)
                prep_k(0)
                prep_qT1(0)
                prep_qT2(0)
                pe.wait_ge(s_wv, 16)
                prep_vv(0)
                prep_kT(0)
                prep_dT(0)
                prep_gate(0)
                prep_brow(0)
                pe.wait_ge(s_setup, 4)

            timeline(body, prologue, pe)

        @block.scalar
        def _(act):
            fn = nc.scalar.activation

            def copy(dst, src, one):
                fn(dst, src, ACT.Copy).then_inc(*one)

            def prep_xnT(t):
                act.wait_ge(prep_t.sem, prep_t.at("xnT", t))
                if begun(t - 1):
                    act.wait_ge(prep_t.sem, prep_t.at("v", t - 1))
                copy(xnT[:, :], PA[0][:, :], prep_a.one("xnT"))

            def prep_q(t):
                act.wait_ge(prep_t.sem, prep_t.at("q", t))
                if begun(t - 1):
                    act.wait_ge(prep_v.sem, prep_v.at("thR", t - 1))
                fn(qtok[:, :], PA[0][:, :], ACT.Silu).then_inc(*prep_a.one("q"))

            def prep_g1(t):
                act.wait_ge(prep_t.sem, prep_t.at("beta", t))
                if begun(t - 1):
                    act.wait_ge(prep_t.sem, prep_t.at("gate", t - 1))
                copy(g1T[:, :], PA[0][0:DG, 0:P], prep_a.one("g1"))
                if begun(t - 1):
                    act.wait_ge(prep_v.sem, prep_v.at("bx", t - 1))
                fn(bt[:, :], PA[0][:, P:P + H], ACT.Tanh, scale=0.5).then_inc(*prep_a.one("beta"))

            def prep_ksq(t):
                act.wait_ge(prep_t.sem, prep_t.at("k", t))
                if begun(t - 1):
                    act.wait_ge(prep_v.sem, prep_v.at("rR", t - 1))
                fn(dv[:, :], PA[0][:, :], ACT.Square).then_inc(*prep_a.one("ksq"))

            def prep_qT(t, s):
                act.wait_ge(prep_t.sem, prep_t.at("qT1", t))
                copy(qT[s][:, :], PA[1][:, :], prep_a.one("qT"))

            def own(h):
                return slice(CH * (h % 2 * 2 + h // 2), CH * (h % 2 * 2 + h // 2 + 1))

            def prep_BDk(t, s):
                act.wait_ge(prep_t.sem, prep_t.at("kT1", t))
                if begun(NC * (t - 1) - 1):
                    act.wait_ge(scan_t.sem, scan_t.at("kh", NC * (t - 1) - 1))
                for h in range(4):
                    q = slice(32 * h, 32 * h + 32)
                    ins = fn(bdk(s)[q, :, :, own(h)].rearrange("p m gp c -> p gp m c"),
                             PA[0][q, :].rearrange("p (gp m c) -> p gp m c", gp=2, c=CH), ACT.Copy)
                ins.then_inc(*prep_a.one("BDk"))

            def prep_rT(t):
                act.wait_ge(prep_t.sem, prep_t.at("dT", t))
                for m in range(4):
                    ins = fn(rT[:, m * P:(m + 1) * P], PA[0][:, m * P:(m + 1) * P], ACT.Identity,
                             scale=wF[:, m:m + 1], bias=wbF[:, m:m + 1])
                ins.then_inc(*prep_a.one("rT"))

            def prep_th(t):
                act.wait_ge(prep_t.sem, prep_t.at("gate", t))
                fn(thT[:, :], PA[1][:, :], ACT.Tanh, scale=0.5).then_inc(*prep_a.one("th"))

            def diag_q(n, half, s):
                act.wait_ge(prep_a.sem, prep_a.at("qT", n))
                if begun(NC * (n - 1) + 4 * half + 3):
                    act.wait_ge(scan_t.sem, scan_t.at("qs", NC * (n - 1) + 4 * half + 3))
                for h in range(4):
                    q = slice(32 * h, 32 * h + 32)
                    ins = fn(bdq[q, half, :, :, own(h)],
                             qT[s][q, :].rearrange("p (g f j c) -> p f g j c", g=4, f=2, j=4)[:, half], ACT.Copy)
                ins.then_inc(*diag_a.one(f"q{half}"))

            def chunk_q(n, j, s):
                if j == 0:
                    act.wait_ge(prep_a.sem, prep_a.at("qT", n))
                fn(SQ[:, :].rearrange("p (gh gp e) -> p gh gp e", gh=2, gp=2)[:, :, :, DH:48],
                   qT[s][:, :].rearrange("p (gp gh j c) -> p j gh gp c", gp=2, gh=2, c=CH)[:, j], ACT.Copy)\
                    .then_inc(*chunk_a.one("q"))

            def take_qh(n, j, s):
                act.wait_ge(scan_t.sem, scan_t.at("qa", NC * n + j))
                if j == 0:
                    if begun(n - 2):
                        act.wait_ge(post_v.sem, post_v.at("n", n - 2))
                fn(chunk_cols(qhR[s], j), QH[:, 0:64].rearrange("p (gh e) -> p gh e", gh=2), ACT.Copy)\
                    .then_inc(*scan_a.one("qh"))

            def post_qsq(n, s):
                act.wait_ge(scan_a.sem, scan_a.at("qh", NC * n + NC - 1))
                if begun(n - 1):
                    act.wait_ge(tail_t.sem, tail_t.at("wo", n - 1))
                fn(o1[:, :], qhR[s][:, :], ACT.Square).then_inc(*post_a.one("qsq"))

            def post_osq(n):
                act.wait_ge(post_v.sem, post_v.at("og", n))
                fn(o1[:, :], o2[:, :], ACT.Square).then_inc(*post_a.one("osq"))

            def tail_xc(n, s, p):
                act.wait_ge(s_xr[s], 16 * p + 16)
                act.wait_ge(tail_v.sem, tail_v.at("nb", n))
                fn(x1[s][:, :], x1[s][:, :], ACT.Identity, bias=nb["a"][:, 0:1]).then_inc(*tail_a.one("xc"))

            def pair_xh(p):
                if begun(NR * p - 1):
                    act.wait_ge(ffn_t.sem, ffn_t.at("u", NR * p - 1))
                for k, b in enumerate((G, U4)):
                    act.wait_ge(pair_t.sem, pair_t.at(f"xT{k}", p))
                    ins = fn(xh[:, :].rearrange("p (k n) -> p k n", k=KD)[:, :, k * P:(k + 1) * P],
                             b[:, :].rearrange("p (k n) -> p k n", k=KD), ACT.Copy)
                ins.then_inc(*pair_a.one("xh"))

            def pair_x1h(p):
                act.wait_ge(tail_v.sem, tail_v.at("x1", 2 * p + 1))
                if not isinstance(p, int) or p > 0:
                    act.wait_ge(s_out, 32 * p)
                for k in range(2):
                    ins = fn(x1h[k][:, :], x1[k][:, :], ACT.Copy)
                ins.then_inc(*pair_a.one("x1h"))

            def ffn_silu(p, r):
                c = NR * p + r
                act.wait_ge(ffn_t.sem, ffn_t.at("g", c))
                if begun(c - 1):
                    act.wait_ge(ffn_v.sem, ffn_v.at("fl", c - 1))
                for q in range(RM):
                    ins = fn(f[:, q * PAIR:(q + 1) * PAIR], G[:, q * PAIR:(q + 1) * PAIR], ACT.Silu,
                             scale=gs[:, RM * r + q:RM * r + q + 1])
                ins.then_inc(*ffn_a.one("silu"))

            def ffn_fh(p, r):
                c = NR * p + r
                act.wait_ge(ffn_v.sem, ffn_v.at("f", c))
                if begun(c - 1):
                    act.wait_ge(down_t.sem, down_t.at("dn", c - 1))
                copy(fh[:, :], f[:, :], ffn_a.one("fh"))

            def body(t, s, h):
                norm, prep, scan, post, tail = live(t)
                o = 1 - s
                ffn = {j: (p, r) for j, p, r, down in rounds(t, s, h) if not down}
                for j in range(NC):
                    if scan and (prep or j + 1 < NC):
                        act.wait_ge(scan_t.sem, scan_t.at("kh", NC * t + j))
                        if j + 1 < NC:
                            chunk_q(t, j + 1, s)
                        else:
                            chunk_q(t + 1, 0, o)
                    if j == 0:
                        if prep:
                            prep_xnT(t + 1)
                        if post:
                            post_qsq(t - 1, o)
                    if j == 1:
                        if prep:
                            prep_q(t + 1)
                        if scan:
                            diag_q(t, 1, s)
                    if j == 2 and prep:
                        prep_ksq(t + 1)
                    if j == 4:
                        if post:
                            post_osq(t - 1)
                        if prep:
                            diag_q(t + 1, 0, o)
                    if j == 5 and prep:
                        prep_BDk(t + 1, o)
                    if j == 6 and prep:
                        prep_rT(t + 1)
                    if j in ffn:
                        ffn_silu(*ffn[j])
                    if scan:
                        take_qh(t, j, s)
                    if j in ffn:
                        ffn_fh(*ffn[j])
                    if j == 0 and tail:
                        tail_xc(t - 2, s, h - 1)
                    if j == 1 and prep:
                        prep_g1(t + 1)
                    if j == 2:
                        if prep:
                            prep_qT(t + 1, o)
                        if s and is_pair(h - 1):
                            pair_xh(h - 1)
                    if j == 6 and prep:
                        prep_th(t + 1)
                    if j == 7 and s and is_pair(h - 1):
                        pair_x1h(h - 1)

            def prologue():
                prep_xnT(0)
                prep_q(0)
                prep_g1(0)
                prep_ksq(0)
                prep_qT(0, 0)
                chunk_q(0, 0, 0)
                act.wait_ge(s_zero, 3)
                diag_q(0, 0, 0)
                prep_BDk(0, 0)
                act.wait_ge(s_setup, 1)
                prep_rT(0)
                prep_th(0)

            timeline(body, prologue, act)

        @block.gpsimd
        def _(pool):
            tt = nc.gpsimd.tensor_tensor

            def power(dst, src, n, one):
                tt(dst, src, cst[:, C_NH:C_NH + n], ALU.pow).then_inc(*one)

            def norm_rs(t):
                pool.wait_ge(norm_v.sem, norm_v.at("veps", t))
                power(rs["p"][:, :], ve["p"][:, :], 1, norm_g.one("rs"))

            def prep_rk(t):
                pool.wait_ge(prep_v.sem, prep_v.at("kse", t))
                power(rk[:, :], kse[:, :], H, prep_g.one("rk"))

            def prep_qb(t, s):
                pool.wait_ge(prep_v.sem, prep_v.at("qR", t))
                m = qR[s][:, :].rearrange("p (gh j e) -> p gh j e", gh=2, e=DH)
                tt(m, m, bR[:, :].rearrange("p (gh e) -> p gh e", gh=2).unsqueeze(2).broadcast_to([P, 2, NC, DH]),
                   ALU.add).then_inc(*prep_g.one("qb"))

            def prep_b1(t):
                pool.wait_ge(prep_a.sem, prep_a.at("beta", t))
                tt(bt[:, :], bt[:, :], cst[:, C_ONE:C_ONE + H], ALU.add).then_inc(*prep_g.one("b1"))

            def chunk_kR(n, j, s):
                c = NC * n + j
                if j == 0:
                    pool.wait_ge(prep_v.sem, prep_v.at("kR", n))
                if begun(c - 1):
                    pool.wait_ge(scan_t.sem, scan_t.at("upd", c - 1))
                for gh in range(2):
                    k = rows(kR[s])[:, gh * NC + j, :]
                    ins = tt(bdkr[:, gh, :].rearrange("p (h d) -> p h d", h=4),
                             k.unsqueeze(1).broadcast_to([P, 4, DH]),
                             wide(cst[:, C_HM:C_HM + 4]), ALU.mult)
                ins.then_inc(*chunk_g.one("kR"))

            def scan_rho(n, j, s):
                c = NC * n + j
                pool.wait_ge(scan_v.sem, scan_v.at("ss", c))
                if begun(c - 1):
                    pool.wait_ge(scan_v.sem, scan_v.at("vx", c - 1))
                power(rho[:, :], ss[:, :], 2, scan_g.one("rho"))
                if j == 0:
                    pool.wait_ge(prep_v.sem, prep_v.at("eM", n))
                pool.wait_ge(scan_g.sem, scan_g.at("rho", c))
                m = etaR[:, s * 16:s * 16 + 16].rearrange("p (gh j) -> p gh j", gh=2)[:, :, j]
                tt(rec[:, :], rho[:, :], m, ALU.mult).then_inc(*scan_g.one("rec"))
                m = etaM[:, s * 32:s * 32 + 32].rearrange("p (gh j gp) -> p gh j gp", gh=2, gp=2)[:, :, j, :]
                tt(re[:, :].rearrange("p (gh gp) -> p gh gp", gh=2), wide(rho[:, :], 2), m, ALU.mult).then_inc(*scan_g.one("re"))

            def post_rq(n):
                pool.wait_ge(post_v.sem, post_v.at("qse", n))
                power(rq[:, :], qse[:, :], H, post_g.one("rq"))

            def post_nw(n):
                pool.wait_ge(post_v.sem, post_v.at("n", n))
                m = o2[:, :].rearrange("p (gh j e) -> p gh j e", gh=2, e=DH)
                tt(m, m, wK[:, :].rearrange("p (gh e) -> p gh e", gh=2).unsqueeze(2).broadcast_to([P, 2, NC, DH]),
                   ALU.mult).then_inc(*post_g.one("nw"))

            def post_o(n, s):
                pool.wait_ge(post_g.sem, post_g.at("nw", n))
                pool.wait_ge(prep_g.sem, prep_g.at("qb", n))
                tt(o2[:, :], o2[:, :], qR[s][:, :], ALU.add).then_inc(*post_g.one("o"))

            def post_ro(n):
                pool.wait_ge(post_v.sem, post_v.at("ose", n))
                power(ro[:, :], ose[:, :], H, post_g.one("ro"))

            def tail_pow(n, k, before, name):
                pool.wait_ge(tail_v.sem, tail_v.at(before, n))
                power(rs[k][:, :], ve[k][:, :], 1, tail_g.one(name))

            def fin_ry(n):
                pool.wait_ge(fin_v.sem, fin_v.at("yve", n))
                power(rs["y"][:, :], ve["y"][:, :], 1, fin_g.one("ry"))

            def body(t, s, h):
                norm, prep, scan, post, tail = live(t)
                o = 1 - s
                fin = s and is_pair(h - 2)
                for j in range(NC):
                    if scan:
                        scan_rho(t, j, s)
                        if j + 1 < NC:
                            chunk_kR(t, j + 1, s)
                    for u in last_units(t, j):
                        pool.wait_ge(s_magic, u + 1)
                        tt(wst[u % 3][:, :], wst[u % 3][:, :], wmg[u % 2][:, :], ALU.add).then_inc(s_shift, 1)
                    if j == 1:
                        if tail:
                            tail_pow(t - 2, "f", "fve", "rf")
                        if post:
                            post_rq(t - 1)
                    if j == 2:
                        if norm:
                            norm_rs(t + 2)
                        if prep:
                            prep_b1(t + 1)
                        if post:
                            post_nw(t - 1)
                    if j == 3:
                        if fin:
                            fin_ry(2 * (h - 2))
                        if post:
                            post_o(t - 1, o)
                        if prep:
                            prep_rk(t + 1)
                    if j == 4:
                        if fin:
                            fin_ry(2 * (h - 2) + 1)
                        if prep:
                            prep_qb(t + 1, o)
                    if j == 5 and post:
                        post_ro(t - 1)
                    if j == 7:
                        if prep:
                            chunk_kR(t + 1, 0, o)
                        if post:
                            tail_pow(t - 1, "a", "ave", "ra")

            def prologue():
                for b in (BDk[0], BDq, BDk[1]):
                    nc.gpsimd.memset(b[:, :], 0.0).then_inc(s_zero, 1)
                pool.wait_ge(s_const, 16)
                norm_rs(0)
                prep_b1(0)
                prep_rk(0)
                norm_rs(1)
                prep_qb(0, 0)
                chunk_kR(0, 0, 0)

            timeline(body, prologue, pool)

        @block.vector
        def _(dve):
            tt, ts, stt = nc.vector.tensor_tensor, nc.vector.tensor_scalar, nc.vector.scalar_tensor_tensor
            red = nc.vector.tensor_reduce

            def add_eps(dst, src, eps, one):
                ts(dst, src, eps, None, ALU.add).then_inc(*one)

            def norm_stats(src, k, steps, names, n):
                a, b, c = names
                nc.vector.bn_stats(st[k][:, :], src).then_inc(*steps.one(a))
                dve.wait_ge(steps.sem, steps.at(a, n))
                nc.vector.memset(pause[:, :], 0.0)
                nc.vector.bn_aggr(mv[k][:, :], st[k][:, :]).then_inc(*steps.one(b))
                dve.wait_ge(steps.sem, steps.at(b, n))
                add_eps(ve[k][:, :], mv[k][:, 1:2], EPS_LN, steps.one(c))

            def x_stats(t):
                dve.wait_ge(s_x, 16 * t + 16)
                norm_stats(xt[:, :], "p", norm_v, ("stats", "mv", "veps"), t)

            def x_norm(t):
                dve.wait_ge(norm_g.sem, norm_g.at("rs", t))
                if begun(t - 1):
                    dve.wait_ge(prep_v.sem, prep_v.at("rR", t - 1))
                ts(xn[:, :], xt[:, :], mv["p"][:, 0:1], rs["p"][:, 0:1], ALU.subtract, ALU.mult)\
                    .then_inc(*norm_v.one("xn"))

            def prep_kss(t):
                dve.wait_ge(prep_a.sem, prep_a.at("ksq", t))
                red(kss[:, :], heads(dv), AX_X, ALU.add).then_inc(*prep_v.one("kss"))
                dve.wait_ge(prep_v.sem, prep_v.at("kss", t))
                add_eps(kse[:, :], kss[:, :], EPS, prep_v.one("kse"))

            def prep_bx(t):
                dve.wait_ge(prep_g.sem, prep_g.at("b1", t))
                if begun(t - 1):
                    dve.wait_ge(prep_t.sem, prep_t.at("brow", t - 1))
                for gh in range(2):
                    e = bt[:, :].rearrange("p (gp gh h) -> p gh gp h", gp=2, gh=2)[:, gh]
                    ins = tt(bx[:, gh * 64:(gh + 1) * 64].rearrange("p (j gp h) -> p j gp h", j=NC, gp=2),
                             e.unsqueeze(1).broadcast_to([P, NC, 2, 4]),
                             cst[:, C_CHM:C_CHM + 64].rearrange("p (j gp h) -> p j gp h", j=NC, gp=2), ALU.mult)
                ins.then_inc(*prep_v.one("bx"))

            def turn(dst, src, one):
                nc.vector.transpose(rows(dst), feat(src)).then_inc(*one)

            def prep_qR(t, s):
                dve.wait_ge(prep_t.sem, prep_t.at("qT2", t))
                if begun(t - 2):
                    dve.wait_ge(post_g.sem, post_g.at("o", t - 2))
                turn(qR[s], PA[1], prep_v.one("qR"))

            def prep_kn(t):
                dve.wait_ge(prep_g.sem, prep_g.at("rk", t))
                dve.wait_ge(prep_t.sem, prep_t.at("qT2", t))
                tt(heads(kn), heads(PA[0]), wide(rk[:, :]), ALU.mult).then_inc(*prep_v.one("kn"))
                dve.wait_ge(prep_v.sem, prep_v.at("kn", t))
                dve.wait_ge(prep_t.sem, prep_t.at("v", t))
                tt(dv[:, :], kn[:, :], PA[1][:, :], ALU.subtract).then_inc(*prep_v.one("d"))

            def prep_kR(t, s):
                dve.wait_ge(prep_t.sem, prep_t.at("kT2", t))
                turn(kR[s], PA[1], prep_v.one("kR"))

            def prep_rR(t, s):
                dve.wait_ge(prep_a.sem, prep_a.at("rT", t))
                turn(rR[s], rT, prep_v.one("rR"))

            def prep_thR(t, s):
                dve.wait_ge(prep_a.sem, prep_a.at("th", t))
                turn(thR[s], thT, prep_v.one("thR"))

            def prep_r(t, s):
                dve.wait_ge(prep_v.sem, prep_v.at("rR", t))
                red(rm[:, :], rows(rR[s]), AX_X, ALU.add).then_inc(*prep_v.one("rm"))
                dve.wait_ge(prep_v.sem, prep_v.at("rm", t))
                stt(out=rows(rR[s]), in0=wide(rm[:, :]), scalar=-1.0 / DH, in1=rows(rR[s]),
                    op0=ALU.mult, op1=ALU.add).then_inc(*prep_v.one("r"))

            def prep_eta(t, s):
                dve.wait_ge(prep_t.sem, prep_t.at("brow", t))
                tt(em.rearrange("p (m h) -> p m h", h=8), PA[0][:, 0:P].rearrange("p (m h) -> p m h", h=8),
                   cst[:, C_ROW:C_ROW + 8].unsqueeze(1).broadcast_to([P, 16, 8]), ALU.mult).then_inc(*prep_v.one("em"))
                dve.wait_ge(prep_v.sem, prep_v.at("em", t))
                red(etaR[:, s * 16:(s + 1) * 16], em.rearrange("p (m h) -> p m h", h=8), AX_X, ALU.add)\
                    .then_inc(*prep_v.one("er"))
                dve.wait_ge(prep_v.sem, prep_v.at("er", t))
                tt(etaM[:, s * 32:(s + 1) * 32].rearrange("p (m gp) -> p m gp", gp=2),
                   wide(etaR[:, s * 16:(s + 1) * 16], 2),
                   cst[:, C_GPM:C_GPM + 2].unsqueeze(1).broadcast_to([P, 16, 2]), ALU.mult).then_inc(*prep_v.one("eM"))

            def g2(t, w=DH):
                return t.rearrange("p (gh e) -> p gh e", e=w)

            def scan_front(n, j, s):
                c = NC * n + j
                dve.wait_ge(scan_t.sem, scan_t.at("kh", c))
                nc.vector.tensor_copy(g2(y[:, :]), KH).then_inc(*scan_v.one("y"))
                dve.wait_ge(scan_v.sem, scan_v.at("y", c))
                tt(g2(ysq[:, :], 33)[:, :, 0:DH], g2(y[:, :]), g2(y[:, :]), ALU.mult).then_inc(*scan_v.one("ysq"))
                tt(PR[:, 0:64], w2K[:, :], y[:, :], ALU.mult).then_inc(*scan_v.one("p"))
                dve.wait_ge(scan_v.sem, scan_v.at("ysq", c))
                red(ss[:, :], g2(ysq[:, :], 33), AX_X, ALU.add).then_inc(*scan_v.one("ss"))
                if j == 0:
                    dve.wait_ge(prep_v.sem, prep_v.at("r", n))
                tt(g2(PR[:, 128:192]), chunk_cols(rR[s], j), g2(y[:, :]), ALU.mult).then_inc(*scan_v.one("ry"))
                dve.wait_ge(scan_v.sem, scan_v.at("p", c))
                tt(PR[:, 64:128], PR[:, 0:64], y[:, :], ALU.mult).then_inc(*scan_v.one("py"))
                if begun(c - 2):
                    dve.wait_ge(scan_t.sem, scan_t.at("qa", c - 2))
                tt(atb(j).rearrange("p gh (h c) -> p gh h c", c=CH),
                   AT.unsqueeze(2).broadcast_to([P, 2, 4, CH]),
                   cst[:, C_TRI:C_TRI + 64].rearrange("p (h c) -> p h c", c=CH).unsqueeze(1)
                   .broadcast_to([P, 2, 4, CH]), ALU.mult).then_inc(*chunk_v.one("at"))
                dve.wait_ge(scan_v.sem, scan_v.at("py", c))
                red(sums[:, 0:6], PR[:, :].rearrange("p (g e) -> p g e", e=DH), AX_X, ALU.add)\
                    .then_inc(*scan_v.one("sums"))
                dve.wait_ge(scan_v.sem, scan_v.at("sums", c))
                stt(out=g2(u[:, :]), in0=wide(sums[:, 0:2]), scalar=1.0 / DH, in1=g2(PR[:, 0:64]),
                    op0=ALU.mult, op1=ALU.subtract).then_inc(*scan_v.one("u"))

            def scan_back(n, j, s):
                c = NC * n + j
                dve.wait_ge(scan_g.sem, scan_g.at("rho", c))
                for gh in range(2):
                    ins = stt(out=h2[:, gh:gh + 1], in0=sums[:, 2 + gh:3 + gh], scalar=rho[:, gh:gh + 1],
                              in1=sums[:, 4 + gh:5 + gh], op0=ALU.mult, op1=ALU.add)
                ins.then_inc(*scan_v.one("h"))
                for gh in range(2):
                    e = slice(gh * DH, (gh + 1) * DH)
                    ins = ts(x2[:, e], y[:, e], rho[:, gh:gh + 1], rho[:, gh:gh + 1], ALU.mult, ALU.mult)
                ins.then_inc(*scan_v.one("x2"))
                dve.wait_ge(scan_v.sem, scan_v.at("u", c))
                for gh in range(2):
                    e = slice(gh * DH, (gh + 1) * DH)
                    ins = stt(out=U[:, e], in0=u[:, e], scalar=rho[:, gh:gh + 1], in1=chunk_cols(rR[s], j)[:, gh, :],
                              op0=ALU.mult, op1=ALU.subtract)
                ins.then_inc(*scan_v.one("U"))
                dve.wait_ge(scan_v.sem, scan_v.at("U", c))
                for gh in range(2):
                    e = slice(gh * DH, (gh + 1) * DH)
                    ins = stt(out=tv[:, e], in0=x2[:, e], scalar=h2[:, gh:gh + 1], in1=U[:, e],
                              op0=ALU.mult, op1=ALU.add)
                ins.then_inc(*scan_v.one("t"))
                dve.wait_ge(scan_v.sem, scan_v.at("t", c))
                dve.wait_ge(scan_g.sem, scan_g.at("re", c))
                if begun(c - 1):
                    dve.wait_ge(scan_t.sem, scan_t.at("qa", c - 1))
                tt(g2(VE[:, :]), g2(tv[:, :]), wide(rec[:, :]), ALU.mult).then_inc(*scan_v.one("ve"))
                tt(VX[:, :].rearrange("p (gh gp e) -> p gh gp e", gh=2, gp=2),
                   g2(tv[:, :]).unsqueeze(2).broadcast_to([P, 2, 2, DH]),
                   g2(re[:, :], 2).unsqueeze(3).broadcast_to([P, 2, 2, DH]), ALU.mult).then_inc(*scan_v.one("vx"))

            def scan_state(n, j):
                c = NC * n + j
                dve.wait_ge(scan_t.sem, scan_t.at("upd", c))
                tt(S, S, dS.rearrange("p (g e) -> p g e", e=DH), ALU.add).then_inc(*scan_v.one("S"))

            def post_qss(n):
                dve.wait_ge(post_a.sem, post_a.at("qsq", n))
                red(qss[:, :], rows(o1), AX_X, ALU.add).then_inc(*post_v.one("qss"))
                dve.wait_ge(post_v.sem, post_v.at("qss", n))
                add_eps(qse[:, :], qss[:, :], DH * EPS, post_v.one("qse"))

            def post_n(n, s):
                dve.wait_ge(post_g.sem, post_g.at("rq", n))
                tt(rows(o2), rows(qhR[s]), wide(rq[:, :]), ALU.mult).then_inc(*post_v.one("n"))

            def post_og(n, s):
                dve.wait_ge(post_g.sem, post_g.at("o", n))
                stt(out=o2[:, :], in0=thR[s][:, :], scalar=1.0, in1=o2[:, :], op0=ALU.add, op1=ALU.mult)\
                    .then_inc(*post_v.one("og"))

            def post_oss(n):
                dve.wait_ge(post_a.sem, post_a.at("osq", n))
                red(oss[:, :], rows(o1), AX_X, ALU.add).then_inc(*post_v.one("oss"))
                dve.wait_ge(post_v.sem, post_v.at("oss", n))
                add_eps(ose[:, :], oss[:, :], 4 * DH * EPS, post_v.one("ose"))

            def post_on(n):
                dve.wait_ge(post_g.sem, post_g.at("ro", n))
                tt(rows(o2), rows(o2), wide(ro[:, :]), ALU.mult).then_inc(*post_v.one("on"))

            def post_ogT(n):
                dve.wait_ge(post_v.sem, post_v.at("on", n))
                nc.vector.transpose(feat(ogT), rows(o2)).then_inc(*post_v.one("ogT"))

            def tail_stats(n):
                dve.wait_ge(tail_t.sem, tail_t.at("wo", n))
                norm_stats(PA[1][:, :], "a", tail_v, ("as", "aa", "ave"), n)

            def tail_nb(n):
                dve.wait_ge(tail_g.sem, tail_g.at("ra", n))
                stt(out=nb["a"][:, :], in0=mv["a"][:, 0:1], scalar=-1.0, in1=rs["a"][:, :], op0=ALU.mult, op1=ALU.mult)\
                    .then_inc(*tail_v.one("nb"))

            def tail_x1(n, s):
                dve.wait_ge(tail_a.sem, tail_a.at("xc", n))
                stt(out=x1[s][:, :], in0=PA[1][:, :], scalar=rs["a"][:, 0:1], in1=x1[s][:, :], op0=ALU.mult, op1=ALU.add)\
                    .then_inc(*tail_v.one("x1"))
                dve.wait_ge(tail_v.sem, tail_v.at("x1", n))
                norm_stats(x1[s][:, :], "f", tail_v, ("fs", "fa", "fve"), n)

            def tail_xf(n, s, p):
                dve.wait_ge(tail_g.sem, tail_g.at("rf", n))
                if begun(p - 1):
                    dve.wait_ge(pair_t.sem, pair_t.at(f"xT{s}", p - 1))
                ts(xn2[s][:, :], x1[s][:, :], mv["f"][:, 0:1], rs["f"][:, 0:1], ALU.subtract, ALU.mult)\
                    .then_inc(*tail_v.one("xf"))

            def pair_xl(p):
                dve.wait_ge(pair_a.sem, pair_a.at("xh", p))
                for k, b in enumerate((G, U4)):
                    v = [a[:, :].rearrange("p (k n) -> p k n", k=KD)[:, :, k * P:(k + 1) * P] for a in (xl, xh)]
                    ins = tt(v[0], b[:, :].rearrange("p (k n) -> p k n", k=KD), v[1].bitcast(F32), ALU.subtract)
                ins.then_inc(*pair_v.one("xl"))

            def ffn_f(p, r):
                c = NR * p + r
                dve.wait_ge(ffn_a.sem, ffn_a.at("silu", c))
                dve.wait_ge(ffn_t.sem, ffn_t.at("u", c))
                for q in range(RM):
                    e = slice(q * PAIR, (q + 1) * PAIR)
                    ins = stt(out=f[:, e], in0=U4[:, e], scalar=us[:, RM * r + q:RM * r + q + 1], in1=f[:, e],
                              op0=ALU.mult, op1=ALU.mult)
                ins.then_inc(*ffn_v.one("f"))

            def ffn_fl(p, r):
                dve.wait_ge(ffn_a.sem, ffn_a.at("fh", NR * p + r))
                tt(fl[:, :], f[:, :], fh[:, :].bitcast(F32), ALU.subtract).then_inc(*ffn_v.one("fl"))

            def fin_y(n, k, p):
                dve.wait_ge(down_t.sem, down_t.at("dn", NR * p + NR - 1))
                if begun(n - 1):
                    dve.wait_ge(fin_v.sem, fin_v.at("out", n - 1))
                tt(yb[:, :], Y[k][:, :], ds[:, :], ALU.mult).then_inc(*fin_v.one("y"))
                dve.wait_ge(fin_v.sem, fin_v.at("y", n))
                norm_stats(yb[:, :], "y", fin_v, ("ys", "ya", "yve"), n)

            def fin_out(n, k):
                dve.wait_ge(fin_g.sem, fin_g.at("ry", n))
                ts(yb[:, :], yb[:, :], mv["y"][:, 0:1], rs["y"][:, 0:1], ALU.subtract, ALU.mult)\
                    .then_inc(*fin_v.one("yn"))
                dve.wait_ge(fin_v.sem, fin_v.at("yn", n))
                tt(x1h[k][:, :], yb[:, :], x1h[k][:, :], ALU.add).then_inc(*fin_v.one("out"))

            def magic(u):
                dve.wait_ge(s_stage[u % 3], 16 * (u // 3 + 1))
                if u >= 2:
                    dve.wait_ge(s_quant, u - 1)
                m = wmg[u % 2]
                ts(m[:, :].bitcast(I32), wst[u % 3][:, :].bitcast(I32), 0x7F800000, 0x00400000,
                   ALU.bitwise_and, ALU.bitwise_or).then_inc(s_mask, 1)
                dve.wait_ge(s_mask, u + 3)
                ts(m[:, :], m[:, :], 1.5 * 2.0 ** -6, 2.0 ** 20, ALU.max, ALU.mult).then_inc(s_magic, 1)

            def quantize(u):
                dve.wait_ge(s_shift, u + 1)
                tt((GW, UW, DW)[u % 3][:, u // 3 * D:(u // 3 + 1) * D], wst[u % 3][:, :], wmg[u % 2][:, :], ALU.subtract)\
                    .then_inc(s_quant, 1)

            def body(t, s, h):
                norm, prep, scan, post, tail = live(t)
                o = 1 - s
                fin = s and is_pair(h - 2)
                ffn = {j: (p, r) for j, p, r, down in rounds(t, s, h) if not down}
                for j in range(NC):
                    if scan:
                        scan_front(t, j, s)
                        scan_back(t, j, s)
                    if j == 0 and tail:
                        tail_nb(t - 2)
                    if j in ffn:
                        ffn_f(*ffn[j])
                    if j == 1 and post:
                        post_qss(t - 1)
                    if j == 2 and post:
                        post_n(t - 1, o)
                    if j == 4 and post:
                        post_oss(t - 1)
                    if j == 6 and post:
                        post_on(t - 1)
                    if j == 7 and prep:
                        prep_thR(t + 1, o)
                    if scan:
                        scan_state(t, j)
                    if j in ffn:
                        ffn_fl(*ffn[j])
                    if j == 0 and tail:
                        tail_x1(t - 2, s)
                    if j == 1:
                        if tail:
                            tail_xf(t - 2, s, h - 1)
                        if norm:
                            x_stats(t + 2)
                    if j == 2:
                        if prep:
                            prep_kss(t + 1)
                            prep_bx(t + 1)
                        if s and is_pair(h - 1):
                            pair_xl(h - 1)
                        if fin:
                            fin_y(2 * (h - 2), 0, h - 2)
                    if j == 3:
                        if prep:
                            prep_qR(t + 1, o)
                        if post:
                            post_og(t - 1, o)
                        if fin:
                            fin_out(2 * (h - 2), 0)
                            fin_y(2 * (h - 2) + 1, 1, h - 2)
                    if j == 4:
                        if prep:
                            prep_kn(t + 1)
                        if fin:
                            fin_out(2 * (h - 2) + 1, 1)
                    if j == 5 and prep:
                        prep_kR(t + 1, o)
                    if j == 6:
                        if post:
                            post_ogT(t - 1)
                        if prep:
                            prep_rR(t + 1, o)
                    if j == 7:
                        if prep:
                            prep_r(t + 1, o)
                            prep_eta(t + 1, o)
                        if post:
                            tail_stats(t - 1)
                        if norm:
                            x_norm(t + 2)
                    for u in last_units(t, j):
                        quantize(u)
                    for u in units(t, j):
                        magic(u)

            def prologue():
                nc.vector.memset(S, 0.0).then_inc(s_mask, 1)
                nc.vector.memset(g2(ysq[:, :], 33)[:, :, DH:DH + 1], DH * EPS).then_inc(s_mask, 1)
                x_stats(0)
                x_norm(0)
                dve.wait_ge(s_small, 16 * 11)
                tt(wbF[:, :], wF[:, :], bF[:, :], ALU.mult).then_inc(s_setup, 1)
                ts(wK[:, :], wR[:, :], KAPPA, None, ALU.mult).then_inc(s_setup, 1)
                stt(out=w2K[:, :], in0=wR[:, :], scalar=KAPPA, in1=wR[:, :], op0=ALU.mult, op1=ALU.mult)\
                    .then_inc(s_setup, 1)
                x_stats(1)
                prep_kss(0)
                prep_bx(0)
                prep_qR(0, 0)
                prep_kn(0)
                prep_kR(0, 0)
                prep_rR(0, 0)
                prep_thR(0, 0)
                prep_r(0, 0)
                prep_eta(0, 0)
                x_norm(1)
                dve.wait_ge(s_wo, 16)
                for g in range(KD):
                    e = slice(g * D, (g + 1) * D)
                    ins = ts(Wo[:, e], Wo[:, e], nw[:, g:g + 1], KAPPA, ALU.mult, ALU.mult)
                ins.then_inc(s_setup, 1)
                dve.wait_ge(s_setup, 4)
                dve.wait_ge(s_mask, 2)

            timeline(body, prologue, dve)


def _consts():
    tok = np.arange(P)
    c, gp, h4 = tok % CH, tok // 64, tok // CH % 4
    table = np.zeros((P, NCONST), np.float32)
    table[:, C_ID:C_ID + P] = np.eye(P)
    table[:, C_REP:C_REP + P] = (tok[:, None] % CH) == c[None, :]
    table[:, C_TRI:C_TRI + 64] = (h4[:, None] == h4[None, :64]) & (c[:, None] <= c[None, :64])
    table[:, C_CHM:C_CHM + 64] = (tok[:, None] // CH) == (np.arange(64)[None, :] // 8)
    col = np.arange(8)
    table[:, C_ROW:C_ROW + 8] = (gp[:, None] == col[None, :] // 4) & (h4[:, None] == col[None, :] % 4)
    table[:, C_ROW:C_ROW + 8] *= KAPPA
    table[:, C_GPM:C_GPM + 2] = gp[:, None] == np.arange(2)[None, :]
    table[:, C_HM:C_HM + 4] = h4[:, None] == np.array([0, 2, 1, 3])[None, :]
    table[:, C_NH:C_NH + 16] = -0.5
    table[:, C_ONE:C_ONE + 16] = 1.0
    return table


def _by_row(a):
    a = a.reshape(2, 2, 4, DH).transpose(0, 2, 1, 3)[:, :, None]
    return np.broadcast_to(a, (2, 4, CH, 2, DH)).reshape(P, 2 * DH)


def _by_feature(a):
    a = a.reshape((2, 2, 2, 2, DH) + a.shape[1:])
    return a.transpose((3, 1, 0, 2) + tuple(range(4, a.ndim))).reshape((4, P) + a.shape[5:])


def kernel(L0_attn_x, L0_attn_Wq, L0_attn_Wk, L0_attn_Wv, L0_attn_Wo, L0_attn_Wbeta, L0_attn_ln_w, L0_attn_ln_b,
           L0_attn_Wg1, L0_attn_Wg2, L0_attn_norm_w, L0_ffn_gate_w, L0_ffn_up_w, L0_ffn_down_w,
           L0_ffn_gate_scale, L0_ffn_up_scale, L0_ffn_down_scale):
    import concourse.bacc as _bacc
    from concourse.bass_utils import run_bass_kernel_spmd as _run

    def blocks(a, n):
        return a.reshape(-1, P, n).transpose(1, 0, 2).reshape(P, -1)

    def columns(a):
        return _by_feature(a.T).reshape(D, -1).T

    A = {k: np.asarray(v) for k, v in locals().items() if k.startswith("L0_")}
    ins = {
        "x": A["L0_attn_x"].reshape(T, D), "wq": columns(A["L0_attn_Wq"]),
        "wk": columns(A["L0_attn_Wk"]), "wv": columns(A["L0_attn_Wv"]),
        "wo": _by_feature(A["L0_attn_Wo"]).reshape(D, D), "wbeta": A["L0_attn_Wbeta"], "wg1": A["L0_attn_Wg1"], "wg2": columns(A["L0_attn_Wg2"]),
        "norm_w": _by_feature(A["L0_attn_norm_w"]).T, "ln_w": _by_row(A["L0_attn_ln_w"]),
        "ln_b": _by_row(A["L0_attn_ln_b"]), "gate_w": blocks(A["L0_ffn_gate_w"], I),
        "up_w": blocks(A["L0_ffn_up_w"], I), "down_w": blocks(A["L0_ffn_down_w"], D),
        "gate_s": A["L0_ffn_gate_scale"].reshape(MI, P).T, "up_s": A["L0_ffn_up_scale"].reshape(MI, P).T,
        "down_s": A["L0_ffn_down_scale"], "ln_wf": _by_feature(A["L0_attn_ln_w"].reshape(-1)).T,
        "ln_bf": _by_feature(A["L0_attn_ln_b"].reshape(-1)).T, "consts": _consts(),
    }
    nc = _bacc.Bacc("TRN2", target_bir_lowering=False, num_devices=1)
    arrays, args = {}, {}
    for name, a in ins.items():
        a = np.ascontiguousarray(a)
        arrays[f"in_{name}"] = a
        args[name] = nc.dram_tensor(f"in_{name}", a.shape, mybir.dt.from_np(a.dtype), kind="ExternalInput").ap()
    args["out"] = nc.dram_tensor("out_0", (T, D), F32, kind="ExternalOutput").ap()
    build(nc, **args)
    r = _run(nc, [arrays], core_ids=[0])
    return r.results[0]["out_0"].reshape(1, T, D)
```

```python
from contextlib import ExitStack

import numpy as np

import concourse.bass as bass
from concourse import mybir

F32 = mybir.dt.float32
F32R = mybir.dt.float32r
I32 = mybir.dt.int32
ALU = mybir.AluOpType
ACT = mybir.ActivationFunctionType
AX_X = mybir.AxisListType.X

P = 128
T, D = 2048, 512
H, DH = 16, 32
CH = 16
DG = 32
I = 1536
NT = T // P
NC = P // CH
KD = D // P
MI = I // P
RM = 2
NR = MI // RM
PAIR = 2 * P
KAPPA = float(DH) ** 0.5
EPS_LN = 1e-5
EPS = 1e-6

C_ID = 0
C_REP = C_ID + P
C_TRI = C_REP + P
C_CHM = C_TRI + 64
C_ROW = C_CHM + 64
C_GPM = C_ROW + 8
C_HM = C_GPM + 2
C_NH = C_HM + 4
C_ONE = C_NH + 16
C_CEN = C_ONE + 16
NCONST = C_CEN + P


class Steps:

    def __init__(self, sem, names):
        self.sem, self.names, self.next = sem, names.split(), 0

    def one(self, name):
        assert self.names[self.next] == name, (name, self.names[self.next])
        self.next = (self.next + 1) % len(self.names)
        return self.sem, 1

    def at(self, name, n):
        return len(self.names) * n + self.names.index(name) + 1


def begun(n):
    return not isinstance(n, int) or n >= 0


def build(nc, x, wq, wk, wv, wo, wbeta, wg1, wg2, norm_w, ln_w, ln_b, gate_w, up_w, down_w,
          gate_s, up_s, down_s, ln_wf, ln_bf, consts, out):
    ctx = ExitStack()
    with ctx:
        def sb(name, cols, dt=F32, rows=P):
            return ctx.enter_context(nc.sbuf_tensor(name, [rows, cols], dt))

        def sem(name):
            return ctx.enter_context(nc.semaphore(name))

        Wq, Wk, Wv, Wo = (sb(n, KD * D) for n in ("Wq", "Wk", "Wv", "Wo"))
        Wg1, Wb = sb("Wg1", KD * DG), sb("Wb", KD * H)
        Wg2 = sb("Wg2", D, rows=DG)
        GW, UW, DW = (sb(n, KD * I, F32R) for n in ("GW", "UW", "DW"))
        nw, gs, us = sb("nw", KD), sb("gs", MI), sb("us", MI)
        ds = sb("ds", D)
        bR = sb("bR", 64)
        wF, bF, wbF = sb("wF", 4), sb("bF", 4), sb("wbF", 4)
        wK, w2K = sb("wK", 64), sb("w2K", 64)
        cst = sb("cst", NCONST)
        ident = cst[:, C_ID:C_ID + P]
        xt, xnT = sb("xt", D), sb("xnT", D)
        xn = dv = rT = sb("xn_dv_rT", D)
        qtok = kn = thT = sb("q_kn_th", D)
        g1T = sb("g1T", P, rows=DG)
        bt, bx = sb("bt", H), sb("bx", P)
        etaR, etaM = sb("etaR", 2 * 16), sb("etaM", 2 * 32)
        qT, qR, rR, kR, thR = ([sb(f"{n}{s}", D) for s in range(2)] for n in ("qT", "qR", "rR", "kR", "thR"))
        BDk = [sb(f"BDk{s}", 2 * NC * 2 * 64) for s in range(2)]
        BDq = sb("BDq", 2 * NC * 2 * 64)
        BDkR, ATB = sb("BDkR", 2 * P), sb("ATB", P)
        SQ = sb("SQ", 4 * 48)
        SQv = SQ[:, :].rearrange("p (g e) -> p g e", g=4)
        S = SQv[:, :, 0:DH]
        ka, ysq = sb("ka", 2 * 48), sb("ysq", 2 * 33)
        kav = ka[:, :].rearrange("p (gh e) -> p gh e", gh=2)
        y, kq = kav[:, :, 0:DH], kav[:, :, DH:48]
        PR, sums, u = sb("PR", 3 * 64), sb("sums", 8), sb("u", 64)
        yy = sb("yy", 2 * 64)
        em = PR[:, 0:P]
        VX, VE = sb("VX", P), sb("VE", 64)
        wR = VE
        ss, rho, re, rec = sb("ss", 2), sb("rho", 2), sb("re", 4), sb("rec", 2)
        qhR = [sb(f"qhR{s}", D) for s in range(2)]
        x1 = [sb(f"x1{s}", D) for s in range(2)]
        x1h = [sb(f"x1h{s}", D) for s in range(2)]
        o1, o2 = sb("o1", D), sb("o2", D)
        ogT = o1
        xh, xl = sb("xh", KD * PAIR, F32R), sb("xl", KD * PAIR, F32R)
        f = sb("f", D)
        fh, fl = sb("fh", D, F32R), sb("fl", D, F32R)
        yb = sb("yb", D)
        xn2 = [sb(f"xn2{s}", D) for s in range(2)]
        st = {n: sb(f"st_{n}", 6) for n in "paf"}
        st["y"] = sb("st_y", 6)
        mv = {n: sb(f"mv_{n}", 2) for n in "pafy"}
        ve = {n: sb(f"ve_{n}", 1) for n in "pafy"}
        rs = {n: sb(f"rs_{n}", 1) for n in "pafy"}
        nm = {n: sb(f"nm_{n}", 1) for n in "pafy"}
        nb = {n: sb(f"nb_{n}", 1) for n in "pafy"}
        kss, rk = sb("kss", H), sb("rk", H)
        qss, rq = sb("qss", H), sb("rq", H)
        oss, ro = sb("oss", H), sb("ro", H)
        pause = sb("pause", 1)
        wst = [x1h[0], x1h[1], xn2[1]]
        wmg = [yb, f]

        bank = [ctx.enter_context(nc.psum_tensor(f"bank{n}", [P, 512], F32)) for n in range(8)]
        KA, dS = bank[0][:, 0:96], bank[0][:, 128:256]
        KAv = KA.rearrange("p (gh e) -> p gh e", gh=2)
        KH = KAv[:, :, 0:DH]
        QH = bank[1]
        PA, G, U4, Y = bank[2:4], bank[4], bank[5], bank[6:8]

        s_const, s_small = sem("s_const"), sem("s_small")
        s_wk, s_wv, s_wq, s_wo = sem("s_wk"), sem("s_wv"), sem("s_wq"), sem("s_wo")
        s_stage = [sem(f"s_stage{n}") for n in range(len(wst))]
        s_magic, s_shift, s_quant = sem("s_magic"), sem("s_shift"), sem("s_quant")
        s_mask = sem("s_mask")
        s_zero = sem("s_zero")
        s_setup = sem("s_setup")
        s_x, s_out = sem("s_x"), sem("s_out")
        s_xr = [sem(f"s_xr{s}") for s in range(2)]

        norm_v = Steps(sem("norm_v"), "stats mv nm veps")
        norm_g = Steps(sem("norm_g"), "rs nb")
        norm_a = Steps(sem("norm_a"), "xn")
        prep_v = Steps(sem("prep_v"), "kss kse qR kn d kR bx rR thR em er eM")
        prep_a = Steps(sem("prep_a"), "xnT q ksq qT BDk g1 beta rT th")
        prep_t = Steps(sem("prep_t"), "xnT q k qT1 qT2 v kT2 kT1 g1 beta dT gate cen brow")
        prep_g = Steps(sem("prep_g"), "rk b1 qb")
        diag_a = Steps(sem("diag_a"), "q0 q1")
        chunk_a = Steps(sem("chunk_a"), "q")
        chunk_g = Steps(sem("chunk_g"), "kR at")
        scan_t = Steps(sem("scan_t"), "kh qs upd qa")
        scan_v = Steps(sem("scan_v"), "y p ysq ry ss py sums u yy h0 h1 g0 g1 t0 t1 vx ve S")
        scan_g = Steps(sem("scan_g"), "rho rec re")
        scan_a = Steps(sem("scan_a"), "qh")
        post_v = Steps(sem("post_v"), "qss qse n og oss ose on ogT")
        post_a = Steps(sem("post_a"), "qsq osq")
        post_g = Steps(sem("post_g"), "rq nw o ro")
        tail_t = Steps(sem("tail_t"), "wo")
        tail_v = Steps(sem("tail_v"), "as aa anm ave x1 fs fa fnm fve")
        tail_a = Steps(sem("tail_a"), "xc xf")
        tail_g = Steps(sem("tail_g"), "ra nba rf nbf")
        pair_t = Steps(sem("pair_t"), "xT0 xT1")
        pair_a = Steps(sem("pair_a"), "xh x1h")
        pair_v = Steps(sem("pair_v"), "xl")
        ffn_t = Steps(sem("ffn_t"), "g u")
        down_t = Steps(sem("down_t"), "dn")
        ffn_a = Steps(sem("ffn_a"), "silu fh")
        ffn_v = Steps(sem("ffn_v"), "f")
        low_v, low_g = Steps(sem("low_v"), "fl"), Steps(sem("low_g"), "fl")
        fin_v = Steps(sem("fin_v"), "y ys ya ynm yve out")
        fin_g = Steps(sem("fin_g"), "ry nby")
        fin_a = Steps(sem("fin_a"), "yc")

        x_t = x.rearrange("(t p) d -> t p d", p=P)
        out_t = out.rearrange("(t p) d -> t p d", p=P)

        def rows(t):
            return t[:, :].rearrange("p (m e) -> p m e", e=DH)

        def heads(t):
            return t[:, :].rearrange("p (h e) -> p h e", e=DH)

        def wide(t, n=DH):
            return t.unsqueeze(2).broadcast_to([t.shape[0], t.shape[1], n])

        def feat(t):
            return t[:, :].rearrange("p (lo m c) -> p m lo c", lo=2, c=CH)

        def bdk(s):
            return BDk[s][:, :].rearrange("p (m gp r) -> p m gp r", gp=2, r=64)

        bdq = BDq[:, :].rearrange("p (f g j r) -> p f g j r", f=2, g=4, j=4)

        def chunk_cols(t, j):
            return t[:, :].rearrange("p (gh j e) -> p gh j e", gh=2, e=DH)[:, :, j, :]

        bdkr = BDkR[:, :].rearrange("p (gh r) -> p gh r", gh=2)

        FILL, DRAIN = 4, 4

        def timeline(body, prologue, eng):
            prologue()
            for t in range(FILL):
                body(t, t % 2, t // 2)
            with eng.Fori(0, (NT - 2 - FILL) // 2) as i:
                for s in range(2):
                    body(2 * i + (FILL + s), s, i + FILL // 2)
            for t in range(NT - 2, NT + DRAIN):
                body(t, t % 2, t // 2)

        def live(t):
            if not isinstance(t, int):
                return True, True, True, True, True
            return t + 2 < NT, t + 1 < NT, t < NT, 0 <= t - 1 < NT, 0 <= t - 2 < NT

        def rounds(t, s, h):
            plan = [(h - 2, 5), (h - 1, 0), (h - 1, 1)] if s else [(h - 2, 2), (h - 2, 3), (h - 2, 4)]
            return {n: p for n, p in enumerate(plan) if is_pair(p[0])}

        def low(p, r):
            if r % 3 == 2:
                return low_v.sem, low_v.at("fl", 2 * p + r // 3)
            return low_g.sem, low_g.at("fl", 4 * p + (r // 3 * 2 + r % 3))

        def is_pair(p):
            return not isinstance(p, int) or 0 <= p < NT // 2

        atb = ATB[:, :].rearrange("p (gh r) -> p gh r", gh=2)

        UNITS = 3 * MI

        def units(t, j):
            c = NC * t + j if isinstance(t, int) else -1
            return [u for u in range(c * 3 // 2, (c + 1) * 3 // 2) if u < UNITS] if c >= 0 else []

        def last_units(t, j):
            return units(t, j - 1) if j else units(t - 1, NC - 1) if isinstance(t, int) and t else []

        block = ctx.enter_context(nc.Block())

        @block.sync
        def _(sp):
            def stage(u):
                src = (gate_w, up_w, down_w)[u % 3]
                sp.dma_start(wst[u % 3][:, :], src[:, u // 3 * D:(u // 3 + 1) * D]).then_inc(s_stage[u % 3], 16)

            sp.dma_start(xt[:, :], x_t[0]).then_inc(s_x, 16)
            sp.dma_start(cst[:, :], consts).then_inc(s_const, 16)
            sp.dma_start(Wq[:, :].rearrange("p (k n) -> p k n", k=KD),
                         wq.rearrange("(k p) n -> p k n", p=P)).then_inc(s_wq, 16)
            for dst, src in ((Wg1, wg1), (Wb, wbeta)):
                sp.dma_start(dst[:, :].rearrange("p (k n) -> p k n", k=KD),
                             src.rearrange("(k p) n -> p k n", p=P)).then_inc(s_small, 16)
            for dst, src, s in ((Wk, wk, s_wk), (Wv, wv, s_wv)):
                sp.dma_start(dst[:, :].rearrange("p (k n) -> p k n", k=KD),
                             src.rearrange("(k p) n -> p k n", p=P)).then_inc(s, 16)
            for dst, src in ((Wg2, wg2), (nw, norm_w), (gs, gate_s), (us, up_s), (wR, ln_w), (bR, ln_b),
                             (wF, ln_wf), (bF, ln_bf)):
                sp.dma_start(dst[:, :], src).then_inc(s_small, 16)
            sp.dma_start(ds[:, :], down_s.partition_broadcast(P)).then_inc(s_small, 16)
            sp.wait_ge(norm_a.sem, norm_a.at("xn", 0))
            sp.dma_start(xt[:, :], x_t[1]).then_inc(s_x, 16)
            sp.dma_start(Wo[:, :].rearrange("p (k n) -> p k n", k=KD),
                         wo.rearrange("(k p) n -> p k n", p=P)).then_inc(s_wo, 16)
            for u in range(3):
                stage(u)

            def body(t, s, h):
                norm, prep, scan, post, tail = live(t)
                if norm:
                    sp.wait_ge(norm_a.sem, norm_a.at("xn", t + 1))
                    sp.dma_start(xt[:, :], x_t[t + 2]).then_inc(s_x, 16)
                if tail:
                    if begun(h - 2):
                        sp.wait_ge(pair_a.sem, pair_a.at("x1h", h - 2))
                    sp.dma_start(x1[s][:, :], x_t[t - 2]).then_inc(s_xr[s], 16)
                for j in range(NC):
                    for u in last_units(t, j):
                        if u + 3 < UNITS:
                            sp.wait_ge(s_quant, u + 1)
                            stage(u + 3)
                if s and is_pair(h - 2):
                    for k in range(2):
                        sp.wait_ge(fin_v.sem, fin_v.at("out", 2 * (h - 2) + k))
                        sp.dma_start(out_t[t - 5 + k], x1h[k][:, :]).then_inc(s_out, 16)

            timeline(body, lambda: None, sp)
            sp.wait_ge(s_out, 16 * NT)

        @block.tensor
        def _(pe):
            mm = nc.tensor.matmul

            def proj(dst, W, n, blocks=range(KD)):
                for k in blocks:
                    ins = mm(dst, xnT[:, k * P:(k + 1) * P], W[:, k * n:(k + 1) * n], start=(k == 0), stop=(k == KD - 1))
                return ins

            def turn(dst, src, one):
                for g in range(4):
                    ins = nc.tensor.transpose(dst[:, g * P:(g + 1) * P], src[:, g * P:(g + 1) * P], ident)
                ins.then_inc(*one)

            def turn_g(dst, src, one):
                for g in range(4):
                    for lo in range(2):
                        m = (2 * lo + g % 2) * P + g // 2 * 64
                        if lo == 0:
                            nc.tensor.transpose(dst[0:64, g * P:(g + 1) * P], src[:, m:m + 64], ident)
                        else:
                            ins = mm(dst[64:P, g * P:(g + 1) * P], src[:, m:m + 64], ident, start=True, stop=True)
                ins.then_inc(*one)

            def prep_xnT(t):
                pe.wait_ge(norm_a.sem, norm_a.at("xn", t))
                if begun(t - 1):
                    pe.wait_ge(prep_v.sem, prep_v.at("em", t - 1))
                turn(PA[0], xn, prep_t.one("xnT"))

            def prep_q(t):
                pe.wait_ge(prep_a.sem, prep_a.at("xnT", t))
                proj(PA[0][:, :], Wq, D).then_inc(*prep_t.one("q"))

            def prep_beta(t):
                pe.wait_ge(prep_a.sem, prep_a.at("BDk", t))
                for k in range(KD):
                    ins = mm(PA[0][0:DG, 0:P], Wg1[:, k * DG:(k + 1) * DG], xnT[:, k * P:(k + 1) * P],
                             start=(k == 0), stop=(k == KD - 1))
                ins.then_inc(*prep_t.one("g1"))
                proj(PA[0][:, P:P + H], Wb, H).then_inc(*prep_t.one("beta"))

            def prep_k(t):
                pe.wait_ge(prep_a.sem, prep_a.at("q", t))
                if begun(t - 3):
                    pe.wait_ge(tail_v.sem, tail_v.at("x1", t - 3))
                proj(PA[0][:, :], Wk, D).then_inc(*prep_t.one("k"))

            def prep_qT1(t):
                turn_g(PA[1], qtok, prep_t.one("qT1"))

            def prep_qT2(t):
                pe.wait_ge(prep_a.sem, prep_a.at("qT", t))
                turn(PA[1], qtok, prep_t.one("qT2"))

            def prep_vv(t):
                pe.wait_ge(prep_v.sem, prep_v.at("qR", t))
                proj(PA[1][:, :], Wv, D).then_inc(*prep_t.one("v"))

            def prep_kT(t):
                pe.wait_ge(prep_v.sem, prep_v.at("d", t))
                turn(PA[1], kn, prep_t.one("kT2"))
                turn_g(PA[0], kn, prep_t.one("kT1"))

            def prep_dT(t):
                pe.wait_ge(prep_a.sem, prep_a.at("beta", t))
                turn(PA[0], dv, prep_t.one("dT"))

            def prep_gate(t):
                pe.wait_ge(prep_v.sem, prep_v.at("kR", t))
                for m in range(4):
                    ins = mm(PA[1][:, m * P:(m + 1) * P], Wg2[:, m * P:(m + 1) * P], g1T[:, :], start=True, stop=True)
                ins.then_inc(*prep_t.one("gate"))

            def prep_cen(t):
                pe.wait_ge(prep_a.sem, prep_a.at("rT", t))
                mm(PA[0][:, :], cst[:, C_CEN:C_CEN + P], rT[:, :], start=True, stop=True).then_inc(*prep_t.one("cen"))

            def prep_brow(t):
                pe.wait_ge(prep_v.sem, prep_v.at("rR", t))
                mm(PA[0][:, 0:P], cst[:, C_REP:C_REP + P], bx[:, :], start=True, stop=True).then_inc(*prep_t.one("brow"))

            def read_state(n, j, s):
                c = NC * n + j
                if j == 0:
                    pe.wait_ge(prep_a.sem, prep_a.at("BDk", n))
                pe.wait_ge(chunk_a.sem, chunk_a.at("q", c))
                if begun(c - 1):
                    pe.wait_ge(scan_v.sem, scan_v.at("S", c - 1))
                for gh in range(2):
                    for gp in range(2):
                        ins = mm(KAv[gp * 64:(gp + 1) * 64, gh, :], bdk(s)[:, gh * NC + j, gp, :],
                                 SQv[:, 2 * gh + gp, :], start=True, stop=True, skip_group_check=True)
                ins.then_inc(*scan_t.one("kh"))
                if j % 4 == 0:
                    pe.wait_ge(diag_a.sem, diag_a.at(f"q{j // 4}", n))
                if begun(c - 1):
                    pe.wait_ge(scan_a.sem, scan_a.at("qh", c - 1))
                for gh in range(2):
                    for gp in range(2):
                        ins = mm(QH[gp * 64:(gp + 1) * 64, gh * DH:(gh + 1) * DH], bdq[:, j // 4, 2 * gp + gh, j % 4, :],
                                 S[:, 2 * gh + gp, :], start=(gh == 0), stop=False, skip_group_check=True)
                ins.then_inc(*scan_t.one("qs"))

            def write_state(n, j):
                c = NC * n + j
                pe.wait_ge(chunk_g.sem, chunk_g.at("at", c))
                pe.wait_ge(scan_v.sem, scan_v.at("vx", c))
                mm(dS[:, 0:64], bdkr[:, 0, :], VX[:, 0:64], start=True, stop=True)
                pe.wait_ge(scan_v.sem, scan_v.at("ve", c))
                ins = mm(dS[:, 64:128], bdkr[:, 1, :], VX[:, 64:128], start=True, stop=True)
                ins.then_inc(*scan_t.one("upd"))
                for gh in range(2):
                    for gp in range(2):
                        p = slice(gp * 64, (gp + 1) * 64)
                        ins = mm(QH[p, gh * DH:(gh + 1) * DH], atb[p, gh, :], VE[p, gh * DH:(gh + 1) * DH],
                                 start=False, stop=True, skip_group_check=True)
                ins.then_inc(*scan_t.one("qa"))

            def post_wo(n):
                pe.wait_ge(post_v.sem, post_v.at("ogT", n))
                if not isinstance(n, int) or n + 2 < NT:
                    pe.wait_ge(prep_a.sem, prep_a.at("th", n + 2))
                else:
                    if begun(n - 1):
                        pe.wait_ge(tail_v.sem, tail_v.at("x1", n - 1))
                for g in range(4):
                    ins = mm(PA[1][:, :], ogT[:, g * P:(g + 1) * P], Wo[:, g * D:(g + 1) * D], start=(g == 0), stop=(g == 3))
                ins.then_inc(*tail_t.one("wo"))

            def pair_xT(p):
                pe.wait_ge(tail_a.sem, tail_a.at("xf", 2 * p + 1))
                if begun(NR * p - 1):
                    pe.wait_ge(ffn_a.sem, ffn_a.at("silu", NR * p - 1))
                turn(G, xn2[0], pair_t.one("xT0"))
                if begun(NR * p - 1):
                    pe.wait_ge(ffn_v.sem, ffn_v.at("f", NR * p - 1))
                turn(U4, xn2[1], pair_t.one("xT1"))

            def ffn_up(W, b, p, r, one):
                for q in range(RM):
                    m = RM * r + q
                    for part in (xh, xl):
                        for k in range(KD):
                            ins = mm(b[:, q * PAIR:(q + 1) * PAIR], W[:, k * I + m * P:k * I + (m + 1) * P],
                                     part[:, k * PAIR:(k + 1) * PAIR], start=(part is xh and k == 0),
                                     stop=(part is xl and k == KD - 1))
                ins.then_inc(*one)

            def ffn_g(p, r):
                if r == 0:
                    if isinstance(p, int) and p == 0:
                        pe.wait_ge(s_quant, UNITS)
                    pe.wait_ge(pair_v.sem, pair_v.at("xl", p))
                if begun(NR * p + (r - 1)):
                    pe.wait_ge(ffn_a.sem, ffn_a.at("silu", NR * p + (r - 1)))
                ffn_up(GW, G, p, r, ffn_t.one("g"))

            def ffn_u(p, r):
                if begun(NR * p + (r - 1)):
                    pe.wait_ge(ffn_v.sem, ffn_v.at("f", NR * p + (r - 1)))
                ffn_up(UW, U4, p, r, ffn_t.one("u"))

            def ffn_down(p, r):
                pe.wait_ge(*low(p, r))
                if r == 0:
                    if begun(2 * p - 1):
                        pe.wait_ge(fin_v.sem, fin_v.at("y", 2 * p - 1))
                for k in range(2):
                    for q in range(RM):
                        m = RM * r + q
                        for part in (fh, fl):
                            ins = mm(Y[k][:, :], part[:, q * PAIR + k * P:q * PAIR + (k + 1) * P], DW[:, m * D:(m + 1) * D],
                                     start=(m == 0 and part is fh), stop=(m == MI - 1 and part is fl))
                ins.then_inc(*down_t.one("dn"))

            def body(t, s, h):
                norm, prep, scan, post, tail = live(t)
                o = 1 - s
                ffn = rounds(t, s, h)
                for j in range(NC):
                    if scan:
                        read_state(t, j, s)
                    if j == 0:
                        if prep:
                            prep_xnT(t + 1)
                        if 0 in ffn:
                            ffn_g(*ffn[0])
                            ffn_u(*ffn[0])
                    if j == 1 and prep:
                        prep_q(t + 1)
                    if j == 2 and prep:
                        prep_k(t + 1)
                    if j == 3:
                        if prep:
                            prep_qT1(t + 1)
                        if 1 in ffn:
                            ffn_g(*ffn[1])
                            ffn_u(*ffn[1])
                    if j == 4 and prep:
                        prep_vv(t + 1)
                    if j == 5:
                        if prep:
                            prep_kT(t + 1)
                        if 2 in ffn:
                            ffn_g(*ffn[2])
                    if j == 6:
                        if prep:
                            prep_dT(t + 1)
                            prep_gate(t + 1)
                        if 2 in ffn:
                            ffn_u(*ffn[2])
                    if j == 7 and post:
                        post_wo(t - 1)
                    if scan:
                        write_state(t, j)
                    if j == 1:
                        if 0 in ffn:
                            ffn_down(*ffn[0])
                        if s and is_pair(h - 1):
                            pair_xT(h - 1)
                    if j == 3 and prep:
                        prep_qT2(t + 1)
                    if j == 4 and 1 in ffn:
                        ffn_down(*ffn[1])
                    if j == 5 and prep:
                        prep_beta(t + 1)
                    if j == 6 and prep:
                        prep_cen(t + 1)
                    if j == 7:
                        if prep:
                            prep_brow(t + 1)
                        if 2 in ffn:
                            ffn_down(*ffn[2])

            def prologue():
                pe.wait_ge(s_const, 16)
                prep_xnT(0)
                pe.wait_ge(s_wq, 16)
                prep_q(0)
                pe.wait_ge(s_small, 16 * 11)
                pe.wait_ge(s_wk, 16)
                prep_k(0)
                prep_qT1(0)
                prep_qT2(0)
                pe.wait_ge(s_wv, 16)
                prep_vv(0)
                prep_kT(0)
                prep_beta(0)
                prep_dT(0)
                prep_gate(0)
                prep_cen(0)
                prep_brow(0)
                pe.wait_ge(s_setup, 4)

            timeline(body, prologue, pe)

        @block.scalar
        def _(act):
            fn = nc.scalar.activation

            def copy(dst, src, one):
                fn(dst, src, ACT.Copy).then_inc(*one)

            def prep_xnT(t):
                act.wait_ge(prep_t.sem, prep_t.at("xnT", t))
                if begun(t - 1):
                    act.wait_ge(prep_t.sem, prep_t.at("beta", t - 1))
                copy(xnT[:, :], PA[0][:, :], prep_a.one("xnT"))

            def prep_q(t):
                act.wait_ge(prep_t.sem, prep_t.at("q", t))
                if begun(t - 1):
                    act.wait_ge(prep_v.sem, prep_v.at("thR", t - 1))
                fn(qtok[:, :], PA[0][:, :], ACT.Silu).then_inc(*prep_a.one("q"))

            def prep_g1(t):
                act.wait_ge(prep_t.sem, prep_t.at("beta", t))
                if begun(t - 1):
                    act.wait_ge(prep_t.sem, prep_t.at("gate", t - 1))
                copy(g1T[:, :], PA[0][0:DG, 0:P], prep_a.one("g1"))
                if begun(t - 1):
                    act.wait_ge(prep_v.sem, prep_v.at("bx", t - 1))
                fn(bt[:, :], PA[0][:, P:P + H], ACT.Tanh, scale=0.5).then_inc(*prep_a.one("beta"))

            def prep_ksq(t):
                act.wait_ge(prep_t.sem, prep_t.at("k", t))
                if begun(t - 1):
                    act.wait_ge(prep_v.sem, prep_v.at("rR", t - 1))
                fn(dv[:, :], PA[0][:, :], ACT.Square).then_inc(*prep_a.one("ksq"))

            def prep_qT(t, s):
                act.wait_ge(prep_t.sem, prep_t.at("qT1", t))
                copy(qT[s][:, :], PA[1][:, :], prep_a.one("qT"))

            def own(h):
                return slice(CH * (h % 2 * 2 + h // 2), CH * (h % 2 * 2 + h // 2 + 1))

            def prep_BDk(t, s):
                act.wait_ge(prep_t.sem, prep_t.at("kT1", t))
                if begun(NC * (t - 1) - 1):
                    act.wait_ge(scan_t.sem, scan_t.at("kh", NC * (t - 1) - 1))
                for h in range(4):
                    q = slice(32 * h, 32 * h + 32)
                    ins = fn(bdk(s)[q, :, :, own(h)].rearrange("p m gp c -> p gp m c"),
                             PA[0][q, :].rearrange("p (gp m c) -> p gp m c", gp=2, c=CH), ACT.Copy)
                ins.then_inc(*prep_a.one("BDk"))

            def prep_rT(t):
                act.wait_ge(prep_t.sem, prep_t.at("dT", t))
                for m in range(4):
                    ins = fn(rT[:, m * P:(m + 1) * P], PA[0][:, m * P:(m + 1) * P], ACT.Identity,
                             scale=wF[:, m:m + 1], bias=wbF[:, m:m + 1])
                ins.then_inc(*prep_a.one("rT"))

            def prep_th(t):
                act.wait_ge(prep_t.sem, prep_t.at("gate", t))
                fn(thT[:, :], PA[1][:, :], ACT.Tanh, scale=0.5).then_inc(*prep_a.one("th"))

            def diag_q(n, half, s):
                act.wait_ge(prep_a.sem, prep_a.at("qT", n))
                if begun(NC * (n - 1) + 4 * half + 3):
                    act.wait_ge(scan_t.sem, scan_t.at("qs", NC * (n - 1) + 4 * half + 3))
                for h in range(4):
                    q = slice(32 * h, 32 * h + 32)
                    ins = fn(bdq[q, half, :, :, own(h)],
                             qT[s][q, :].rearrange("p (g f j c) -> p f g j c", g=4, f=2, j=4)[:, half], ACT.Copy)
                ins.then_inc(*diag_a.one(f"q{half}"))

            def chunk_q(n, j, s):
                if j == 0:
                    act.wait_ge(prep_a.sem, prep_a.at("qT", n))
                fn(SQ[:, :].rearrange("p (gh gp e) -> p gh gp e", gh=2, gp=2)[:, :, :, DH:48],
                   qT[s][:, :].rearrange("p (gp gh j c) -> p j gh gp c", gp=2, gh=2, c=CH)[:, j], ACT.Copy)\
                    .then_inc(*chunk_a.one("q"))

            def take_qh(n, j, s):
                act.wait_ge(scan_t.sem, scan_t.at("qa", NC * n + j))
                if j == 0:
                    if begun(n - 2):
                        act.wait_ge(post_v.sem, post_v.at("n", n - 2))
                fn(chunk_cols(qhR[s], j), QH[:, 0:64].rearrange("p (gh e) -> p gh e", gh=2), ACT.Copy)\
                    .then_inc(*scan_a.one("qh"))

            def post_qsq(n, s):
                act.wait_ge(scan_a.sem, scan_a.at("qh", NC * n + NC - 1))
                if begun(n - 1):
                    act.wait_ge(tail_t.sem, tail_t.at("wo", n - 1))
                fn(o1[:, :], qhR[s][:, :], ACT.Square).then_inc(*post_a.one("qsq"))

            def post_osq(n):
                act.wait_ge(post_v.sem, post_v.at("og", n))
                fn(o1[:, :], o2[:, :], ACT.Square).then_inc(*post_a.one("osq"))

            def tail_xc(n, s, p):
                act.wait_ge(s_xr[s], 16 * p + 16)
                act.wait_ge(tail_g.sem, tail_g.at("nba", n))
                fn(x1[s][:, :], x1[s][:, :], ACT.Identity, bias=nb["a"][:, 0:1]).then_inc(*tail_a.one("xc"))

            def tail_xf(n, s, p):
                act.wait_ge(tail_g.sem, tail_g.at("nbf", n))
                if begun(p - 1):
                    act.wait_ge(pair_t.sem, pair_t.at(f"xT{s}", p - 1))
                elif s:
                    act.wait_ge(s_quant, UNITS)
                fn(xn2[s][:, :], x1[s][:, :], ACT.Identity, scale=rs["f"][:, 0:1], bias=nb["f"][:, 0:1])\
                    .then_inc(*tail_a.one("xf"))

            def fin_yc(n, k):
                act.wait_ge(fin_g.sem, fin_g.at("nby", n))
                fn(x1h[k][:, :], x1h[k][:, :], ACT.Identity, bias=nb["y"][:, 0:1]).then_inc(*fin_a.one("yc"))

            def x_norm(t):
                act.wait_ge(norm_g.sem, norm_g.at("nb", t))
                if begun(t - 1):
                    act.wait_ge(prep_t.sem, prep_t.at("cen", t - 1))
                fn(xn[:, :], xt[:, :], ACT.Identity, scale=rs["p"][:, 0:1], bias=nb["p"][:, 0:1])\
                    .then_inc(*norm_a.one("xn"))

            def pair_xh(p):
                if begun(NR * p - 1):
                    act.wait_ge(ffn_t.sem, ffn_t.at("u", NR * p - 1))
                for k, b in enumerate((G, U4)):
                    act.wait_ge(pair_t.sem, pair_t.at(f"xT{k}", p))
                    ins = fn(xh[:, :].rearrange("p (k n) -> p k n", k=KD)[:, :, k * P:(k + 1) * P],
                             b[:, :].rearrange("p (k n) -> p k n", k=KD), ACT.Copy)
                ins.then_inc(*pair_a.one("xh"))

            def pair_x1h(p):
                act.wait_ge(tail_v.sem, tail_v.at("x1", 2 * p + 1))
                if not isinstance(p, int) or p > 0:
                    act.wait_ge(s_out, 32 * p)
                for k in range(2):
                    ins = fn(x1h[k][:, :], x1[k][:, :], ACT.Copy)
                ins.then_inc(*pair_a.one("x1h"))

            def ffn_silu(p, r):
                c = NR * p + r
                act.wait_ge(ffn_t.sem, ffn_t.at("g", c))
                last = (p, r - 1) if r else (p - 1, NR - 1)
                if begun(last[0]):
                    act.wait_ge(*low(*last))
                for q in range(RM):
                    ins = fn(f[:, q * PAIR:(q + 1) * PAIR], G[:, q * PAIR:(q + 1) * PAIR], ACT.Silu,
                             scale=gs[:, RM * r + q:RM * r + q + 1])
                ins.then_inc(*ffn_a.one("silu"))

            def ffn_fh(p, r):
                c = NR * p + r
                act.wait_ge(ffn_v.sem, ffn_v.at("f", c))
                if begun(c - 1):
                    act.wait_ge(down_t.sem, down_t.at("dn", c - 1))
                copy(fh[:, :], f[:, :], ffn_a.one("fh"))

            def body(t, s, h):
                norm, prep, scan, post, tail = live(t)
                o = 1 - s
                fin = s and is_pair(h - 2)
                ffn = rounds(t, s, h)
                for j in range(NC):
                    if scan and (prep or j + 1 < NC):
                        act.wait_ge(scan_t.sem, scan_t.at("kh", NC * t + j))
                        if j + 1 < NC:
                            chunk_q(t, j + 1, s)
                        else:
                            chunk_q(t + 1, 0, o)
                    if j == 0:
                        if prep:
                            prep_xnT(t + 1)
                        if post:
                            post_qsq(t - 1, o)
                        if 0 in ffn:
                            ffn_silu(*ffn[0])
                        if tail:
                            tail_xc(t - 2, s, h - 1)
                    if j == 1:
                        if tail:
                            tail_xf(t - 2, s, h - 1)
                        if prep:
                            prep_q(t + 1)
                        if scan:
                            diag_q(t, 1, s)
                    if j == 2:
                        if s and is_pair(h - 1):
                            pair_xh(h - 1)
                        if prep:
                            prep_ksq(t + 1)
                    if j == 3:
                        if prep:
                            prep_qT(t + 1, o)
                        if 1 in ffn:
                            ffn_silu(*ffn[1])
                        if fin:
                            fin_yc(2 * (h - 2), 0)
                    if j == 4:
                        if 1 in ffn:
                            ffn_fh(*ffn[1])
                        if post:
                            post_osq(t - 1)
                        if prep:
                            diag_q(t + 1, 0, o)
                    if j == 5:
                        if prep:
                            prep_BDk(t + 1, o)
                        if 2 in ffn:
                            ffn_silu(*ffn[2])
                    if j == 6:
                        if prep:
                            prep_rT(t + 1)
                            prep_th(t + 1)
                        if fin:
                            fin_yc(2 * (h - 2) + 1, 1)
                    if j == 7 and norm:
                        x_norm(t + 2)
                    if scan:
                        take_qh(t, j, s)
                    if j == 0 and 0 in ffn:
                        ffn_fh(*ffn[0])
                    if j == 5 and prep:
                        prep_g1(t + 1)
                    if j == 6 and 2 in ffn:
                        ffn_fh(*ffn[2])
                    if j == 7 and s and is_pair(h - 1):
                        pair_x1h(h - 1)

            def prologue():
                x_norm(0)
                prep_xnT(0)
                prep_q(0)
                prep_ksq(0)
                prep_qT(0, 0)
                chunk_q(0, 0, 0)
                act.wait_ge(s_zero, 3)
                diag_q(0, 0, 0)
                prep_BDk(0, 0)
                prep_g1(0)
                act.wait_ge(s_setup, 1)
                prep_rT(0)
                prep_th(0)
                x_norm(1)

            timeline(body, prologue, act)

        @block.gpsimd
        def _(pool):
            tt = nc.gpsimd.tensor_tensor

            def power(dst, src, n, one):
                tt(dst, src, cst[:, C_NH:C_NH + n], ALU.pow).then_inc(*one)

            def scale_bias(k, steps, n, rs_name, nb_name):
                power(rs[k][:, :], ve[k][:, :], 1, steps.one(rs_name))
                pool.wait_ge(steps.sem, steps.at(rs_name, n))
                tt(nb[k][:, :], nm[k][:, :], rs[k][:, :], ALU.mult).then_inc(*steps.one(nb_name))

            def norm_rs(t):
                pool.wait_ge(norm_v.sem, norm_v.at("veps", t))
                scale_bias("p", norm_g, t, "rs", "nb")

            def ffn_fl(p, r):
                pool.wait_ge(ffn_a.sem, ffn_a.at("fh", NR * p + r))
                tt(fl[:, :], f[:, :], fh[:, :].bitcast(F32), ALU.subtract).then_inc(*low_g.one("fl"))

            def prep_rk(t):
                pool.wait_ge(prep_v.sem, prep_v.at("kse", t))
                power(rk[:, :], kss[:, :], H, prep_g.one("rk"))

            def prep_qb(t, s):
                pool.wait_ge(prep_v.sem, prep_v.at("qR", t))
                m = qR[s][:, :].rearrange("p (gh j e) -> p gh j e", gh=2, e=DH)
                tt(m, m, bR[:, :].rearrange("p (gh e) -> p gh e", gh=2).unsqueeze(2).broadcast_to([P, 2, NC, DH]),
                   ALU.add).then_inc(*prep_g.one("qb"))

            def prep_b1(t):
                pool.wait_ge(prep_a.sem, prep_a.at("beta", t))
                tt(bt[:, :], bt[:, :], cst[:, C_ONE:C_ONE + H], ALU.add).then_inc(*prep_g.one("b1"))

            def chunk_kR(n, j, s):
                c = NC * n + j
                if j == 0:
                    pool.wait_ge(prep_v.sem, prep_v.at("kR", n))
                if begun(c - 1):
                    pool.wait_ge(scan_t.sem, scan_t.at("upd", c - 1))
                for gh in range(2):
                    k = rows(kR[s])[:, gh * NC + j, :]
                    ins = tt(bdkr[:, gh, :].rearrange("p (h d) -> p h d", h=4),
                             k.unsqueeze(1).broadcast_to([P, 4, DH]),
                             wide(cst[:, C_HM:C_HM + 4]), ALU.mult)
                ins.then_inc(*chunk_g.one("kR"))

            def scan_rho(n, j, s):
                c = NC * n + j
                pool.wait_ge(scan_v.sem, scan_v.at("ss", c))
                if begun(c - 1):
                    pool.wait_ge(scan_v.sem, scan_v.at("ve", c - 1))
                power(rho[:, :], ss[:, :], 2, scan_g.one("rho"))
                if j == 0:
                    pool.wait_ge(prep_v.sem, prep_v.at("eM", n))
                pool.wait_ge(scan_g.sem, scan_g.at("rho", c))
                m = etaR[:, s * 16:s * 16 + 16].rearrange("p (gh j) -> p gh j", gh=2)[:, :, j]
                tt(rec[:, :], rho[:, :], m, ALU.mult).then_inc(*scan_g.one("rec"))
                m = etaM[:, s * 32:s * 32 + 32].rearrange("p (gh j gp) -> p gh j gp", gh=2, gp=2)[:, :, j, :]
                tt(re[:, :].rearrange("p (gh gp) -> p gh gp", gh=2), wide(rho[:, :], 2), m, ALU.mult).then_inc(*scan_g.one("re"))

            def chunk_at(n, j):
                c = NC * n + j
                pool.wait_ge(scan_v.sem, scan_v.at("y", c))
                tt(atb.rearrange("p gh (h c) -> p gh h c", c=CH),
                   kq.unsqueeze(2).broadcast_to([P, 2, 4, CH]),
                   cst[:, C_TRI:C_TRI + 64].rearrange("p (h c) -> p h c", c=CH).unsqueeze(1)
                   .broadcast_to([P, 2, 4, CH]), ALU.mult).then_inc(*chunk_g.one("at"))

            def post_rq(n):
                pool.wait_ge(post_v.sem, post_v.at("qse", n))
                power(rq[:, :], qss[:, :], H, post_g.one("rq"))

            def post_nw(n):
                pool.wait_ge(post_v.sem, post_v.at("n", n))
                m = o2[:, :].rearrange("p (gh j e) -> p gh j e", gh=2, e=DH)
                tt(m, m, wK[:, :].rearrange("p (gh e) -> p gh e", gh=2).unsqueeze(2).broadcast_to([P, 2, NC, DH]),
                   ALU.mult).then_inc(*post_g.one("nw"))

            def post_o(n, s):
                pool.wait_ge(post_g.sem, post_g.at("nw", n))
                pool.wait_ge(prep_g.sem, prep_g.at("qb", n))
                tt(o2[:, :], o2[:, :], qR[s][:, :], ALU.add).then_inc(*post_g.one("o"))

            def post_ro(n):
                pool.wait_ge(post_v.sem, post_v.at("ose", n))
                power(ro[:, :], oss[:, :], H, post_g.one("ro"))

            def tail_ra(n):
                pool.wait_ge(tail_v.sem, tail_v.at("ave", n))
                scale_bias("a", tail_g, n, "ra", "nba")

            def tail_rf(n):
                pool.wait_ge(tail_v.sem, tail_v.at("fve", n))
                scale_bias("f", tail_g, n, "rf", "nbf")

            def fin_ry(n):
                pool.wait_ge(fin_v.sem, fin_v.at("yve", n))
                scale_bias("y", fin_g, n, "ry", "nby")

            def body(t, s, h):
                norm, prep, scan, post, tail = live(t)
                o = 1 - s
                fin = s and is_pair(h - 2)
                ffn = rounds(t, s, h)
                for j in range(NC):
                    if scan:
                        scan_rho(t, j, s)
                        chunk_at(t, j)
                    if j == 0 and tail:
                        tail_ra(t - 2)
                    for u in last_units(t, j):
                        pool.wait_ge(s_magic, u + 1)
                        tt(wst[u % 3][:, :], wst[u % 3][:, :], wmg[u % 2][:, :], ALU.add).then_inc(s_shift, 1)
                    if j == 1:
                        if tail:
                            tail_rf(t - 2)
                        if post:
                            post_rq(t - 1)
                    if j == 2:
                        if post:
                            post_nw(t - 1)
                    if j == 3:
                        if fin:
                            fin_ry(2 * (h - 2))
                        if post:
                            post_o(t - 1, o)
                        if prep:
                            prep_rk(t + 1)
                    if j == 4 and 1 in ffn:
                        ffn_fl(*ffn[1])
                    if j == 7 and 2 in ffn:
                        ffn_fl(*ffn[2])
                    if j == 5 and post:
                        post_ro(t - 1)
                    if j == 6:
                        if fin:
                            fin_ry(2 * (h - 2) + 1)
                        if norm:
                            norm_rs(t + 2)
                        if prep:
                            prep_b1(t + 1)
                            prep_qb(t + 1, o)
                    if scan and j + 1 < NC:
                        chunk_kR(t, j + 1, s)
                    if prep and j + 1 == NC:
                        chunk_kR(t + 1, 0, o)

            def prologue():
                for b in (BDk[0], BDq, BDk[1]):
                    nc.gpsimd.memset(b[:, :], 0.0).then_inc(s_zero, 1)
                pool.wait_ge(s_const, 16)
                norm_rs(0)
                prep_rk(0)
                norm_rs(1)
                prep_b1(0)
                prep_qb(0, 0)
                chunk_kR(0, 0, 0)

            timeline(body, prologue, pool)

        @block.vector
        def _(dve):
            tt, ts, stt = nc.vector.tensor_tensor, nc.vector.tensor_scalar, nc.vector.scalar_tensor_tensor
            red = nc.vector.tensor_reduce

            def add_eps(dst, src, eps, one):
                ts(dst, src, eps, None, ALU.add).then_inc(*one)

            def norm_stats(src, k, steps, names, n):
                a, b, c, d = names
                nc.vector.bn_stats(st[k][:, :], src).then_inc(*steps.one(a))
                dve.wait_ge(steps.sem, steps.at(a, n))
                nc.vector.memset(pause[:, :], 0.0)
                nc.vector.bn_aggr(mv[k][:, :], st[k][:, :]).then_inc(*steps.one(b))
                dve.wait_ge(steps.sem, steps.at(b, n))
                ts(nm[k][:, :], mv[k][:, 0:1], -1.0, None, ALU.mult).then_inc(*steps.one(c))
                add_eps(ve[k][:, :], mv[k][:, 1:2], EPS_LN, steps.one(d))

            def x_stats(t):
                dve.wait_ge(s_x, 16 * t + 16)
                norm_stats(xt[:, :], "p", norm_v, ("stats", "mv", "nm", "veps"), t)

            def prep_kss(t):
                dve.wait_ge(prep_a.sem, prep_a.at("ksq", t))
                red(kss[:, :], heads(dv), AX_X, ALU.add).then_inc(*prep_v.one("kss"))
                dve.wait_ge(prep_v.sem, prep_v.at("kss", t))
                add_eps(kss[:, :], kss[:, :], EPS, prep_v.one("kse"))

            def prep_bx(t):
                dve.wait_ge(prep_g.sem, prep_g.at("b1", t))
                if begun(t - 1):
                    dve.wait_ge(prep_t.sem, prep_t.at("brow", t - 1))
                for gh in range(2):
                    e = bt[:, :].rearrange("p (gp gh h) -> p gh gp h", gp=2, gh=2)[:, gh]
                    ins = tt(bx[:, gh * 64:(gh + 1) * 64].rearrange("p (j gp h) -> p j gp h", j=NC, gp=2),
                             e.unsqueeze(1).broadcast_to([P, NC, 2, 4]),
                             cst[:, C_CHM:C_CHM + 64].rearrange("p (j gp h) -> p j gp h", j=NC, gp=2), ALU.mult)
                ins.then_inc(*prep_v.one("bx"))

            def turn(dst, src, one):
                nc.vector.transpose(rows(dst), feat(src)).then_inc(*one)

            def prep_qR(t, s):
                dve.wait_ge(prep_t.sem, prep_t.at("qT2", t))
                if begun(t - 2):
                    dve.wait_ge(post_g.sem, post_g.at("o", t - 2))
                turn(qR[s], PA[1], prep_v.one("qR"))

            def prep_kn(t):
                dve.wait_ge(prep_g.sem, prep_g.at("rk", t))
                dve.wait_ge(prep_t.sem, prep_t.at("qT2", t))
                tt(heads(kn), heads(PA[0]), wide(rk[:, :]), ALU.mult).then_inc(*prep_v.one("kn"))

            def prep_d(t):
                dve.wait_ge(prep_v.sem, prep_v.at("kn", t))
                dve.wait_ge(prep_t.sem, prep_t.at("v", t))
                tt(dv[:, :], kn[:, :], PA[1][:, :], ALU.subtract).then_inc(*prep_v.one("d"))

            def prep_kR(t, s):
                dve.wait_ge(prep_t.sem, prep_t.at("kT2", t))
                turn(kR[s], PA[1], prep_v.one("kR"))

            def prep_rR(t, s):
                dve.wait_ge(prep_t.sem, prep_t.at("cen", t))
                turn(rR[s], PA[0], prep_v.one("rR"))

            def prep_thR(t, s):
                dve.wait_ge(prep_a.sem, prep_a.at("th", t))
                turn(thR[s], thT, prep_v.one("thR"))

            def prep_eta(t, s):
                dve.wait_ge(prep_t.sem, prep_t.at("brow", t))
                tt(em.rearrange("p (m h) -> p m h", h=8), PA[0][:, 0:P].rearrange("p (m h) -> p m h", h=8),
                   cst[:, C_ROW:C_ROW + 8].unsqueeze(1).broadcast_to([P, 16, 8]), ALU.mult).then_inc(*prep_v.one("em"))
                dve.wait_ge(prep_v.sem, prep_v.at("em", t))
                red(etaR[:, s * 16:(s + 1) * 16], em.rearrange("p (m h) -> p m h", h=8), AX_X, ALU.add)\
                    .then_inc(*prep_v.one("er"))
                dve.wait_ge(prep_v.sem, prep_v.at("er", t))
                tt(etaM[:, s * 32:(s + 1) * 32].rearrange("p (m gp) -> p m gp", gp=2),
                   wide(etaR[:, s * 16:(s + 1) * 16], 2),
                   cst[:, C_GPM:C_GPM + 2].unsqueeze(1).broadcast_to([P, 16, 2]), ALU.mult).then_inc(*prep_v.one("eM"))

            def g2(t, w=DH):
                return t.rearrange("p (gh e) -> p gh e", e=w)

            def scan_front(n, j, s):
                c = NC * n + j
                dve.wait_ge(scan_t.sem, scan_t.at("kh", c))
                nc.vector.tensor_copy(ka[:, :], KA).then_inc(*scan_v.one("y"))
                tt(g2(PR[:, 0:64]), g2(w2K[:, :]), KH, ALU.mult).then_inc(*scan_v.one("p"))
                dve.wait_ge(scan_v.sem, scan_v.at("y", c))
                tt(g2(ysq[:, :], 33)[:, :, 0:DH], y, y, ALU.mult).then_inc(*scan_v.one("ysq"))
                if j == 0:
                    dve.wait_ge(prep_v.sem, prep_v.at("rR", n))
                tt(g2(PR[:, 128:192]), chunk_cols(rR[s], j), y, ALU.mult).then_inc(*scan_v.one("ry"))
                dve.wait_ge(scan_v.sem, scan_v.at("ysq", c))
                red(ss[:, :], g2(ysq[:, :], 33), AX_X, ALU.add).then_inc(*scan_v.one("ss"))
                dve.wait_ge(scan_v.sem, scan_v.at("p", c))
                tt(g2(PR[:, 64:128]), g2(PR[:, 0:64]), y, ALU.mult).then_inc(*scan_v.one("py"))
                dve.wait_ge(scan_v.sem, scan_v.at("py", c))
                red(sums[:, 0:6], PR[:, :].rearrange("p (g e) -> p g e", e=DH), AX_X, ALU.add)\
                    .then_inc(*scan_v.one("sums"))
                dve.wait_ge(scan_v.sem, scan_v.at("sums", c))
                stt(out=g2(u[:, :]), in0=wide(sums[:, 0:2]), scalar=1.0 / DH, in1=g2(PR[:, 0:64]),
                    op0=ALU.mult, op1=ALU.subtract).then_inc(*scan_v.one("u"))
                tt(yy[:, :].rearrange("p (k gh e) -> p k gh e", k=2, gh=2),
                   sums[:, 2:6].rearrange("p (k gh) -> p k gh", k=2).unsqueeze(3).broadcast_to([P, 2, 2, DH]),
                   y.unsqueeze(1).broadcast_to([P, 2, 2, DH]), ALU.mult).then_inc(*scan_v.one("yy"))

            def scan_back(n, j, s):
                c = NC * n + j
                dve.wait_ge(scan_g.sem, scan_g.at("rho", c))
                r_j = chunk_cols(rR[s], j)
                for before, after, add, op in (("yy", "h", g2(yy[:, 64:128]), ALU.add), ("h", "g", g2(u[:, :]), ALU.add),
                                               ("g", "t", r_j, ALU.subtract)):
                    for gh in range(2):
                        dve.wait_ge(scan_v.sem, scan_v.at(before if before == "yy" else f"{before}{gh}", c))
                        e = slice(gh * DH, (gh + 1) * DH)
                        stt(out=yy[:, e], in0=yy[:, e], scalar=rho[:, gh:gh + 1], in1=add[:, gh, :],
                            op0=ALU.mult, op1=op).then_inc(*scan_v.one(f"{after}{gh}"))
                dve.wait_ge(scan_v.sem, scan_v.at("t1", c))
                dve.wait_ge(scan_g.sem, scan_g.at("re", c))
                tt(VX[:, :].rearrange("p (gh gp e) -> p gh gp e", gh=2, gp=2),
                   g2(yy[:, 0:64]).unsqueeze(2).broadcast_to([P, 2, 2, DH]),
                   g2(re[:, :], 2).unsqueeze(3).broadcast_to([P, 2, 2, DH]), ALU.mult).then_inc(*scan_v.one("vx"))
                tt(g2(VE[:, :]), g2(yy[:, 0:64]), wide(rec[:, :]), ALU.mult).then_inc(*scan_v.one("ve"))

            def scan_state(n, j):
                c = NC * n + j
                dve.wait_ge(scan_t.sem, scan_t.at("upd", c))
                tt(S, S, dS.rearrange("p (g e) -> p g e", e=DH), ALU.add).then_inc(*scan_v.one("S"))

            def post_qss(n):
                dve.wait_ge(post_a.sem, post_a.at("qsq", n))
                red(qss[:, :], rows(o1), AX_X, ALU.add).then_inc(*post_v.one("qss"))
                dve.wait_ge(post_v.sem, post_v.at("qss", n))
                add_eps(qss[:, :], qss[:, :], DH * EPS, post_v.one("qse"))

            def post_n(n, s):
                dve.wait_ge(post_g.sem, post_g.at("rq", n))
                tt(rows(o2), rows(qhR[s]), wide(rq[:, :]), ALU.mult).then_inc(*post_v.one("n"))

            def post_og(n, s):
                dve.wait_ge(post_g.sem, post_g.at("o", n))
                stt(out=o2[:, :], in0=thR[s][:, :], scalar=1.0, in1=o2[:, :], op0=ALU.add, op1=ALU.mult)\
                    .then_inc(*post_v.one("og"))

            def post_oss(n):
                dve.wait_ge(post_a.sem, post_a.at("osq", n))
                red(oss[:, :], rows(o1), AX_X, ALU.add).then_inc(*post_v.one("oss"))
                dve.wait_ge(post_v.sem, post_v.at("oss", n))
                add_eps(oss[:, :], oss[:, :], 4 * DH * EPS, post_v.one("ose"))

            def post_on(n):
                dve.wait_ge(post_g.sem, post_g.at("ro", n))
                tt(rows(o2), rows(o2), wide(ro[:, :]), ALU.mult).then_inc(*post_v.one("on"))

            def post_ogT(n):
                dve.wait_ge(post_v.sem, post_v.at("on", n))
                nc.vector.transpose(feat(ogT), rows(o2)).then_inc(*post_v.one("ogT"))

            def tail_stats(n):
                dve.wait_ge(tail_t.sem, tail_t.at("wo", n))
                norm_stats(PA[1][:, :], "a", tail_v, ("as", "aa", "anm", "ave"), n)

            def tail_x1(n, s):
                dve.wait_ge(tail_a.sem, tail_a.at("xc", n))
                stt(out=x1[s][:, :], in0=PA[1][:, :], scalar=rs["a"][:, 0:1], in1=x1[s][:, :], op0=ALU.mult, op1=ALU.add)\
                    .then_inc(*tail_v.one("x1"))
                dve.wait_ge(tail_v.sem, tail_v.at("x1", n))
                norm_stats(x1[s][:, :], "f", tail_v, ("fs", "fa", "fnm", "fve"), n)

            def pair_xl(p):
                dve.wait_ge(pair_a.sem, pair_a.at("xh", p))
                for k, b in enumerate((G, U4)):
                    v = [a[:, :].rearrange("p (k n) -> p k n", k=KD)[:, :, k * P:(k + 1) * P] for a in (xl, xh)]
                    ins = tt(v[0], b[:, :].rearrange("p (k n) -> p k n", k=KD), v[1].bitcast(F32), ALU.subtract)
                ins.then_inc(*pair_v.one("xl"))

            def ffn_f(p, r):
                c = NR * p + r
                dve.wait_ge(ffn_a.sem, ffn_a.at("silu", c))
                dve.wait_ge(ffn_t.sem, ffn_t.at("u", c))
                for q in range(RM):
                    e = slice(q * PAIR, (q + 1) * PAIR)
                    ins = stt(out=f[:, e], in0=U4[:, e], scalar=us[:, RM * r + q:RM * r + q + 1], in1=f[:, e],
                              op0=ALU.mult, op1=ALU.mult)
                ins.then_inc(*ffn_v.one("f"))

            def ffn_fl(p, r):
                dve.wait_ge(ffn_a.sem, ffn_a.at("fh", NR * p + r))
                tt(fl[:, :], f[:, :], fh[:, :].bitcast(F32), ALU.subtract).then_inc(*low_v.one("fl"))

            def fin_y(n, k, p):
                dve.wait_ge(down_t.sem, down_t.at("dn", NR * p + NR - 1))
                if begun(n - 1):
                    dve.wait_ge(fin_v.sem, fin_v.at("out", n - 1))
                tt(yb[:, :], Y[k][:, :], ds[:, :], ALU.mult).then_inc(*fin_v.one("y"))

            def fin_stats(n):
                dve.wait_ge(fin_v.sem, fin_v.at("y", n))
                norm_stats(yb[:, :], "y", fin_v, ("ys", "ya", "ynm", "yve"), n)

            def fin_out(n, k):
                dve.wait_ge(fin_a.sem, fin_a.at("yc", n))
                stt(out=x1h[k][:, :], in0=yb[:, :], scalar=rs["y"][:, 0:1], in1=x1h[k][:, :], op0=ALU.mult, op1=ALU.add)\
                    .then_inc(*fin_v.one("out"))

            def magic(u):
                dve.wait_ge(s_stage[u % 3], 16 * (u // 3 + 1))
                if u >= 2:
                    dve.wait_ge(s_quant, u - 1)
                m = wmg[u % 2]
                ts(m[:, :].bitcast(I32), wst[u % 3][:, :].bitcast(I32), 0x7F800000, 0x00400000,
                   ALU.bitwise_and, ALU.bitwise_or).then_inc(s_mask, 1)
                dve.wait_ge(s_mask, u + 3)
                ts(m[:, :], m[:, :], 1.5 * 2.0 ** -6, 2.0 ** 20, ALU.max, ALU.mult).then_inc(s_magic, 1)

            def quantize(u):
                dve.wait_ge(s_shift, u + 1)
                tt((GW, UW, DW)[u % 3][:, u // 3 * D:(u // 3 + 1) * D], wst[u % 3][:, :], wmg[u % 2][:, :], ALU.subtract)\
                    .then_inc(s_quant, 1)

            def body(t, s, h):
                norm, prep, scan, post, tail = live(t)
                o = 1 - s
                fin = s and is_pair(h - 2)
                ffn = rounds(t, s, h)
                for j in range(NC):
                    if scan:
                        scan_front(t, j, s)
                        scan_back(t, j, s)
                    if j == 0 and post:
                        post_qss(t - 1)
                    if j == 1 and 0 in ffn:
                        ffn_fl(*ffn[0])
                    if j == 2 and fin:
                        fin_y(2 * (h - 2), 0, h - 2)
                    if j == 3 and 1 in ffn:
                        ffn_f(*ffn[1])
                    if j == 4 and prep:
                        prep_kn(t + 1)
                    if j == 5 and prep:
                        prep_kR(t + 1, o)
                    if j == 6:
                        if post:
                            post_on(t - 1)
                            post_ogT(t - 1)
                    if j == 7:
                        if prep:
                            prep_rR(t + 1, o)
                            prep_thR(t + 1, o)
                    if scan:
                        scan_state(t, j)
                    if j == 0:
                        if tail:
                            tail_x1(t - 2, s)
                        if 0 in ffn:
                            ffn_f(*ffn[0])
                    if j == 1 and post:
                        post_n(t - 1, o)
                    if j == 2:
                        if s and is_pair(h - 1):
                            pair_xl(h - 1)
                        if fin:
                            fin_stats(2 * (h - 2))
                        if prep:
                            prep_kss(t + 1)
                    if j == 3:
                        if prep:
                            prep_qR(t + 1, o)
                        if fin:
                            fin_out(2 * (h - 2), 0)
                            fin_y(2 * (h - 2) + 1, 1, h - 2)
                        if post:
                            post_og(t - 1, o)
                    if j == 4:
                        if prep:
                            prep_d(t + 1)
                        if post:
                            post_oss(t - 1)
                    if j == 5:
                        if fin:
                            fin_stats(2 * (h - 2) + 1)
                        if norm:
                            x_stats(t + 2)
                    if j == 6:
                        if prep:
                            prep_bx(t + 1)
                        if 2 in ffn:
                            ffn_f(*ffn[2])
                        if fin:
                            fin_out(2 * (h - 2) + 1, 1)
                    if j == 7:
                        if prep:
                            prep_eta(t + 1, o)
                        if post:
                            tail_stats(t - 1)
                    for u in last_units(t, j):
                        quantize(u)
                    for u in units(t, j):
                        magic(u)

            def prologue():
                nc.vector.memset(S, 0.0).then_inc(s_mask, 1)
                nc.vector.memset(g2(ysq[:, :], 33)[:, :, DH:DH + 1], DH * EPS).then_inc(s_mask, 1)
                x_stats(0)
                dve.wait_ge(s_small, 16 * 11)
                tt(wbF[:, :], wF[:, :], bF[:, :], ALU.mult).then_inc(s_setup, 1)
                ts(wK[:, :], wR[:, :], KAPPA, None, ALU.mult).then_inc(s_setup, 1)
                stt(out=w2K[:, :], in0=wR[:, :], scalar=KAPPA, in1=wR[:, :], op0=ALU.mult, op1=ALU.mult)\
                    .then_inc(s_setup, 1)
                x_stats(1)
                prep_kss(0)
                prep_qR(0, 0)
                prep_kn(0)
                prep_d(0)
                prep_kR(0, 0)
                prep_bx(0)
                prep_rR(0, 0)
                prep_thR(0, 0)
                prep_eta(0, 0)
                dve.wait_ge(s_wo, 16)
                for g in range(KD):
                    e = slice(g * D, (g + 1) * D)
                    ins = ts(Wo[:, e], Wo[:, e], nw[:, g:g + 1], KAPPA, ALU.mult, ALU.mult)
                ins.then_inc(s_setup, 1)
                dve.wait_ge(s_setup, 4)
                dve.wait_ge(s_mask, 2)

            timeline(body, prologue, dve)


def _consts():
    tok = np.arange(P)
    c, gp, h4 = tok % CH, tok // 64, tok // CH % 4
    table = np.zeros((P, NCONST), np.float32)
    table[:, C_ID:C_ID + P] = np.eye(P)
    table[:, C_REP:C_REP + P] = (tok[:, None] % CH) == c[None, :]
    table[:, C_TRI:C_TRI + 64] = (h4[:, None] == h4[None, :64]) & (c[:, None] <= c[None, :64])
    table[:, C_CHM:C_CHM + 64] = (tok[:, None] // CH) == (np.arange(64)[None, :] // 8)
    col = np.arange(8)
    table[:, C_ROW:C_ROW + 8] = (gp[:, None] == col[None, :] // 4) & (h4[:, None] == col[None, :] % 4)
    table[:, C_ROW:C_ROW + 8] *= KAPPA
    table[:, C_GPM:C_GPM + 2] = gp[:, None] == np.arange(2)[None, :]
    table[:, C_HM:C_HM + 4] = h4[:, None] == np.array([0, 2, 1, 3])[None, :]
    table[:, C_NH:C_NH + 16] = -0.5
    table[:, C_ONE:C_ONE + 16] = 1.0
    table[:, C_CEN:C_CEN + P] = np.eye(P) - (tok[:, None] // DH == tok[None, :] // DH) / DH
    return table


def _by_row(a):
    a = a.reshape(2, 2, 4, DH).transpose(0, 2, 1, 3)[:, :, None]
    return np.broadcast_to(a, (2, 4, CH, 2, DH)).reshape(P, 2 * DH)


def _by_feature(a):
    a = a.reshape((2, 2, 2, 2, DH) + a.shape[1:])
    return a.transpose((3, 1, 0, 2) + tuple(range(4, a.ndim))).reshape((4, P) + a.shape[5:])


def kernel(L0_attn_x, L0_attn_Wq, L0_attn_Wk, L0_attn_Wv, L0_attn_Wo, L0_attn_Wbeta, L0_attn_ln_w, L0_attn_ln_b,
           L0_attn_Wg1, L0_attn_Wg2, L0_attn_norm_w, L0_ffn_gate_w, L0_ffn_up_w, L0_ffn_down_w,
           L0_ffn_gate_scale, L0_ffn_up_scale, L0_ffn_down_scale):
    import concourse.bacc as _bacc
    from concourse.bass_utils import run_bass_kernel_spmd as _run

    def blocks(a, n):
        return a.reshape(-1, P, n).transpose(1, 0, 2).reshape(P, -1)

    def columns(a):
        return _by_feature(a.T).reshape(D, -1).T

    A = {k: np.asarray(v) for k, v in locals().items() if k.startswith("L0_")}
    ins = {
        "x": A["L0_attn_x"].reshape(T, D), "wq": columns(A["L0_attn_Wq"]),
        "wk": columns(A["L0_attn_Wk"]), "wv": columns(A["L0_attn_Wv"]),
        "wo": _by_feature(A["L0_attn_Wo"]).reshape(D, D), "wbeta": A["L0_attn_Wbeta"], "wg1": A["L0_attn_Wg1"], "wg2": columns(A["L0_attn_Wg2"]),
        "norm_w": _by_feature(A["L0_attn_norm_w"]).T, "ln_w": _by_row(A["L0_attn_ln_w"]),
        "ln_b": _by_row(A["L0_attn_ln_b"]), "gate_w": blocks(A["L0_ffn_gate_w"], I),
        "up_w": blocks(A["L0_ffn_up_w"], I), "down_w": blocks(A["L0_ffn_down_w"], D),
        "gate_s": A["L0_ffn_gate_scale"].reshape(MI, P).T, "up_s": A["L0_ffn_up_scale"].reshape(MI, P).T,
        "down_s": A["L0_ffn_down_scale"], "ln_wf": _by_feature(A["L0_attn_ln_w"].reshape(-1)).T,
        "ln_bf": _by_feature(A["L0_attn_ln_b"].reshape(-1)).T, "consts": _consts(),
    }
    nc = _bacc.Bacc("TRN2", target_bir_lowering=False, num_devices=1)
    arrays, args = {}, {}
    for name, a in ins.items():
        a = np.ascontiguousarray(a)
        arrays[f"in_{name}"] = a
        args[name] = nc.dram_tensor(f"in_{name}", a.shape, mybir.dt.from_np(a.dtype), kind="ExternalInput").ap()
    args["out"] = nc.dram_tensor("out_0", (T, D), F32, kind="ExternalOutput").ap()
    build(nc, **args)
    r = _run(nc, [arrays], core_ids=[0])
    return r.results[0]["out_0"].reshape(1, T, D)
```
